# Optimizing a Trainium2 kernel written in Bass

```python
import numpy as np
import jax
import jax.numpy as jnp

def _softmax(x, axis=-1):
    return jax.nn.softmax(x, axis=axis)

def _gelu(x):
    return jax.nn.gelu(x, approximate=True)

def _silu(x):
    return jax.nn.silu(x)

def _sigmoid(x):
    return jax.nn.sigmoid(x)

def _layernorm(x, axis=-1, eps=1e-05):
    m = jnp.mean(x, axis=axis, keepdims=True)
    v = jnp.var(x, axis=axis, keepdims=True)
    return (x - m) / jnp.sqrt(v + eps)

def _scatter_add(tgt, idx, src, axis=0):
    return tgt.at[idx].add(src)

def _segment_sum(src, seg, n):
    return jax.ops.segment_sum(src, seg, n)
kernel_name = 'mk_early_fusion_embed_d1_tok_img256_r4_2f1540'

def setup_inputs(seed: int=0):
    np.random.seed(seed)
    _w = jnp.asarray

    def _rec_inputs():
        import jax
        import jax.numpy as jnp
        _rk = jax.random.key(seed)
        x = -0.000202321 + 1.00025 * jax.random.normal(jax.random.fold_in(_rk, 1), (16, 64, 56, 56), jnp.float32)
        x_txt = jax.random.randint(jax.random.fold_in(_rk, 51), (16, 77), 0, 16, jnp.int32)
        pos_S = jnp.broadcast_to(jnp.arange(77, dtype=jnp.int32), (77,))
        return (x, x_txt, pos_S)
    x, x_txt, pos_S = _rec_inputs()

    def _L0_tok_setup():
        import jax, jax.numpy as jnp
        import numpy as np
        B, C, H, W = (8, 64, 56, 56)
        K = 3

        def _unfold3x3(x):
            b, c, h, w = x.shape
            xp = jnp.pad(x, ((0, 0), (0, 0), (1, 1), (1, 1)))
            patches = jnp.stack([xp[:, :, i:i + h, j:j + w] for i in range(K) for j in range(K)], axis=2)
            return patches.reshape(b, c * K * K, h * w).transpose(0, 2, 1)
        key = jax.random.key(seed)
        ks = jax.random.split(key, 8)
        d = C * K * K
        s1 = 1.0 / np.sqrt(d)
        s2 = 1.0 / np.sqrt(C)
        return {'x': jax.random.normal(ks[0], (B, C, H, W), jnp.float32), 'W1': jax.random.uniform(ks[1], (d, C), jnp.float32, -s1, s1), 'b1': jax.random.uniform(ks[2], (C,), jnp.float32, -s1, s1), 'W2': jax.random.uniform(ks[3], (C, d), jnp.float32, -s2, s2), 'b2': jax.random.uniform(ks[4], (d,), jnp.float32, -s2, s2), 'W3': jax.random.uniform(ks[5], (d, C), jnp.float32, -s1, s1), 'b3': jax.random.uniform(ks[6], (C,), jnp.float32, -s1, s1)}
    _L0_tok_all = _L0_tok_setup()
    _L0_tok_in = {k: v for k, v in _L0_tok_all.items() if k in ('W1', 'b1', 'W2', 'b2', 'W3', 'b3')}
    del _L0_tok_all

    def _L0_txt_setup():
        import jax, jax.numpy as jnp
        import numpy as np
        import math
        EMB_DIM = 64
        HEADS = 8
        HEAD_DIM = EMB_DIM // HEADS
        N_LAYERS = 6
        GRID_H = 32
        GRID_W = 32
        SEQ = GRID_H * GRID_W
        LN_EPS = 1e-05

        def _layernorm(x, w, b):
            mu = jnp.mean(x, axis=-1, keepdims=True)
            var = jnp.mean(jnp.square(x - mu), axis=-1, keepdims=True)
            return (x - mu) * jax.lax.rsqrt(var + LN_EPS) * w + b

        def _sinusoidal_table(num_pos, dim):
            inv_freq = 1.0 / 10000.0 ** (jnp.arange(0, dim, 2, dtype=jnp.float32) / dim)
            t = jnp.arange(num_pos, dtype=jnp.float32)
            sinusoid = t[:, None] * inv_freq[None, :]
            return jnp.concatenate([jnp.sin(sinusoid), jnp.cos(sinusoid)], axis=-1)

        def _alibi_bias(num_heads, seq_len):
            xs, ys = jnp.meshgrid(jnp.arange(GRID_H), jnp.arange(GRID_W), indexing='ij')
            xf = xs.reshape(-1).astype(jnp.float32)
            yf = ys.reshape(-1).astype(jnp.float32)
            dist = jnp.abs(xf[:, None] - xf[None, :]) + jnp.abs(yf[:, None] - yf[None, :])
            dist = jnp.abs(dist[:seq_len, :seq_len])
            i = jnp.arange(num_heads, dtype=jnp.float32)
            slopes_l = -2.0 ** (-(1.0 + i))
            slopes_r = -2.0 ** (-(0.5 + i))
            alibi_l = slopes_l[:, None, None] * dist[None]
            alibi_r = slopes_r[:, None, None] * dist[None]
            return jnp.triu(alibi_r) + jnp.tril(alibi_l)
        key = jax.random.key(seed)
        ks = jax.random.split(key, 8)
        B, S, D, L = (16, SEQ, EMB_DIM, N_LAYERS)
        H2 = 2 * 128
        return {'tokens': jax.random.randint(ks[0], (B, S), 0, 16), 'pos_ids': jnp.arange(S), 'emb_table': jax.random.normal(ks[1], (16, D), dtype=jnp.float32), 'input_weight': jnp.ones((1,), jnp.float32), 'position_weight': jnp.ones((1,), jnp.float32), 'ln1_w': jnp.ones((L, D), jnp.float32), 'ln1_b': jnp.zeros((L, D), jnp.float32), 'ln2_w': jnp.ones((L, D), jnp.float32), 'ln2_b': jnp.zeros((L, D), jnp.float32), 'w1': jax.random.normal(ks[2], (L, D, H2), dtype=jnp.float32) * (1.0 / np.sqrt(D)), 'b1': jnp.zeros((L, H2), jnp.float32), 'w2': jax.random.normal(ks[3], (L, H2, D), dtype=jnp.float32) * (1.0 / np.sqrt(H2)), 'b2': jnp.zeros((L, D), jnp.float32), 'lnf_w': jnp.ones((D,), jnp.float32), 'lnf_b': jnp.zeros((D,), jnp.float32)}
    _L0_txt_all = _L0_txt_setup()
    _L0_txt_in = {k: v for k, v in _L0_txt_all.items() if k in ('emb_table', 'input_weight', 'position_weight', 'ln1_w', 'ln1_b', 'ln2_w', 'ln2_b', 'w1', 'b1', 'w2', 'b2', 'lnf_w', 'lnf_b')}
    del _L0_txt_all

    def _L0_attn_setup():
        import jax, jax.numpy as jnp
        import numpy as np
        DIM = 64
        HEADS = 4
        DIM_HEAD = 32
        NUM_MEM = 4
        HIDDEN = HEADS * DIM_HEAD
        SCALE = DIM_HEAD ** (-0.5)

        def rmsnorm(x, g):
            n = jnp.linalg.norm(x, axis=-1, keepdims=True)
            return x / jnp.maximum(n, 1e-12) * g * x.shape[-1] ** 0.5
        key = jax.random.key(seed)
        ks = jax.random.split(key, 8)
        B, N = (4, 4096)
        return {'x': jax.random.normal(ks[0], (B, N, DIM), jnp.float32), 't': jax.random.normal(ks[1], (B,), jnp.float32), 'w_qkv': jax.random.normal(ks[2], (DIM, 3 * HIDDEN), jnp.float32) * 0.02, 'mem_kv': jax.random.normal(ks[3], (2, HEADS, DIM_HEAD, NUM_MEM), jnp.float32), 'w_out': jax.random.normal(ks[4], (HIDDEN, DIM), jnp.float32) * 0.02, 'b_out': jnp.zeros((DIM,), jnp.float32), 'g_out': jnp.ones((DIM,), jnp.float32), 'g_pre': jnp.ones((DIM,), jnp.float32)}
    _L0_attn_all = _L0_attn_setup()
    _L0_attn_in = {k: v for k, v in _L0_attn_all.items() if k in ('t', 'w_qkv', 'mem_kv', 'w_out', 'b_out', 'g_out', 'g_pre')}
    del _L0_attn_all

    def _L0_ffn_setup():
        import math
        import jax, jax.numpy as jnp
        import numpy as np
        CAPACITY_FACTOR = 1.25
        key = jax.random.key(seed)
        ks = jax.random.split(key, 5)
        B, L, D, F, E = (8, 2048, 64, 256, 8)
        h = jax.random.normal(ks[0], (B, L, D), dtype=jnp.float32)
        gate_w = jax.random.normal(ks[1], (D, E), dtype=jnp.float32) * 0.02
        gate_b = jnp.zeros((E,), dtype=jnp.float32)
        w1 = jax.random.normal(ks[2], (E, D, F), dtype=jnp.float32) * (1.0 / math.sqrt(D))
        b1 = jnp.zeros((E, F), dtype=jnp.float32)
        w2 = jax.random.normal(ks[3], (E, F, D), dtype=jnp.float32) * (1.0 / math.sqrt(F))
        b2 = jnp.zeros((E, D), dtype=jnp.float32)
        return {'h': h, 'gate_w': gate_w, 'gate_b': gate_b, 'w1': w1, 'b1': b1, 'w2': w2, 'b2': b2}
    _L0_ffn_all = _L0_ffn_setup()
    _L0_ffn_in = {k: v for k, v in _L0_ffn_all.items() if k in ('gate_w', 'gate_b', 'w1', 'b1', 'w2', 'b2')}
    del _L0_ffn_all
    return {'x': x, 'x_txt': x_txt, 'pos_S': pos_S, 'L0_tok_W1': _L0_tok_in['W1'], 'L0_tok_b1': _L0_tok_in['b1'], 'L0_tok_W2': _L0_tok_in['W2'], 'L0_tok_b2': _L0_tok_in['b2'], 'L0_tok_W3': _L0_tok_in['W3'], 'L0_tok_b3': _L0_tok_in['b3'], 'L0_txt_emb_table': _L0_txt_in['emb_table'], 'L0_txt_input_weight': _L0_txt_in['input_weight'], 'L0_txt_position_weight': _L0_txt_in['position_weight'], 'L0_txt_ln1_w': _L0_txt_in['ln1_w'], 'L0_txt_ln1_b': _L0_txt_in['ln1_b'], 'L0_txt_ln2_w': _L0_txt_in['ln2_w'], 'L0_txt_ln2_b': _L0_txt_in['ln2_b'], 'L0_txt_w1': _L0_txt_in['w1'], 'L0_txt_b1': _L0_txt_in['b1'], 'L0_txt_w2': _L0_txt_in['w2'], 'L0_txt_b2': _L0_txt_in['b2'], 'L0_txt_lnf_w': _L0_txt_in['lnf_w'], 'L0_txt_lnf_b': _L0_txt_in['lnf_b'], 'L0_attn_t': _L0_attn_in['t'], 'L0_attn_w_qkv': _L0_attn_in['w_qkv'], 'L0_attn_mem_kv': _L0_attn_in['mem_kv'], 'L0_attn_w_out': _L0_attn_in['w_out'], 'L0_attn_b_out': _L0_attn_in['b_out'], 'L0_attn_g_out': _L0_attn_in['g_out'], 'L0_attn_g_pre': _L0_attn_in['g_pre'], 'L0_ffn_gate_w': _L0_ffn_in['gate_w'], 'L0_ffn_gate_b': _L0_ffn_in['gate_b'], 'L0_ffn_w1': _L0_ffn_in['w1'], 'L0_ffn_b1': _L0_ffn_in['b1'], 'L0_ffn_w2': _L0_ffn_in['w2'], 'L0_ffn_b2': _L0_ffn_in['b2']}

def reference(x, x_txt, pos_S, L0_tok_W1, L0_tok_b1, L0_tok_W2, L0_tok_b2, L0_tok_W3, L0_tok_b3, L0_txt_emb_table, L0_txt_input_weight, L0_txt_position_weight, L0_txt_ln1_w, L0_txt_ln1_b, L0_txt_ln2_w, L0_txt_ln2_b, L0_txt_w1, L0_txt_b1, L0_txt_w2, L0_txt_b2, L0_txt_lnf_w, L0_txt_lnf_b, L0_attn_t, L0_attn_w_qkv, L0_attn_mem_kv, L0_attn_w_out, L0_attn_b_out, L0_attn_g_out, L0_attn_g_pre, L0_ffn_gate_w, L0_ffn_gate_b, L0_ffn_w1, L0_ffn_b1, L0_ffn_w2, L0_ffn_b2):
    import jax
    import jax.numpy as jnp

    def _L0_tok_ref(x, W1, b1, W2, b2, W3, b3):
        import jax, jax.numpy as jnp
        import numpy as np
        B, C, H, W = (8, 64, 56, 56)
        K = 3

        def _unfold3x3(x):
            b, c, h, w = x.shape
            xp = jnp.pad(x, ((0, 0), (0, 0), (1, 1), (1, 1)))
            patches = jnp.stack([xp[:, :, i:i + h, j:j + w] for i in range(K) for j in range(K)], axis=2)
            return patches.reshape(b, c * K * K, h * w).transpose(0, 2, 1)
        t = _unfold3x3(x)
        h1 = jax.nn.relu(jnp.einsum('bld,dc->blc', t, W1) + b1)
        s = jax.nn.sigmoid(jnp.einsum('blc,cd->bld', h1, W2) + b2)
        out = jnp.einsum('bld,dc->blc', t * s, W3) + b3
        return out

    def _L0_txt_ref(tokens, pos_ids, emb_table, input_weight, position_weight, ln1_w, ln1_b, ln2_w, ln2_b, w1, b1, w2, b2, lnf_w, lnf_b):
        import jax, jax.numpy as jnp
        import numpy as np
        import math
        EMB_DIM = 64
        HEADS = 8
        HEAD_DIM = EMB_DIM // HEADS
        N_LAYERS = 6
        GRID_H = 32
        GRID_W = 32
        SEQ = GRID_H * GRID_W
        LN_EPS = 1e-05

        def _layernorm(x, w, b):
            mu = jnp.mean(x, axis=-1, keepdims=True)
            var = jnp.mean(jnp.square(x - mu), axis=-1, keepdims=True)
            return (x - mu) * jax.lax.rsqrt(var + LN_EPS) * w + b

        def _sinusoidal_table(num_pos, dim):
            inv_freq = 1.0 / 10000.0 ** (jnp.arange(0, dim, 2, dtype=jnp.float32) / dim)
            t = jnp.arange(num_pos, dtype=jnp.float32)
            sinusoid = t[:, None] * inv_freq[None, :]
            return jnp.concatenate([jnp.sin(sinusoid), jnp.cos(sinusoid)], axis=-1)

        def _alibi_bias(num_heads, seq_len):
            xs, ys = jnp.meshgrid(jnp.arange(GRID_H), jnp.arange(GRID_W), indexing='ij')
            xf = xs.reshape(-1).astype(jnp.float32)
            yf = ys.reshape(-1).astype(jnp.float32)
            dist = jnp.abs(xf[:, None] - xf[None, :]) + jnp.abs(yf[:, None] - yf[None, :])
            dist = jnp.abs(dist[:seq_len, :seq_len])
            i = jnp.arange(num_heads, dtype=jnp.float32)
            slopes_l = -2.0 ** (-(1.0 + i))
            slopes_r = -2.0 ** (-(0.5 + i))
            alibi_l = slopes_l[:, None, None] * dist[None]
            alibi_r = slopes_r[:, None, None] * dist[None]
            return jnp.triu(alibi_r) + jnp.tril(alibi_l)
        B, S = tokens.shape
        x_emb = emb_table[tokens]
        pos_emb = _sinusoidal_table(SEQ, EMB_DIM)[pos_ids][None]
        x = input_weight * x_emb + position_weight * pos_emb
        bias = _alibi_bias(HEADS, S)[None]
        scale = 1.0 / math.sqrt(HEAD_DIM)
        for l in range(N_LAYERS):
            xn = _layernorm(x, ln1_w[l], ln1_b[l])
            qkv = xn.reshape(B, S, HEADS, HEAD_DIM).transpose(0, 2, 1, 3)
            scores = jnp.einsum('bhsd,bhtd->bhst', qkv, qkv) * scale + bias
            attn = jax.nn.softmax(scores, axis=-1)
            out = jnp.einsum('bhst,bhtd->bhsd', attn, qkv)
            out = out.transpose(0, 2, 1, 3).reshape(B, S, EMB_DIM)
            x = x + out
            xn = _layernorm(x, ln2_w[l], ln2_b[l])
            h = jax.nn.gelu(xn @ w1[l] + b1[l], approximate=False)
            x = x + (h @ w2[l] + b2[l])
        return _layernorm(x, lnf_w, lnf_b)

    def _L0_attn_ref(x, t, w_qkv, mem_kv, w_out, b_out, g_out, g_pre):
        import jax, jax.numpy as jnp
        import numpy as np
        DIM = 64
        HEADS = 4
        DIM_HEAD = 32
        NUM_MEM = 4
        HIDDEN = HEADS * DIM_HEAD
        SCALE = DIM_HEAD ** (-0.5)

        def rmsnorm(x, g):
            n = jnp.linalg.norm(x, axis=-1, keepdims=True)
            return x / jnp.maximum(n, 1e-12) * g * x.shape[-1] ** 0.5
        b, n, c = x.shape
        xn = rmsnorm(x, g_pre)
        qkv = xn @ w_qkv
        q, k, v = jnp.split(qkv, 3, axis=-1)

        def to_heads(z):
            return z.reshape(b, n, HEADS, DIM_HEAD).transpose(0, 2, 3, 1)
        q, k, v = map(to_heads, (q, k, v))
        mk = jnp.broadcast_to(mem_kv[0], (b, HEADS, DIM_HEAD, NUM_MEM))
        mv = jnp.broadcast_to(mem_kv[1], (b, HEADS, DIM_HEAD, NUM_MEM))
        k = jnp.concatenate([mk, k], axis=-1)
        v = jnp.concatenate([mv, v], axis=-1)
        q = jax.nn.softmax(q, axis=-2) * SCALE
        k = jax.nn.softmax(k, axis=-1)
        context = jnp.einsum('bhdn,bhen->bhde', k, v)
        out = jnp.einsum('bhde,bhdn->bhen', context, q)
        out = out.transpose(0, 3, 1, 2).reshape(b, n, HIDDEN)
        out = rmsnorm(out @ w_out + b_out, g_out)
        return out + x

    def _L0_ffn_ref(h, gate_w, gate_b, w1, b1, w2, b2):
        import math
        import jax, jax.numpy as jnp
        import numpy as np
        CAPACITY_FACTOR = 1.25
        B, L, D = h.shape
        E = gate_w.shape[1]
        T = B * L
        C = max(1, math.ceil(CAPACITY_FACTOR * T / E))
        x = h.reshape(T, D)
        logits = x @ gate_w + gate_b
        probs = jax.nn.softmax(logits, axis=-1)
        idx = jnp.argmax(probs, axis=-1)
        prb = jnp.take_along_axis(probs, idx[:, None], axis=1)[:, 0]
        one_hot = jax.nn.one_hot(idx, E, dtype=jnp.float32)
        pos = (jnp.cumsum(one_hot, axis=0) * one_hot).sum(-1).astype(jnp.int32) - 1
        kept = pos < C
        pos_safe = jnp.where(kept, pos, C)
        buf = jnp.zeros((E, C, D), dtype=h.dtype).at[idx, pos_safe].set(x, mode='drop')
        hmid = jax.nn.relu(jnp.einsum('ecd,edf->ecf', buf, w1) + b1[:, None, :])
        ybuf = jnp.einsum('ecf,efd->ecd', hmid, w2) + b2[:, None, :]
        pos_g = jnp.minimum(pos, C - 1)
        y_tok = ybuf[idx, pos_g] * (prb * kept)[:, None]
        y = y_tok.reshape(B, L, D)
        y = jnp.nan_to_num(y, nan=0.0, posinf=10000.0, neginf=-10000.0)
        return y
    h = _L0_tok_ref(x, L0_tok_W1, L0_tok_b1, L0_tok_W2, L0_tok_b2, L0_tok_W3, L0_tok_b3)
    h = jnp.concatenate([h, _L0_txt_ref(x_txt, pos_S, L0_txt_emb_table, L0_txt_input_weight, L0_txt_position_weight, L0_txt_ln1_w, L0_txt_ln1_b, L0_txt_ln2_w, L0_txt_ln2_b, L0_txt_w1, L0_txt_b1, L0_txt_w2, L0_txt_b2, L0_txt_lnf_w, L0_txt_lnf_b)], axis=1)
    h = h + _L0_attn_ref(_layernorm(h, axis=-1), L0_attn_t, L0_attn_w_qkv, L0_attn_mem_kv, L0_attn_w_out, L0_attn_b_out, L0_attn_g_out, L0_attn_g_pre)
    h = h + _L0_ffn_ref(_layernorm(h, axis=-1), L0_ffn_gate_w, L0_ffn_gate_b, L0_ffn_w1, L0_ffn_b1, L0_ffn_w2, L0_ffn_b2)
    return h

_drawn_inputs = setup_inputs


def setup_inputs(seed=0):
    import zlib

    import numpy as np

    out = dict(_drawn_inputs(seed))
    spreads = {'L0_txt_ln1_w': (1.0, 0.2),
     'L0_txt_ln1_b': (0.0, 0.365),
     'L0_txt_ln2_w': (1.0, 0.6),
     'L0_txt_ln2_b': (0.0, 0.781),
     'L0_txt_b1': (0.0, 0.694),
     'L0_txt_b2': (0.0, 0.438),
     'L0_txt_lnf_w': (1.0, 0.2),
     'L0_txt_lnf_b': (0.0, 0.357),
     'L0_attn_b_out': (0.0, 0.1),
     'L0_attn_g_out': (1.0, 0.2),
     'L0_attn_g_pre': (1.0, 0.6),
     'L0_ffn_gate_b': (0.0, 0.1),
     'L0_ffn_b1': (0.0, 0.8),
     'L0_ffn_b2': (0.0, 0.8)}
    factors = {'L0_tok_b1': 8.0, 'L0_attn_w_qkv': 8.0, 'L0_attn_mem_kv': 8.0, 'L0_attn_w_out': 8.0}
    for name, (base, spread) in spreads.items():
        noise = np.random.default_rng([zlib.crc32(name.encode()), seed]).standard_normal(out[name].shape)
        drawn = base * np.exp(spread * noise) if base else spread * noise
        out[name] = jnp.asarray(drawn.astype(out[name].dtype))
    for name, factor in factors.items():
        out[name] = (out[name] * factor).astype(out[name].dtype)
    return out
```

```python
from contextlib import ExitStack

import concourse.bass as bass
from concourse import mybir

F32 = mybir.dt.float32
I32 = mybir.dt.int32
ALU = mybir.AluOpType
ACT = mybir.ActivationFunctionType
AX = mybir.AxisListType.X

P = 128
C = 64
NB = 16
HW = 56
PW = HW + 2
IMG = HW * HW
SEQ = 77
N = IMG + SEQ
TOK = NB * N
XROW = PW * PW + 4
ROWS = 8
TT = ROWS * HW
HALF = TT // 2
GROUPS = HW // ROWS
NCH = 5
TP = TT // 4
LAYERS = 6
HEADS, HD = 8, 8
HALFS = HEADS // 2 * SEQ
FF = 256
TABLE = 1024
LN_EPS = 1e-5
PER_LAYER = NB + 2

CH = 27
CP = N // CH
AH, AD, MEM = 4, 32, 4
HID = AH * AD
KW = N // 7
E = 8
CAP = -(-(5 * TOK) // (4 * E))
ST = 504
SP_ = 126
TILES_E = -(-CAP // ST)
STRIDE = TILES_E * ST
SLOTS = E * STRIDE
RW = C + 4
FAR = 1 << 20
FMAX = 3.4028234663852886e38

assert CH * CP == N and 7 * KW == N


def early_fusion(nc, x_pad, x_txt, pos_ids, tw1, tb1, tw2, tb2, tw3, tb3, emb, iw, pw, ln1w, ln1b, ln2w, ln2b,
                 fw1, fb1, fw2, fb2, wqkv, memk, memv, wout, bout, gout, gpre, gate, ew1, eb1, ew2, eb2,
                 ident_d, table_d, bias_d, hmask_d, bd_d, tri_d, keep_d, desc_d, vocab_d, tokn_d, out):
    h_d = nc.dram_tensor("h_scratch", (TOK, C), F32, kind="Internal").ap()
    slots_d = nc.dram_tensor("slots_scratch", (SLOTS, RW), F32, kind="Internal").ap()
    h_f = h_d.rearrange("t c -> (t c)")
    out_f = out.rearrange("b n c -> (b n c)")
    out_rows = out.rearrange("b n c -> (b n) c")
    slots_f = slots_d.rearrange("t c -> (t c)")

    with ExitStack() as ctx:
        def sb(name, shape, dt=F32):
            return ctx.enter_context(nc.sbuf_tensor(name, shape, dt))

        def sem(name):
            return ctx.enter_context(nc.semaphore(name))

        PS = ctx.enter_context(nc.psum_tensor("PS", [P, 8, 512], F32))

        ident = sb("ident", [P, P])
        w1c = sb("w1c", [P, NCH, C])
        w2c = sb("w2c", [P, NCH, P])
        w3c = sb("w3c", [P, NCH, C])
        b1c = sb("b1c", [P, 1])
        b2c = sb("b2c", [P, NCH])
        b3r = sb("b3r", [TP, C])
        bias_t = sb("bias_t", [SEQ, 2, HALFS])
        hmask = sb("hmask", [C, HEADS])
        spare = sb("spare", [P, 16])
        spare2 = sb("spare2", [1, 48])
        halfneg = sb("halfneg", [P, 2 * CH])
        zeros = sb("zeros", [P, 1071])

        XNT = [sb(f"XNT{i}", [C + 1, N]) for i in range(2)]
        XFT = sb("XFT", [C + 1, N])
        WQ = [sb(f"WQ{i}", [C + 1, 3 * HID]) for i in range(2)]
        gpre_s = sb("gpre_s", [C, 1])
        KM = sb("KM", [P, 8])
        memk_s = sb("memk_s", [P, MEM])
        VM = sb("VM", [MEM, HID + 1])
        V = [sb(f"V{i}", [CP, 2, HID + 1]) for i in range(2)]
        BD = sb("BD", [P, P])
        wout_s = sb("wout_s", [P, C])
        bout_s = sb("bout_s", [CP, C])
        gout_s = sb("gout_s", [CP, C])
        gate_s = sb("gate_s", [C + 1, E])
        DESC = sb("DESC", [CP, CH, E])
        KEEP = sb("KEEP", [CP, E * CH])
        CR = sb("CR", [CP, E])
        TRI = sb("TRI", [CP, CP])
        ONES = sb("ONES", [CP, CP])
        TKN = sb("TKN", [CP, CH])
        rs = sb("rs", [SEQ, HEADS])
        V9 = [sb(f"V9_{i}", [SEQ, HEADS, HD + 1]) for i in range(4)]

        mix_scope = ExitStack()
        outer, ctx = ctx, mix_scope
        PA = [sb(f"PA{i}", [P, 10 * PW]) for i in range(2)]
        PB = [sb(f"PB{i}", [P, 8 * PW]) for i in range(2)]
        H1 = sb("H1", [P, HALF])
        S = sb("S", [P, NCH, TT])
        TS = sb("TS", [P, NCH, TT])
        OT = [sb(f"OT{i}", [TP, 4, C]) for i in range(2)]
        XS = sb("XS", [SEQ, NB, C])
        XNt = sb("XNt", [SEQ, NB, C])
        TC_ = sb("TC_", [SEQ, NB, C])
        TSQ = sb("TSQ", [SEQ, NB, C])
        st1 = sb("st1", [SEQ, NB])
        st2 = sb("st2", [SEQ, NB])
        strs = sb("strs", [SEQ, NB])
        lnw = sb("lnw", [SEQ, 4, C])
        fb2r = sb("fb2r", [SEQ, C])
        tw1s = sb("tw1s", [C, FF])
        tw2s = sb("tw2s", [P, 2, C])
        tb1s = sb("tb1s", [P, 2])
        XB = [sb(f"XB{i}", [SEQ, C]) for i in range(4)]
        XT = sb("XT", [C, SEQ])
        KX = sb("KX", [C, HEADS, SEQ])
        SB_ = sb("SB_", [SEQ, 2, HALFS])
        mx = sb("mx", [SEQ, HEADS])
        PR = sb("PR", [SEQ, 2, HALFS])
        PT = sb("PT", [SEQ, 2, HALFS])
        AO = sb("AO", [SEQ, HEADS, HD])
        X2T = sb("X2T", [C, NB * SEQ])
        GH = sb("GH", [P, 2, NB * SEQ])
        toki = sb("toki", [16, NB * SEQ], I32)
        tokf = sb("tokf", [16, NB * SEQ])
        vocab = sb("vocab", [P, 8])
        posi = sb("posi", [P, SEQ], I32)
        posf = sb("posf", [P, SEQ])
        poh = sb("poh", [P, 8, SEQ])
        tabs = sb("tabs", [P, 8, C])
        embs = sb("embs", [16, C])
        iws = sb("iws", [SEQ, 2])
        posw = sb("posw", [SEQ, C])

        mix_scope.close()
        ctx = outer

        X = [sb(f"X{i}", [CP, CH, C]) for i in range(2)]
        XC = sb("XC", [CP, CH, C])
        SQ = sb("SQ", [CP, CH, C])
        XN = sb("XN", [CP, CH, C])
        XIN = [sb(f"XIN{i}", [CP, CH, C]) for i in range(2)]
        Y = sb("Y", [CP, CH, C])
        SQ2 = sb("SQ2", [CP, CH, C])
        XF = sb("XF", [CP, CH, C])
        ROW = [sb(f"ROW{i}", [CP, CH, RW]) for i in range(2)]
        QT = sb("QT", [P, N])
        fs = sb("fs", [CP, 8, CH])
        vv = sb("vv", [CP, 2 * CH])
        rr = sb("rr", [CP, 2 * CH])
        vv2 = sb("vv2", [CP, CH])
        rr2 = sb("rr2", [CP, CH])
        vv3 = sb("vv3", [CP, CH])
        rr3 = sb("rr3", [CP, CH])
        gs = sb("gs", [CP, 6, CH])
        NK = [sb(f"NK{i}", [P, 1]) for i in range(2)]
        EM = sb("EM", [P, MEM])
        EMT = [sb(f"EMT{i}", [MEM, P]) for i in range(2)]
        EK = [sb(f"EK{i}", [CP, 2, HID]) for i in range(2)]
        QS = [sb(f"QS{i}", [CP, 2, HID]) for i in range(2)]
        QE = [sb(f"QE{i}", [CP, 2, HID]) for i in range(2)]
        QN = [sb(f"QN{i}", [CP, 2, HID]) for i in range(2)]
        qm = sb("qm", [CP, 2, AH])
        qsum = sb("qsum", [CP, 2, AH])
        rq = [sb(f"rq{i}", [CP, 2, AH]) for i in range(2)]
        rden = sb("rden", [P, 1])
        CN = sb("CN", [P, P])
        CT = sb("CT", [P, P])
        MM = sb("MM", [P, C])
        D = sb("D", [CP, CH, E])
        EX = sb("EX", [CP, CH, E])
        CAND = sb("CAND", [CP, CH, E])
        OH = sb("OH", [CP, E, CH])
        SC = sb("SC", [CP, E, CH])
        PX = sb("PX", [CP, E, CH])
        RT = sb("RT", [CP, E])
        SLOT = [sb(f"SLOT{i}", [CP, CH], I32) for i in range(2)]

        R = [sb(f"R{i}", [SP_, 4, RW]) for i in range(4)]
        RX = [sb(f"RX{i}", [SP_, 4, C]) for i in range(2)]
        XE = [sb(f"XE{i}", [C, ST]) for i in range(2)]
        HE = [sb(f"HE{i}", [P, 2, ST]) for i in range(2)]
        YE = sb("YE", [SP_, 4, C])
        GE_ = sb("GE_", [SP_, 4, C])
        FM = sb("FM", [SP_, 4, C])
        CE = sb("CE", [SP_, 4, C])
        EQ = sb("EQ", [SP_, 4, C])
        OE = [sb(f"OE{i}", [SP_, 4, C]) for i in range(4)]
        t0 = sb("t0", [SP_, 4])
        t1 = sb("t1", [SP_, 4])
        IDX = [sb(f"IDX{i}", [SP_, 4], I32) for i in range(4)]
        W1E = [sb(f"W1E{i}", [C, FF]) for i in range(2)]
        W2E = [sb(f"W2E{i}", [P, 2, C]) for i in range(2)]
        B1E = [sb(f"B1E{i}", [P, 2]) for i in range(2)]
        B2E = [sb(f"B2E{i}", [SP_, C]) for i in range(2)]

        names = """consts zeroed vinit dinit
            pa_in0 pa_in1 conv_done relu_done gate_mm tanh_done prod_done mix_mm mix_out st0 st1 h_text
            ln_xc ln_sq ln_var ln_pow ln_out lnd v9_done t_done kx_done xt_done sc_done soft_sub exp_done
            ptr_done pt_done pv_done ao_done aod softd ffw x2_tr x2_cp f1_mm gelu_done f2_mm f2_add
            emb_oh emb_mm embd wts xb_done passed_pe passed_dve passed_pool
            x_in0 x_in1 f_xc f_sq f_var f_pow f_xn f_xin fd f_tr f_trc f_km f_kmx f_nk f_nkr f_wrow f_em f_emt f_emc
            q_mm q_ek q_v q_sub q_exp q_rq q_n q_tr q_trc q_gd q_ctx
            p_cn p_ct p_ctc p_m p_mc p_y p_yb p_sq p_ss p_pow p_yn p_yx p_h2 p_c2 p_c2s p_v3 p_pw3 p_xf p_xt p_xtc
            p_lg p_d p_ex p_rt p_tri p_slot pd o_st s_sc0 s_sc1 crd
            e_in0 e_in1 e_in2 e_in3 e_x e_xt e_xc e_h e_ha e_hd e_y e_o ed e_w0 e_w1 e_s0 e_s1 e_s2 e_s3""".split()
        z = {n: sem(n) for n in names}
        block = ctx.enter_context(nc.Block())

        pa_in = [z["pa_in0"], z["pa_in1"]]
        stored = [z["st0"], z["st1"]]
        x_in = [z["x_in0"], z["x_in1"]]
        scat = [z["s_sc0"], z["s_sc1"]]
        e_w = [z["e_w0"], z["e_w1"]]
        e_in = [z[f"e_in{i}"] for i in range(4)]
        e_sc = [z[f"e_s{i}"] for i in range(4)]

        consts = [(ident[:], ident_d), (w1c[:], tw1), (w2c[:], tw2), (w3c[:], tw3), (b1c[:], tb1), (b2c[:], tb2), (b3r[:], tb3),
                  (bias_t[:], bias_d), (hmask[:], hmask_d), (vocab[:], vocab_d), (toki[:], x_txt), (posi[:], pos_ids),
                  (tabs[:], table_d), (embs[:], emb), (iws[:, 0:1], iw), (iws[:, 1:2], pw), (gpre_s[:], gpre),
                  (WQ[0][:], wqkv), (WQ[1][:], wqkv), (memk_s[:], memk), (VM[:], memv), (wout_s[:], wout), (bout_s[:], bout),
                  (gout_s[:], gout), (gate_s[:], gate), (BD[:], bd_d), (TRI[:], tri_d), (KEEP[:], keep_d), (DESC[:], desc_d),
                  (TKN[:], tokn_d), (lnw[:, 2, :], ln1w[0]), (lnw[:, 3, :], ln1b[0])]
        ALL_CONSTS = 16 * len(consts)

        class Chain:

            def __init__(self, eng, s, base):
                self.eng, self.s, self.base, self.n = eng, s, base, 0

            def after(self, ins, own=False):
                self.n += 1
                ins.then_inc(self.s, 1)
                self.eng.wait_ge(self.s, self.base + self.n)
                if own:
                    self.eng.sem_inc(z["passed_dve"], 1)

        LN_STEPS, AO_STEPS, SOFT_STEPS = 5, 2, 2

        def tile_place(l, n):
            return (n, l) if n < NB else (4 + 2 * l + n - NB, GROUPS - 1)

        @block.sync
        def _(sp):
            for dst, src in consts:
                sp.dma_start(dst, src).then_inc(z["consts"], 16)

            def load_tile(par, b, g):
                for half in range(2):
                    rows = slice(C * half, C * half + C)
                    sp.dma_start(PA[par][rows, :], x_pad[b, :, bass.ds(g * (ROWS * PW) + half, 10 * PW)]
                                 ).then_inc(pa_in[par], 16)
                    sp.dma_start(PB[par][rows, :], x_pad[b, :, bass.ds(g * (ROWS * PW) + 2 + half * PW, 8 * PW)]
                                 ).then_inc(pa_in[par], 16)

            def store_tile(i, par, b, g):
                sp.wait_ge(z["mix_out"], i + 1)
                sp.dma_start(h_f[bass.ds(b * (N * C) + g * (TT * C), TT * C)].rearrange("(p f) -> p f", p=TP),
                             OT[par][:, :, :].rearrange("p j c -> p (j c)")).then_inc(stored[par], 16)

            load_tile(0, 0, 0)
            load_tile(1, 1, 0)
            sp.wait_ge(z["zeroed"], 1)
            for k in range(SLOTS * RW // (P * 1071)):
                sp.dma_start(slots_f[k * P * 1071:(k + 1) * P * 1071].rearrange("(p f) -> p f", p=P),
                             zeros[:, :]).then_inc(z["wts"], 16)
            with sp.Fori(0, LAYERS) as l:
                for n in range(PER_LAYER):
                    i = l * PER_LAYER + n
                    if n == 0:
                        sp.wait_ge(z["f2_add"], l * 4 + 1)
                        sp.wait_ge(z["ln_out"], 2 * l + 1)
                        sp.dma_start(tw1s[:, :], fw1[l]).then_inc(z["ffw"], 16)
                        sp.dma_start(tw2s[:, :, :], fw2[l]).then_inc(z["ffw"], 16)
                        sp.dma_start(tb1s[:, :], fb1[l]).then_inc(z["ffw"], 16)
                        sp.dma_start(fb2r[:, :], fb2[l]).then_inc(z["ffw"], 16)
                        sp.dma_start(lnw[:, 0, :], ln2w[l]).then_inc(z["ffw"], 16)
                        sp.dma_start(lnw[:, 1, :], ln2b[l]).then_inc(z["ffw"], 16)
                        sp.dma_start(lnw[:, 2, :], ln1w[l + 1]).then_inc(z["ffw"], 16)
                        sp.dma_start(lnw[:, 3, :], ln1b[l + 1]).then_inc(z["ffw"], 16)
                    sp.wait_ge(z["prod_done"], NCH * i + NCH)
                    b, g = tile_place(l, n + 2) if n + 2 < PER_LAYER else tile_place(l + 1, n + 2 - PER_LAYER)
                    load_tile(n % 2, b, g)
                    b, g = tile_place(l, n)
                    store_tile(i, n % 2, b, g)
            for n in range(4):
                i = LAYERS * PER_LAYER + n
                if n < 2:
                    sp.wait_ge(z["prod_done"], NCH * i + NCH)
                    load_tile(n % 2, n + 2, GROUPS - 1)
                store_tile(i, n % 2, n, GROUPS - 1)
            sp.wait_ge(z["ln_out"], 2 * LAYERS + 1)
            sp.dma_start(h_d.rearrange("(b n) c -> n b c", b=NB)[IMG:N, :, :], XNt[:, :, :]).then_inc(z["h_text"], 16)

            for par in range(2):
                sp.wait_ge(stored[par], 16 * (56 + 1))
            sp.wait_ge(z["h_text"], 16)

            def load_x(b, par):
                sp.dma_start(X[par][:, :, :].rearrange("p j c -> p (j c)"),
                             h_f[bass.ds(b * (N * C), N * C)].rearrange("(p f) -> p f", p=CP)).then_inc(x_in[par], 16)

            def store_h(b, par):
                sp.wait_ge(z["p_h2"], b + 1)
                sp.dma_start(out_f[bass.ds(b * (N * C), N * C)].rearrange("(p j c) -> p j c", p=CP, j=CH),
                             ROW[par][:, :, 0:C]).then_inc(z["o_st"], 16)

            load_x(0, 0)
            load_x(1, 1)
            with sp.Fori(0, NB // 2 - 1) as k:
                for par in range(2):
                    b = 2 * k + par
                    store_h(b, par)
                    load_x(b + 2, par)
            for b in (NB - 2, NB - 1):
                store_h(b, b % 2)

            def load_w(e, par):
                sp.dma_start(W1E[par][:, :], ew1[e]).then_inc(e_w[par], 16)
                sp.dma_start(W2E[par][:, :, :], ew2[e]).then_inc(e_w[par], 16)
                sp.dma_start(B1E[par][:, :], eb1[e]).then_inc(e_w[par], 16)
                sp.dma_start(B2E[par][:, :], eb2[e]).then_inc(e_w[par], 16)

            def load_r(t, q):
                sp.dma_start(R[q][:, :, :].rearrange("p j c -> p (j c)"),
                             slots_f[bass.ds(t * (ST * RW), ST * RW)].rearrange("(p f) -> p f", p=SP_)
                             ).then_inc(e_in[q], 16)

            load_w(0, 0)
            load_w(1, 1)
            for par in range(2):
                sp.wait_ge(scat[par], 16 * CH * (NB // 2) + 16)
            for q in range(4):
                load_r(q, q)
            tiles = E * TILES_E
            with sp.Fori(0, E // 2 - 1) as e2:
                for ep in range(2):
                    e = 2 * e2 + ep
                    with sp.Fori(0, TILES_E // 4) as k:
                        for q in range(4):
                            t = e * TILES_E + k * 4 + q
                            sp.wait_ge(z["e_o"], t + 1)
                            load_r(t + 4, q)
                    load_w(e + 2, ep)
            tail = (E - 2) * TILES_E
            with sp.Fori(0, 2 * TILES_E // 4 - 1) as k:
                for q in range(4):
                    sp.wait_ge(z["e_o"], tail + k * 4 + q + 1)
                    load_r(tail + k * 4 + q + 4, q)
            for q in range(4):
                sp.wait_ge(e_sc[q], 64 * (tiles // 4) + 16)
            sp.wait_ge(z["o_st"], 16 * NB + 16)

        @block.tensor
        def _(pe):
            def wait_first(s, value):
                pe.wait_ge(s, value)
                pe.sem_inc(z["passed_pe"], 1)

            def mm(o, w, r, start=True, stop=True):
                return nc.tensor.matmul(o, w, r, start=start, stop=stop)

            def views(par, half, c):
                pa = PA[par][:, :].rearrange("p (r w) -> p r w", w=PW)
                pb = PB[par][:, :].rearrange("p (r w) -> p r w", w=PW)
                r0 = 4 * half
                if c < 3:
                    return pa[:, c + r0:c + r0 + 4, 0:HW]
                if c == 3:
                    return pb[:, r0:r0 + 4, 0:HW]
                return pa[0:C, 2 + r0:6 + r0, 2:2 + HW]

            def conv(i, par, rounds):
                pe.wait_ge(pa_in[par], 64 * rounds)
                for c in range(NCH):
                    k = C if c == NCH - 1 else P
                    for half in range(2):
                        last = mm(PS[C * half:C * half + C, 0, 0:HALF], w1c[0:k, c, :], views(par, half, c),
                                  start=(c == 0), stop=(c == NCH - 1))
                last.then_inc(z["conv_done"], 1)

            def gates(i, odd, c0=0, c1=NCH):
                for c in range(c0, c1):
                    if c >= 2:
                        wait_first(z["tanh_done"], NCH * i + c - 1)
                    m = C if c == NCH - 1 else P
                    bank = 1 + 2 * ((odd + c) % 2)
                    for half in range(2):
                        last = mm(PS[0:m, bank + half, 0:HALF], w2c[C * half:C * half + C, c, 0:m],
                                  H1[C * half:C * half + C, :])
                    last.then_inc(z["gate_mm"], 1)

            def mix(i):
                for j in range(4):
                    for c in range(NCH):
                        k = C if c == NCH - 1 else P
                        if j == 0:
                            pe.wait_ge(z["prod_done"], NCH * i + c + 1)
                        last = mm(PS[0:TP, 5, C * j:C * j + C], TS[0:k, c, j::4], w3c[0:k, c, :],
                                  start=(c == 0), stop=(c == NCH - 1))
                last.then_inc(z["mix_mm"], 1)

            def text_turn(j, q):
                wait_first(z["v9_done"], j + 1)
                nc.tensor.transpose(PS[0:C, 0, 256:256 + SEQ], XB[q][:, :], ident[0:SEQ, 0:SEQ]
                                    ).then_inc(z["t_done"], 1)

            def text_scores(j):
                pe.wait_ge(z["kx_done"], j + 1)
                pe.wait_ge(z["ao_done"], j + 1)
                for s in range(2):
                    last = mm(PS[0:SEQ, 6 + s, 0:HALFS], XT[:, :], KX[:, 4 * s:4 * s + 4, :])
                last.then_inc(z["sc_done"], 1)

            def text_probs_turn(j):
                pe.wait_ge(z["exp_done"], j + 1)
                for h in range(HEADS):
                    s, o = h // 4, h % 4 * SEQ
                    last = nc.tensor.transpose(PS[0:SEQ, 6 + s, o:o + SEQ], PR[:, s, o:o + SEQ], ident[0:SEQ, 0:SEQ])
                last.then_inc(z["ptr_done"], 1)

            def text_values(j, q):
                pe.wait_ge(z["pt_done"], j + 1)
                for h in range(HEADS):
                    s, o = h // 4, h % 4 * SEQ
                    last = mm(PS[0:SEQ, 6, 384 + 9 * h:393 + 9 * h], PT[:, s, o:o + SEQ], V9[q][:, h, :])
                last.then_inc(z["pv_done"], 1)

            pe.wait_ge(z["consts"], ALL_CONSTS)
            pe.wait_ge(z["emb_oh"], 1)
            for c in range(8):
                last = mm(PS[0:SEQ, 0, 0:C], poh[:, c, :], tabs[:, c, :], start=(c == 0), stop=(c == 7))
            for b in range(NB):
                last = mm(PS[0:SEQ, 1 + b // 8, C * (b % 8):C * (b % 8) + C], tokf[:, SEQ * b:SEQ * b + SEQ], embs[:, :])
            last.then_inc(z["emb_mm"], 1)
            pe.wait_ge(z["embd"], 4)

            with pe.Fori(0, LAYERS) as l:
                with pe.Fori(0, NB // 4) as k:
                    for q in range(4):
                        i = l * PER_LAYER + k * 4 + q
                        j = l * NB + k * 4 + q
                        if q == 0:
                            conv(i, q % 2, l * 9 + k * 2 + q // 2 + 1)
                        pe.wait_ge(z["relu_done"], i + 1)
                        text_turn(j, q)
                        gates(i, q, 0, 3)
                        if q:
                            text_values(j - 1, q - 1)
                        gates(i, q, 3, NCH)
                        text_scores(j)
                        if q < 3:
                            conv(i + 1, (q + 1) % 2, l * 9 + k * 2 + (q + 1) // 2 + 1)
                        mix(i)
                        text_probs_turn(j)
                        if q == 3:
                            text_values(j, q)
                for u in range(2):
                    i = l * PER_LAYER + NB + u
                    conv(i, u, l * 9 + 9)
                    pe.wait_ge(z["relu_done"], i + 1)
                    gates(i, u)
                    mix(i)
                pe.wait_ge(z["ffw"], 128 * l + 128)
                wait_first(z["ln_out"], 2 * l + 2)
                for n in range(4):
                    if n >= 2:
                        wait_first(z["x2_cp"], l * 4 + n - 1)
                    for m in range(4):
                        last = nc.tensor.transpose(PS[0:C, 6 + n % 2, SEQ * m:SEQ * m + SEQ], XNt[:, 4 * n + m, :],
                                                   ident[0:SEQ, 0:SEQ])
                    last.then_inc(z["x2_tr"], 1)
                for n in range(4):
                    pe.wait_ge(z["x2_cp"], l * 4 + max(n, 0) + 1)
                    for f in range(2):
                        i8 = 2 * n + f
                        if n == 0:
                            pe.wait_ge(z["x2_cp"], l * 4 + 4)
                        else:
                            pe.wait_ge(z["gelu_done"], l * 8 + i8 - 1)
                        mm(PS[:, 6 + f, 0:HALFS], tw1s[:, P * f:P * f + P], X2T[:, HALFS * n:HALFS * n + HALFS]
                           ).then_inc(z["f1_mm"], 1)
                for n in range(4):
                    pe.wait_ge(z["gelu_done"], l * 8 + 2 * n + 2)
                    if n:
                        pe.wait_ge(z["f2_add"], l * 4 + n + 1)
                    else:
                        pe.wait_ge(z["mix_out"], l * PER_LAYER + PER_LAYER)
                    for m in range(4):
                        for f in range(2):
                            o = SEQ * (4 * n + m)
                            last = mm(PS[0:SEQ, 5, 256 + C * m:256 + C * m + C], GH[:, f, o:o + SEQ], tw2s[:, f, :],
                                      start=(f == 0), stop=(f == 1))
                    last.then_inc(z["f2_mm"], 1)
            for n in range(4):
                i = LAYERS * PER_LAYER + n
                conv(i, n % 2, LAYERS * 9 + n // 2 + 1)
                pe.wait_ge(z["relu_done"], i + 1)
                gates(i, n)
                mix(i)

            T0, T1, T2 = 4, 5, 6
            CTX = 7
            pe.wait_ge(z["mix_out"], LAYERS * PER_LAYER + 4)

            def pre(b, par):
                wait_first(z["f_xn"], b + 1)
                for g in range(7):
                    if g >= 2:
                        wait_first(z["f_trc"], 7 * b + g - 1)
                    js = range(4 * g, min(4 * g + 4, CH))
                    for j in js:
                        last = nc.tensor.transpose(PS[0:C, T0 + g % 2, CP * (j - 4 * g):CP * (j - 4 * g) + CP],
                                                   XN[:, j, :], ident[0:CP, 0:CP])
                    last.then_inc(z["f_tr"], 1)
                pe.wait_ge(z["f_trc"], 7 * b + 7)
                for g in range(7):
                    if g >= 2:
                        pe.wait_ge(z["f_kmx"], 7 * b + g - 1)
                    mm(PS[:, T0 + g % 2, 0:KW], WQ[par][0:C, HID:2 * HID], XNT[par][0:C, KW * g:KW * g + KW]
                       ).then_inc(z["f_km"], 1)
                pe.wait_ge(z["f_nk"], b + 1)
                mm(PS[C:C + 1, T0, 0:P], NK[par][:, :], ident[:, :]).then_inc(z["f_nkr"], 1)
                pe.wait_ge(z["f_em"], b + 1)
                nc.tensor.transpose(PS[0:MEM, T1, 0:P], EM[:, :], ident[:, :]).then_inc(z["f_emt"], 1)
                pe.wait_ge(z["f_wrow"], b + 1)
                pe.wait_ge(z["f_emc"], b + 1)

            def chunks(g):
                return range(2 * g, min(2 * g + 2, CH))

            NG = 14

            def project(b, par, g):
                G = NG * b + g
                if g >= 2:
                    pe.wait_ge(z["q_v"], G - 1)
                    pe.wait_ge(z["q_sub"], G - 1)
                for j in chunks(g):
                    x, s = XNT[par][:, CP * j:CP * j + CP], j % 2
                    mm(PS[0:CP, g % 2, HID * s:HID * s + HID], x, WQ[par][:, 0:HID])
                    last = mm(PS[0:CP, 2 + g % 2, 2 * HID * s:2 * HID * s + 2 * HID], x, WQ[par][:, HID:3 * HID])
                last.then_inc(z["q_mm"], 1)

            def context(b, g):
                G = NG * b + g
                pe.wait_ge(z["q_ek"], G + 1)
                pe.wait_ge(z["q_v"], G + 1)
                for j in chunks(g):
                    last = mm(PS[:, CTX, 0:HID + 1], EK[g % 2][:, j % 2, :], V[g % 2][:, j % 2, :],
                              start=False, stop=(j == CH - 1))
                last.then_inc(z["q_ctx"], 1)

            def turn_q(b, g):
                G = NG * b + g
                pe.wait_ge(z["q_n"], G + 1)
                if g >= 1:
                    pe.wait_ge(z["q_trc"], G)
                for j in chunks(g):
                    o = CP * (j % 2)
                    last = nc.tensor.transpose(PS[:, T2, o:o + CP], QN[g % 2][:, j % 2, :], ident[0:CP, 0:CP])
                last.then_inc(z["q_tr"], 1)

            def groups(b, par):
                project(b, par, 0)
                mm(PS[:, CTX, 0:HID + 1], EMT[par][:, :], VM[:, :], start=True, stop=False)
                for g in range(NG):
                    if g + 1 < NG:
                        project(b, par, g + 1)
                    context(b, g)
                    if g:
                        turn_q(b, g - 1)
                turn_q(b, NG - 1)

            def post(b, par):
                pe.wait_ge(z["p_cn"], b + 1)
                nc.tensor.transpose(PS[:, T0, 0:P], CN[:, :], ident[:, :]).then_inc(z["p_ct"], 1)
                pe.wait_ge(z["p_ctc"], b + 1)
                mm(PS[:, T1, 0:C], CT[:, :], wout_s[:, :]).then_inc(z["p_m"], 1)
                pe.wait_ge(z["p_mc"], b + 1)
                pe.wait_ge(z["q_trc"], NG * b + NG)
                for g in range(4):
                    if g >= 2:
                        pe.wait_ge(z["p_yb"], 4 * b + g - 1)
                    for j in range(8 * g, min(8 * g + 8, CH)):
                        last = mm(PS[0:CP, T0 + g % 2, C * (j % 8):C * (j % 8) + C], QT[:, CP * j:CP * j + CP], MM[:, :])
                    last.then_inc(z["p_y"], 1)
                wait_first(z["p_xf"], b + 1)
                for g in range(7):
                    if g >= 2:
                        wait_first(z["p_xtc"], 7 * b + g - 1)
                    for j in range(4 * g, min(4 * g + 4, CH)):
                        last = nc.tensor.transpose(PS[0:C, T0 + g % 2, CP * (j - 4 * g):CP * (j - 4 * g) + CP],
                                                   XF[:, j, :], ident[0:CP, 0:CP])
                    last.then_inc(z["p_xt"], 1)
                pe.wait_ge(z["p_xtc"], 7 * b + 7)
                for j in range(CH):
                    last = mm(PS[0:CP, T0, E * j:E * j + E], XFT[:, CP * j:CP * j + CP], gate_s[:, :])
                last.then_inc(z["p_lg"], 1)
                pe.wait_ge(z["p_rt"], b + 1)
                mm(PS[0:CP, T1, 0:E], TRI[:, :], RT[:, :], start=True, stop=False)
                mm(PS[0:CP, T1, 0:E], ONES[:, :], CR[:, :], start=False, stop=True).then_inc(z["p_tri"], 1)
                pe.wait_ge(z["p_slot"], b + 1)

            pre(0, 0)
            with pe.Fori(0, NB // 2 - 1) as k:
                for par in range(2):
                    b = 2 * k + par
                    groups(b, par)
                    pre(b + 1, 1 - par)
                    post(b, par)
            for b in (NB - 2, NB - 1):
                groups(b, b % 2)
                if b + 1 < NB:
                    pre(b + 1, 1 - b % 2)
                post(b, b % 2)

            def turn_x(t, q):
                wait_first(z["e_x"], t + 1)
                for k4 in range(4):
                    last = nc.tensor.transpose(PS[0:C, q % 2, SP_ * k4:SP_ * k4 + SP_], RX[q % 2][:, k4, :],
                                               ident[0:SP_, 0:SP_])
                last.then_inc(z["e_xt"], 1)

            def mlp(t, q, ep):
                pe.wait_ge(z["e_xc"], t + 1)
                for f in range(2):
                    mm(PS[:, 2 + 2 * (q % 2) + f, 0:ST], W1E[ep][:, P * f:P * f + P], XE[q % 2][:, :]
                       ).then_inc(z["e_h"], 1)
                pe.wait_ge(z["e_ha"], t + 1)
                pe.wait_ge(z["e_hd"], t + 1)
                for k4 in range(4):
                    for f in range(2):
                        last = mm(PS[0:SP_, 6 + q % 2, C * k4:C * k4 + C], HE[q % 2][:, f, SP_ * k4:SP_ * k4 + SP_],
                                  W2E[ep][:, f, :], start=(f == 0), stop=(f == 1))
                last.then_inc(z["e_y"], 1)

            with pe.Fori(0, E // 2) as e2:
                for ep in range(2):
                    e = 2 * e2 + ep
                    with pe.Fori(0, TILES_E // 4) as k:
                        pe.wait_ge(e_w[ep], 64 * e2 + 64)
                        t = e * TILES_E + k * 4
                        turn_x(t, 0)
                        for q in range(4):
                            if q < 3:
                                turn_x(t + q + 1, q + 1)
                            mlp(t + q, q, ep)

        @block.scalar
        def _(act):
            def fn(o, i, f, **kw):
                return nc.scalar.activation(o, i, f, **kw)

            def relu(i):
                act.wait_ge(z["conv_done"], i + 1)
                fn(H1[:, :], PS[:, 0, 0:HALF], ACT.Relu, bias=b1c[:, 0:1]).then_inc(z["relu_done"], 1)

            def tanhs(i, odd):
                for c in range(NCH):
                    act.wait_ge(z["gate_mm"], NCH * i + c + 1)
                    m = C if c == NCH - 1 else P
                    bank = 1 + 2 * ((odd + c) % 2)
                    fn(S[0:m, c, :].rearrange("p (a n) -> p a n", a=2), PS[0:m, bank:bank + 2, 0:HALF],
                       ACT.Tanh, bias=b2c[0:m, c:c + 1], scale=0.5).then_inc(z["tanh_done"], 1)

            def square_ln(n):
                act.wait_ge(z["ln_xc"], n + 1)
                fn(TSQ[:, :, :], TC_[:, :, :], ACT.Square).then_inc(z["ln_sq"], 1)

            act.wait_ge(z["consts"], ALL_CONSTS)
            act.wait_ge(z["dinit"], 1)
            square_ln(0)
            with act.Fori(0, LAYERS) as l:
                with act.Fori(0, NB // 4) as k:
                    for q in range(4):
                        i = l * PER_LAYER + k * 4 + q
                        j = l * NB + k * 4 + q
                        if q == 0:
                            relu(i)
                        act.wait_ge(z["t_done"], j + 1)
                        fn(XT[:, :], PS[0:C, 0, 256:256 + SEQ], ACT.Copy).then_inc(z["xt_done"], 1)
                        tanhs(i, q)
                        if q < 3:
                            relu(i + 1)
                        act.wait_ge(z["soft_sub"], j + 1)
                        fn(PR[:, :, :], SB_[:, :, :], ACT.Exp).then_inc(z["exp_done"], 1)
                        act.wait_ge(z["ptr_done"], j + 1)
                        fn(PT[:, :, :], PS[0:SEQ, 6:8, 0:HALFS], ACT.Copy).then_inc(z["pt_done"], 1)
                for u in range(2):
                    i = l * PER_LAYER + NB + u
                    relu(i)
                    if u == 0:
                        square_ln(2 * l + 1)
                    tanhs(i, u)
                for n in range(4):
                    act.wait_ge(z["x2_tr"], l * 4 + n + 1)
                    fn(X2T[:, HALFS * n:HALFS * n + HALFS], PS[0:C, 6 + n % 2, 0:HALFS], ACT.Copy
                       ).then_inc(z["x2_cp"], 1)
                for n in range(4):
                    for f in range(2):
                        act.wait_ge(z["f1_mm"], l * 8 + 2 * n + f + 1)
                        fn(GH[:, f, HALFS * n:HALFS * n + HALFS], PS[:, 6 + f, 0:HALFS], ACT.Gelu,
                           bias=tb1s[:, f:f + 1]).then_inc(z["gelu_done"], 1)
                square_ln(2 * l + 2)
            for n in range(4):
                i = LAYERS * PER_LAYER + n
                relu(i)
                tanhs(i, n)

            T0, T1, T2 = 4, 5, 6
            NG = 14

            def pre(b, par):
                act.wait_ge(z["f_xc"], b + 1)
                fn(SQ[:, :, :], XC[:, :, :], ACT.Square).then_inc(z["f_sq"], 1)
                for g in range(7):
                    act.wait_ge(z["f_tr"], 7 * b + g + 1)
                    w = CP * min(4, CH - 4 * g)
                    fn(XNT[par][0:C, 4 * CP * g:4 * CP * g + w], PS[0:C, T0 + g % 2, 0:w], ACT.Copy
                       ).then_inc(z["f_trc"], 1)
                act.wait_ge(z["f_nk"], b + 1)
                fn(EM[:, :], memk_s[:, :], ACT.Exp, bias=NK[par][:, :]).then_inc(z["f_em"], 1)
                act.wait_ge(z["f_emt"], b + 1)
                fn(EMT[par][:, :], PS[0:MEM, T1, 0:P], ACT.Copy).then_inc(z["f_emc"], 1)

            def n_of(g):
                return min(2, CH - 2 * g)

            def groups(b):
                def copy_q(g):
                    act.wait_ge(z["q_tr"], NG * b + g + 1)
                    w = CP * n_of(g)
                    fn(QT[:, 2 * CP * g:2 * CP * g + w], PS[:, T2, 0:w], ACT.Copy
                       ).then_inc(z["q_trc"], 1)

                for g in range(NG):
                    G = NG * b + g
                    n = n_of(g)
                    kv = PS[0:CP, 2 + g % 2, 0:2 * HID * n].rearrange("p (n c) -> p n c", n=n)
                    act.wait_ge(z["q_mm"], G + 1)
                    if g >= 2:
                        act.wait_ge(z["q_ctx"], G - 1)
                    fn(EK[g % 2][:, 0:n, :], kv[:, :, 0:HID], ACT.Exp).then_inc(z["q_ek"], 1)
                    fn(V[g % 2][:, 0:n, 0:HID], kv[:, :, HID:2 * HID], ACT.Copy).then_inc(z["q_v"], 1)
                    act.wait_ge(z["q_sub"], G + 1)
                    fn(QE[g % 2][:, 0:n, :], QS[g % 2][:, 0:n, :], ACT.Exp).then_inc(z["q_exp"], 1)
                    if g:
                        copy_q(g - 1)
                copy_q(NG - 1)

            def post(b, par):
                act.wait_ge(z["p_yb"], 4 * b + 4)
                fn(SQ2[:, :, :], Y[:, :, :], ACT.Square).then_inc(z["p_sq"], 1)
                act.wait_ge(z["p_c2"], b + 1)
                fn(SQ2[:, :, :], XF[:, :, :], ACT.Square).then_inc(z["p_c2s"], 1)
                for g in range(7):
                    act.wait_ge(z["p_xt"], 7 * b + g + 1)
                    w = CP * min(4, CH - 4 * g)
                    fn(XFT[0:C, 4 * CP * g:4 * CP * g + w], PS[0:C, T0 + g % 2, 0:w], ACT.Copy
                       ).then_inc(z["p_xtc"], 1)
                act.wait_ge(z["p_d"], b + 1)
                fn(EX[:, :, :], D[:, :, :], ACT.Exp).then_inc(z["p_ex"], 1)

            pre(0, 0)
            with act.Fori(0, NB // 2 - 1) as k:
                for par in range(2):
                    b = 2 * k + par
                    groups(b)
                    pre(b + 1, 1 - par)
                    post(b, par)
            for b in (NB - 2, NB - 1):
                groups(b)
                if b + 1 < NB:
                    pre(b + 1, 1 - b % 2)
                post(b, b % 2)

            with act.Fori(0, E // 2) as e2:
                for ep in range(2):
                    e = 2 * e2 + ep
                    with act.Fori(0, TILES_E // 4) as k:
                        act.wait_ge(e_w[ep], 64 * e2 + 64)
                        t = e * TILES_E + k * 4

                        def copy_x(q):
                            act.wait_ge(z["e_xt"], t + q + 1)
                            fn(XE[q % 2][:, :], PS[0:C, q % 2, 0:ST], ACT.Copy).then_inc(z["e_xc"], 1)

                        copy_x(0)
                        for q in range(4):
                            if q < 3:
                                copy_x(q + 1)
                            act.wait_ge(z["e_h"], 2 * t + 2 * q + 2)
                            fn(HE[q % 2][:, 0, :], PS[:, 2 + 2 * (q % 2), 0:ST], ACT.Relu,
                               bias=B1E[ep][:, 0:1]).then_inc(z["e_ha"], 1)

        @block.gpsimd
        def _(pool):
            gp = nc.gpsimd
            for n, s in enumerate(scat + e_sc):
                pool.dma_start(spare2[0:1, 8 * n:8 * n + 8], vocab_d[0:1, :]).then_inc(s, 16)
            pool.wait_ge(z["zeroed"], 1)

            def ln_power(n):
                pool.wait_ge(z["ln_var"], n + 1)
                gp.tensor_tensor(strs[:, :], st2[:, :], halfneg[0:SEQ, 0:NB], ALU.pow).then_inc(z["ln_pow"], 1)

            ln_power(0)
            with pool.Fori(0, LAYERS) as l:
                with pool.Fori(0, NB // 4) as k:
                    pool.wait_ge(z["ln_out"], 2 * l + 1)
                    for q in range(4):
                        j = l * NB + k * 4 + q
                        pool.wait_ge(z["pv_done"], j + 1)
                        gp.tensor_copy(XB[q][:, :], XNt[:, bass.ds(k * 4 + q, 1), :].rearrange("p o c -> p (o c)"))
                        gp.tensor_copy(V9[q][:, :, 0:HD],
                                       XNt[:, bass.ds(k * 4 + q, 1), :].rearrange("p o (h d) -> p (o h) d", h=HEADS)
                                       ).then_inc(z["v9_done"], 1)
                ln_power(2 * l + 1)
                ln_power(2 * l + 2)

            NG = 14

            def pre(b, par):
                pool.wait_ge(z["f_var"], b + 1)
                gp.tensor_tensor(rr[:, :], vv[:, :], halfneg[0:CP, :], ALU.pow).then_inc(z["f_pow"], 1)
                pool.wait_ge(z["f_pow"], b + 1)
                gp.tensor_tensor(XIN[par][:, :, :], XC[:, :, :], rr[:, 0:CH].unsqueeze(2).to_broadcast([CP, CH, C]),
                                 ALU.mult).then_inc(z["f_xin"], 1)

            def groups(b):
                for g in range(NG):
                    G = NG * b + g
                    n = min(2, CH - 2 * g)
                    pool.wait_ge(z["q_rq"], G + 1)
                    if g >= 2:
                        pool.wait_ge(z["q_tr"], G - 1)
                    gp.tensor_tensor(QN[g % 2][:, 0:n, :].rearrange("p n (h d) -> p (n h) d", h=AH),
                                     QE[g % 2][:, 0:n, :].rearrange("p n (h d) -> p (n h) d", h=AH),
                                     rq[g % 2][:, 0:n, :].rearrange("p n h -> p (n h)").unsqueeze(2)
                                     .to_broadcast([CP, n * AH, AD]), ALU.mult).then_inc(z["q_n"], 1)

            def post(b, par, rounds):
                pool.wait_ge(z["p_ss"], b + 1)
                gp.tensor_tensor(rr2[:, :], vv2[:, :], halfneg[0:CP, CH:2 * CH], ALU.pow).then_inc(z["p_pow"], 1)
                pool.wait_ge(z["p_yn"], b + 1)
                pool.wait_ge(z["f_xin"], b + 1)
                gp.tensor_tensor(Y[:, :, :], Y[:, :, :], XIN[par][:, :, :], ALU.add).then_inc(z["p_yx"], 1)
                pool.wait_ge(z["p_v3"], b + 1)
                gp.tensor_tensor(rr3[:, :], vv3[:, :], halfneg[0:CP, 0:CH], ALU.pow).then_inc(z["p_pw3"], 1)
                pool.wait_ge(z["p_slot"], b + 1)
                pool.sem_inc(z["passed_pool"], 1)
                for j in range(CH):
                    gp.indirect_dma_start(out=slots_d[:, :],
                                          out_offset=bass.IndirectOffsetOnAxis(ap=SLOT[par][:, j:j + 1], axis=0),
                                          in_=ROW[par][:, j, :], in_offset=None, bounds_check=SLOTS - 1,
                                          oob_is_err=False).then_inc(scat[par], 16)

            pool.wait_ge(z["wts"], 16 * (SLOTS * RW // (P * 1071)))
            pre(0, 0)
            with pool.Fori(0, NB // 2 - 1) as k:
                for par in range(2):
                    b = 2 * k + par
                    groups(b)
                    pre(b + 1, 1 - par)
                    post(b, par, k)
            for b in (NB - 2, NB - 1):
                groups(b)
                if b + 1 < NB:
                    pre(b + 1, 1 - b % 2)
                post(b, b % 2, b // 2)

            pool.wait_ge(z["o_st"], 16 * NB + 16)
            with pool.Fori(0, E * TILES_E // 4) as k:
                for q in range(4):
                    pool.wait_ge(z["e_o"], k * 4 + q + 1)
                    pool.sem_inc(z["passed_pool"], 1)
                    for k4 in range(4):
                        gp.indirect_dma_start(out=out_rows,
                                              out_offset=bass.IndirectOffsetOnAxis(ap=IDX[q][:, k4:k4 + 1], axis=0),
                                              in_=OE[q][:, k4, :], in_offset=None, bounds_check=TOK - 1,
                                              oob_is_err=False).then_inc(e_sc[q], 16)

        @block.vector
        def _(dve):
            ve = nc.vector

            def bc(ap, shape):
                return ap.to_broadcast(shape)

            LNX = [SEQ, NB, C]

            def layernorm(n, w):
                ch = Chain(dve, z["lnd"], n * LN_STEPS)
                ch.after(ve.reduce_sum(st1[:, :], XS[:, :, :], AX))
                ch.after(ve.tensor_scalar(st1[:, :], st1[:, :], -1.0 / C, None, ALU.mult))
                ve.tensor_tensor(TC_[:, :, :], XS[:, :, :], bc(st1[:, :].unsqueeze(2), LNX), ALU.add
                                 ).then_inc(z["ln_xc"], 1)
                dve.wait_ge(z["ln_sq"], n + 1)
                ch.after(ve.reduce_sum(st2[:, :], TSQ[:, :, :], AX))
                ve.tensor_scalar(st2[:, :], st2[:, :], 1.0 / C, LN_EPS, ALU.mult, ALU.add).then_inc(z["ln_var"], 1)
                dve.wait_ge(z["ln_pow"], n + 1)
                ch.after(ve.tensor_tensor(TC_[:, :, :], TC_[:, :, :], bc(strs[:, :].unsqueeze(2), LNX), ALU.mult))
                ch.after(ve.tensor_tensor(TC_[:, :, :], TC_[:, :, :], bc(lnw[:, w:w + 1, :], LNX), ALU.mult))
                assert ch.n == LN_STEPS
                ve.tensor_tensor(XNt[:, :, :], TC_[:, :, :], bc(lnw[:, w + 1:w + 2, :], LNX), ALU.add
                                 ).then_inc(z["ln_out"], 1)

            def views(par, c):
                pa = PA[par][:, :].rearrange("p (r w) -> p r w", w=PW)
                pb = PB[par][:, :].rearrange("p (r w) -> p r w", w=PW)
                if c < 3:
                    return pa[:, c:c + ROWS, 0:HW]
                if c == 3:
                    return pb[:, 0:ROWS, 0:HW]
                return pa[0:C, 2:2 + ROWS, 2:2 + HW]

            def products(i, par, rounds, c0=0, c1=NCH):
                dve.wait_ge(pa_in[par], 64 * rounds)
                for c in range(c0, c1):
                    m = C if c == NCH - 1 else P
                    dve.wait_ge(z["tanh_done"], NCH * i + c + 1)
                    ve.scalar_tensor_tensor(TS[0:m, c, :].rearrange("p (r w) -> p r w", w=HW),
                                            S[0:m, c, :].rearrange("p (r w) -> p r w", w=HW), 1.0, views(par, c),
                                            op0=ALU.add, op1=ALU.mult).then_inc(z["prod_done"], 1)

            def mix_out(i, par, rounds):
                dve.wait_ge(z["mix_mm"], i + 1)
                dve.wait_ge(stored[par], 16 * rounds)
                ve.tensor_tensor(OT[par][:, :, :], PS[0:TP, 5, 0:4 * C].rearrange("p (j c) -> p j c", j=4),
                                 bc(b3r[:, :].unsqueeze(1), [TP, 4, C]), ALU.add).then_inc(z["mix_out"], 1)

            def attend_out(j, b):
                ch = Chain(dve, z["aod"], j * AO_STEPS)
                dve.wait_ge(z["pv_done"], 4 + j + 1)
                o9 = PS[0:SEQ, 6, 384:384 + 9 * HEADS].rearrange("p (h d) -> p h d", h=HEADS)
                ch.after(ve.reciprocal(rs[:, :], o9[:, :, HD]))
                ch.after(ve.tensor_tensor(AO[:, :, :], o9[:, :, 0:HD], bc(rs[:, :].unsqueeze(2), [SEQ, HEADS, HD]),
                                          ALU.mult))
                xs = XS[:, bass.ds(b, 1), :].rearrange("p o c -> p (o c)")
                ve.tensor_tensor(xs, xs, AO[:, :, :].rearrange("p h d -> p (h d)"), ALU.add).then_inc(z["ao_done"], 1)

            def softmax(j):
                ch = Chain(dve, z["softd"], j * SOFT_STEPS)
                dve.wait_ge(z["sc_done"], j + 1)
                ch.after(ve.tensor_tensor(SB_[:, :, :], PS[0:SEQ, 6:8, 0:HALFS], bias_t[:, :, :], ALU.add))
                s3 = SB_[:, :, :].rearrange("p a (h t) -> p (a h) t", h=4)
                ch.after(ve.reduce_max(mx[:, :], s3, AX))
                ve.tensor_tensor(s3, s3, bc(mx[:, :].unsqueeze(2), [SEQ, HEADS, SEQ]), ALU.subtract
                                 ).then_inc(z["soft_sub"], 1)

            ve.memset(halfneg[:, 0:CH], -0.5)
            ve.memset(halfneg[:, CH:2 * CH], 0.5)
            for q in range(4):
                ve.memset(V9[q][:, :, HD:HD + 1], 1.0)
            ve.memset(XFT[C:C + 1, :], 1.0)
            ve.memset(ONES[:, :], 1.0)
            ve.memset(CR[:, :], 0.0)
            for par in range(2):
                ve.memset(V[par][:, :, HID:HID + 1], 1.0)
                ve.memset(XNT[par][C:C + 1, :], 1.0)
            credits = [(stored[0], 16), (stored[1], 16), (z["f2_add"], 1), (z["pv_done"], 4),
                       (z["ao_done"], 1), (z["o_st"], 16)]
            for n, (s, v) in enumerate(credits):
                ve.memset(spare[:, n:n + 1], 0.0).then_inc(s, v)
            ve.memset(zeros[:, :], 0.0).then_inc(z["zeroed"], 1)
            dve.wait_ge(z["consts"], ALL_CONSTS)
            ini = Chain(dve, z["embd"], 0)
            ve.memset(KM[:, :], 0.0)
            ve.tensor_scalar(w3c[:, :, :], w3c[:, :, :], 0.5, None, ALU.mult)
            ve.tensor_scalar(gout_s[:, :], gout_s[:, :], float(C) ** 0.5, None, ALU.mult)
            ini.after(ve.tensor_scalar(gpre_s[:, :], gpre_s[:, :], float(C) ** 0.5, None, ALU.mult))
            for par in range(2):
                ve.tensor_scalar(WQ[par][0:C, :], WQ[par][0:C, :], gpre_s[:, 0:1], None, ALU.mult)
            ve.tensor_scalar(b2c[:, :], b2c[:, :], 0.5, None, ALU.mult).then_inc(z["dinit"], 1)
            ve.tensor_copy(tokf[:, :], toki[:, :])
            ini.after(ve.tensor_copy(posf[:, :], posi[:, :]))
            for c in range(8):
                ve.tensor_scalar(poh[:, c, :], posf[:, :], vocab[:, c:c + 1], None, ALU.is_equal)
            ve.tensor_scalar(tokf[:, :], tokf[:, :], vocab[0:16, 0:1], None, ALU.is_equal).then_inc(z["emb_oh"], 1)
            dve.wait_ge(z["emb_mm"], 1)
            ini.after(ve.tensor_scalar(posw[:, :], PS[0:SEQ, 0, 0:C], iws[:, 1:2], None, ALU.mult))
            for s in range(2):
                o = ve.scalar_tensor_tensor(XS[:, 8 * s:8 * s + 8, :],
                                            PS[0:SEQ, 1 + s, :].rearrange("p (b c) -> p b c", c=C), iws[:, 0:1],
                                            bc(posw[:, :].unsqueeze(1), [SEQ, 8, C]), op0=ALU.mult, op1=ALU.add)
            ini.after(o)
            layernorm(0, 2)
            with dve.Fori(0, LAYERS) as l:
                with dve.Fori(0, NB // 4) as k:
                    for q in range(4):
                        i = l * PER_LAYER + k * 4 + q
                        j = l * NB + k * 4 + q
                        rounds = l * 9 + k * 2 + q // 2 + 1
                        dve.wait_ge(z["xt_done"], j + 1)
                        ve.tensor_tensor(KX[:, :, :], bc(XT[:, :].unsqueeze(1), [C, HEADS, SEQ]),
                                         bc(hmask[:, :].unsqueeze(2), [C, HEADS, SEQ]), ALU.mult
                                         ).then_inc(z["kx_done"], 1)
                        products(i, q % 2, rounds, 0, 2)
                        if q:
                            attend_out(j - 1, k * 4 + q - 1)
                        products(i, q % 2, rounds, 2, NCH)
                        softmax(j)
                        mix_out(i, q % 2, rounds)
                        if q == 3:
                            attend_out(j, k * 4 + q)
                dve.wait_ge(z["ao_done"], l * NB + NB + 1)
                dve.wait_ge(z["ffw"], 128 * l + 128)
                layernorm(2 * l + 1, 0)
                for u in range(2):
                    i = l * PER_LAYER + NB + u
                    products(i, u, l * 9 + 9)
                    mix_out(i, u, l * 9 + 9)
                for n in range(4):
                    dve.wait_ge(z["f2_mm"], l * 4 + n + 1)
                    xs = XS[:, 4 * n:4 * n + 4, :]
                    ve.tensor_tensor(xs, xs, PS[0:SEQ, 5, 256:512].rearrange("p (m c) -> p m c", m=4), ALU.add
                                     ).then_inc(z["f2_add"], 1)
                dve.wait_ge(z["f2_add"], l * 4 + 4 + 1)
                ve.tensor_tensor(XS[:, :, :], XS[:, :, :], bc(fb2r[:, :].unsqueeze(1), LNX), ALU.add
                                 ).then_inc(z["xb_done"], 1)
                dve.wait_ge(z["xb_done"], l + 1)
                layernorm(2 * l + 2, 2)
            for n in range(4):
                i = LAYERS * PER_LAYER + n
                products(i, n % 2, LAYERS * 9 + n // 2 + 1)
                mix_out(i, n % 2, LAYERS * 9 + n // 2 + 1)

            T0, T1 = 4, 5
            CTX = 7
            NG = 14
            BX = [CP, CH, C]
            PRE, QG, POST = 8, 2, 18

            mk = Chain(dve, z["crd"], 0)
            mk.after(ve.reduce_max(KM[:, 7:8], memk_s[:, :], AX))

            def pre(b, par, rounds):
                ch = Chain(dve, z["fd"], b * PRE)
                dve.wait_ge(x_in[par], 16 * rounds)
                if not (isinstance(b, int) and b == 0):
                    dve.wait_ge(z["f_xin"], b)
                    dve.wait_ge(z["f_tr"], 7 * b)
                ch.after(ve.reduce_sum(fs[:, 0, :], X[par][:, :, :], AX))
                ch.after(ve.tensor_scalar(fs[:, 0, :], fs[:, 0, :], -1.0 / C, None, ALU.mult))
                ve.tensor_tensor(XC[:, :, :], X[par][:, :, :], bc(fs[:, 0, :].unsqueeze(2), BX), ALU.add
                                 ).then_inc(z["f_xc"], 1)
                dve.wait_ge(z["f_sq"], b + 1)
                ch.after(ve.reduce_sum(vv[:, CH:2 * CH], SQ[:, :, :], AX))
                ve.tensor_scalar(vv[:, 0:CH], vv[:, CH:2 * CH], 1.0 / C, LN_EPS, ALU.mult, ALU.add
                                 ).then_inc(z["f_var"], 1)
                dve.wait_ge(z["f_pow"], b + 1)
                ch.after(ve.tensor_tensor(fs[:, 1, :], rr[:, 0:CH], rr[:, CH:2 * CH], ALU.mult))
                ch.after(ve.tensor_scalar(fs[:, 1, :], fs[:, 1, :], 1e-12, None, ALU.max))
                ch.after(ve.reciprocal(fs[:, 2, :], fs[:, 1, :]))
                ch.after(ve.tensor_tensor(fs[:, 3, :], fs[:, 2, :], rr[:, 0:CH], ALU.mult))
                ve.tensor_tensor(XN[:, :, :], XC[:, :, :], bc(fs[:, 3, :].unsqueeze(2), BX), ALU.mult
                                 ).then_inc(z["f_xn"], 1)
                for g in range(7):
                    dve.wait_ge(z["f_km"], 7 * b + g + 1)
                    ve.reduce_max(KM[:, g:g + 1], PS[:, T0 + g % 2, 0:KW], AX).then_inc(z["f_kmx"], 1)
                dve.wait_ge(z["f_kmx"], 7 * b + 7)
                ch.after(ve.reduce_max(NK[par][:, :], KM[:, :], AX))
                ve.tensor_scalar(NK[par][:, :], NK[par][:, :], -1.0, None, ALU.mult).then_inc(z["f_nk"], 1)
                dve.wait_ge(z["f_nkr"], b + 1)
                ve.tensor_copy(WQ[par][C:C + 1, HID:2 * HID], PS[C:C + 1, T0, 0:P]).then_inc(z["f_wrow"], 1)
                assert ch.n == PRE

            def groups(b):
                for g in range(NG):
                    G = NG * b + g
                    n = min(2, CH - 2 * g)
                    ch = Chain(dve, z["q_gd"], G * QG)
                    q4 = PS[0:CP, g % 2, 0:HID * n].rearrange("p (n h d) -> p n h d", h=AH, d=AD)
                    qs = QS[g % 2][:, 0:n, :].rearrange("p n (h d) -> p n h d", h=AH)
                    qe = QE[g % 2][:, 0:n, :].rearrange("p n (h d) -> p n h d", h=AH)
                    dve.wait_ge(z["q_mm"], G + 1)
                    ch.after(ve.reduce_max(qm[:, 0:n, :], q4, AX))
                    ve.tensor_tensor(qs, q4, bc(qm[:, 0:n, :].unsqueeze(3), [CP, n, AH, AD]), ALU.subtract
                                     ).then_inc(z["q_sub"], 1)
                    dve.wait_ge(z["q_exp"], G + 1)
                    ch.after(ve.reduce_sum(qsum[:, 0:n, :], qe, AX))
                    if g >= 2:
                        dve.wait_ge(z["q_n"], G - 1)
                    ve.reciprocal(rq[g % 2][:, 0:n, :], qsum[:, 0:n, :]).then_inc(z["q_rq"], 1)

            def post(b, par, rounds):
                ch = Chain(dve, z["pd"], b * POST)
                dve.wait_ge(z["q_ctx"], NG * b + NG)
                ch.after(ve.reciprocal(rden[:, :], PS[:, CTX, HID:HID + 1]))
                ve.scalar_tensor_tensor(CN[:, :], PS[:, CTX, 0:HID], rden[:, 0:1], BD[:, :], op0=ALU.mult,
                                        op1=ALU.mult).then_inc(z["p_cn"], 1)
                dve.wait_ge(z["p_ct"], b + 1)
                ve.tensor_copy(CT[:, :], PS[:, T0, 0:P]).then_inc(z["p_ctc"], 1)
                dve.wait_ge(z["p_m"], b + 1)
                ve.tensor_copy(MM[:, :], PS[:, T1, 0:C]).then_inc(z["p_mc"], 1)
                for g in range(4):
                    n = min(8, CH - 8 * g)
                    dve.wait_ge(z["p_y"], 4 * b + g + 1)
                    ve.tensor_tensor(Y[:, 8 * g:8 * g + n, :],
                                     PS[0:CP, T0 + g % 2, 0:C * n].rearrange("p (j c) -> p j c", c=C),
                                     bc(bout_s[:, :].unsqueeze(1), [CP, n, C]), ALU.add).then_inc(z["p_yb"], 1)
                dve.wait_ge(z["p_sq"], b + 1)
                ve.reduce_sum(vv2[:, :], SQ2[:, :, :], AX).then_inc(z["p_ss"], 1)
                dve.wait_ge(z["p_pow"], b + 1)
                ch.after(ve.tensor_scalar(gs[:, 0, :], rr2[:, :], 1e-12, None, ALU.max))
                ch.after(ve.reciprocal(gs[:, 1, :], gs[:, 0, :]))
                ch.after(ve.tensor_tensor(Y[:, :, :], Y[:, :, :], bc(gs[:, 1, :].unsqueeze(2), BX), ALU.mult))
                ve.tensor_tensor(Y[:, :, :], Y[:, :, :], bc(gout_s[:, :].unsqueeze(1), BX), ALU.mult
                                 ).then_inc(z["p_yn"], 1)
                dve.wait_ge(scat[par], rounds * (16 * CH) + 16)
                dve.wait_ge(z["o_st"], b * 16 + 16)
                dve.wait_ge(z["p_yx"], b + 1)
                h2 = ROW[par][:, :, 0:C]
                ve.tensor_tensor(h2, Y[:, :, :], X[par][:, :, :], ALU.add).then_inc(z["p_h2"], 1)
                dve.wait_ge(z["p_h2"], b + 1)
                ch.after(ve.reduce_sum(gs[:, 2, :], h2, AX))
                ch.after(ve.tensor_scalar(ROW[par][:, :, C], gs[:, 2, :], -1.0 / C, None, ALU.mult))
                ve.tensor_tensor(XF[:, :, :], h2, bc(ROW[par][:, :, C:C + 1], BX), ALU.add).then_inc(z["p_c2"], 1)
                dve.wait_ge(z["p_c2s"], b + 1)
                ch.after(ve.reduce_sum(vv3[:, :], SQ2[:, :, :], AX))
                ve.tensor_scalar(vv3[:, :], vv3[:, :], 1.0 / C, LN_EPS, ALU.mult, ALU.add).then_inc(z["p_v3"], 1)
                dve.wait_ge(z["p_pw3"], b + 1)
                ve.tensor_copy(ROW[par][:, :, C + 1], rr3[:, :])
                ve.tensor_copy(ROW[par][:, :, C + 3], TKN[:, :])
                ve.tensor_tensor(XF[:, :, :], XF[:, :, :], bc(rr3[:, :].unsqueeze(2), BX), ALU.mult
                                 ).then_inc(z["p_xf"], 1)
                dve.wait_ge(z["p_xf"], b + 1)
                ve.tensor_scalar(TKN[:, :], TKN[:, :], float(N), None, ALU.add)
                dve.wait_ge(z["p_lg"], b + 1)
                lg = PS[0:CP, T0, 0:CH * E].rearrange("p (j e) -> p j e", e=E)
                ch.after(ve.reduce_max(gs[:, 3, :], lg, AX))
                ve.tensor_tensor(D[:, :, :], lg, bc(gs[:, 3, :].unsqueeze(2), [CP, CH, E]), ALU.subtract
                                 ).then_inc(z["p_d"], 1)
                dve.wait_ge(z["p_d"], b + 1)
                ch.after(ve.scalar_tensor_tensor(CAND[:, :, :], D[:, :, :], 0.0, DESC[:, :, :], op0=ALU.is_ge,
                                                 op1=ALU.mult))
                ch.after(ve.reduce_max(gs[:, 4, :], CAND[:, :, :], AX))
                ch.after(ve.tensor_tensor(OH[:, :, :].rearrange("p e j -> p j e"), DESC[:, :, :],
                                          bc(gs[:, 4, :].unsqueeze(2), [CP, CH, E]), ALU.is_equal))
                ch.after(ve.tensor_tensor_scan(SC[:, :, :].rearrange("p e j -> p (e j)"), KEEP[:, :],
                                               OH[:, :, :].rearrange("p e j -> p (e j)"), 0.0, ALU.mult, ALU.add))
                ve.tensor_copy(RT[:, :], SC[:, :, CH - 1]).then_inc(z["p_rt"], 1)
                dve.wait_ge(z["p_ex"], b + 1)
                ch.after(ve.reduce_sum(gs[:, 5, :], EX[:, :, :], AX))
                ve.reciprocal(ROW[par][:, :, C + 2], gs[:, 5, :])
                dve.wait_ge(z["p_tri"], b + 1)
                ve.tensor_tensor(CR[:, :], CR[:, :], RT[:, :], ALU.add)
                ch.after(ve.tensor_tensor(PX[:, :, :], SC[:, :, :], bc(PS[0:CP, T1, 0:E].unsqueeze(2), [CP, E, CH]),
                                          ALU.add))
                ch.after(ve.tensor_tensor(PX[:, :, :], PX[:, :, :], OH[:, :, :], ALU.mult))
                ch.after(ve.reduce_sum(gs[:, 0, :], PX[:, :, :].rearrange("p e j -> p j e"), AX))
                ve.tensor_scalar(gs[:, 1, :], gs[:, 0, :], float(CAP), float(FAR), ALU.is_gt, ALU.mult)
                ch.after(ve.tensor_scalar(gs[:, 2, :], gs[:, 4, :], -float(STRIDE), float(E * STRIDE - 1), ALU.mult,
                                          ALU.add))
                ch.after(ve.tensor_tensor(gs[:, 2, :], gs[:, 2, :], gs[:, 0, :], ALU.add))
                ve.tensor_tensor(SLOT[par][:, :], gs[:, 2, :], gs[:, 1, :], ALU.add).then_inc(z["p_slot"], 1)
                assert ch.n == POST, ch.n

            pre(0, 0, 1)
            with dve.Fori(0, NB // 2 - 1) as k:
                for par in range(2):
                    b = 2 * k + par
                    groups(b)
                    pre(b + 1, 1 - par, k + 1 + par)
                    post(b, par, k)
            for b in (NB - 2, NB - 1):
                groups(b)
                if b + 1 < NB:
                    pre(b + 1, 1 - b % 2, NB // 2)
                post(b, b % 2, NB // 2 - 1)

            XS4 = [SP_, 4, C]
            EXP = 7

            def prepare(t, q, rounds):
                dve.wait_ge(e_in[q], 16 * rounds)
                for k4 in range(4):
                    o = ve.tensor_scalar(RX[q % 2][:, k4, :], R[q][:, k4, 0:C], R[q][:, k4, C:C + 1],
                                         R[q][:, k4, C + 1:C + 2], ALU.add, ALU.mult)
                o.then_inc(z["e_x"], 1)

            with dve.Fori(0, E // 2) as e2:
                for ep in range(2):
                    e = 2 * e2 + ep
                    with dve.Fori(0, TILES_E // 4) as k:
                        dve.wait_ge(e_w[ep], 64 * e2 + 64)
                        t4 = e * TILES_E + k * 4
                        rounds = e * (TILES_E // 4) + k + 1
                        prepare(t4, 0, rounds)
                        for q in range(4):
                            t = t4 + q
                            if q < 3:
                                prepare(t + 1, q + 1, rounds)
                            ch = Chain(dve, z["ed"], t * EXP)
                            dve.wait_ge(z["e_h"], 2 * t + 2)
                            ve.tensor_scalar(HE[q % 2][:, 1, :], PS[:, 3 + 2 * (q % 2), 0:ST], B1E[ep][:, 1:2], 0.0,
                                             ALU.add, ALU.max).then_inc(z["e_hd"], 1)
                            ve.tensor_scalar(t0[:, :], R[q][:, :, C + 3], 0.0, float(FAR), ALU.is_equal, ALU.mult)
                            ch.after(ve.tensor_scalar(t1[:, :], R[q][:, :, C + 3], -1.0, None, ALU.add))
                            dve.wait_ge(e_sc[q], 64 * rounds - 48)
                            ve.tensor_tensor(IDX[q][:, :], t0[:, :], t1[:, :], ALU.add)
                            dve.wait_ge(z["e_y"], t + 1)
                            ch.after(ve.tensor_tensor(YE[:, :, :],
                                                      PS[0:SP_, 6 + q % 2, 0:4 * C].rearrange("p (j c) -> p j c", c=C),
                                                      bc(B2E[ep][:, :].unsqueeze(1), XS4), ALU.add))
                            ch.after(ve.tensor_tensor(YE[:, :, :], YE[:, :, :], bc(R[q][:, :, C + 2:C + 3], XS4),
                                                      ALU.mult))
                            ve.tensor_scalar(GE_[:, :, :], YE[:, :, :], -FMAX, None, ALU.is_ge)
                            ve.tensor_tensor(EQ[:, :, :], YE[:, :, :], YE[:, :, :], ALU.is_equal)
                            ch.after(ve.tensor_scalar(CE[:, :, :], YE[:, :, :], 1e4, -1e4, ALU.min, ALU.max))
                            ch.after(ve.scalar_tensor_tensor(FM[:, :, :], YE[:, :, :], FMAX, GE_[:, :, :],
                                                             op0=ALU.is_le, op1=ALU.mult))
                            ch.after(ve.tensor_tensor(CE[:, :, :], CE[:, :, :], EQ[:, :, :], ALU.mult), own=True)
                            ch.after(ve.copy_predicated(CE[:, :, :], FM[:, :, :].bitcast(I32), YE[:, :, :]))
                            ve.tensor_tensor(OE[q][:, :, :], CE[:, :, :], R[q][:, :, 0:C], ALU.add
                                             ).then_inc(z["e_o"], 1)
                            assert ch.n == EXP, ch.n


def kernel(**inputs):
    import numpy as np
    import concourse.bacc as bacc
    from concourse.bass_utils import run_bass_kernel_spmd

    g = {k: np.asarray(v) for k, v in inputs.items()}
    f32 = np.float32

    def rep(a, n):
        return np.ascontiguousarray(np.broadcast_to(a[None], (n,) + a.shape))

    x_pad = np.zeros((NB, C, XROW), f32)
    x_pad[:, :, :PW * PW].reshape(NB, C, PW, PW)[:, :, 1:-1, 1:-1] = g["x"]
    pairs = [(0, 1), (3, 4), (6, 7), (2, 5), (8,)]

    def rows_of(w):
        w = w.reshape(C, 9, -1)
        o = np.zeros((P, NCH, w.shape[2]), f32)
        for c, taps in enumerate(pairs):
            for s, t in enumerate(taps):
                o[C * s:C * s + C, c] = w[:, t]
        return o

    w2 = g["L0_tok_W2"].reshape(C, C, 9)
    b2 = g["L0_tok_b2"].reshape(C, 9)
    tw2, tb2 = np.zeros((P, NCH, P), f32), np.zeros((P, NCH), f32)
    for c, taps in enumerate(pairs):
        for s, t in enumerate(taps):
            tw2[0:C, c, C * s:C * s + C] = tw2[C:P, c, C * s:C * s + C] = w2[:, :, t]
            tb2[C * s:C * s + C, c] = b2[:, t]
    wqkv = np.zeros((C + 1, 3 * HID), f32)
    wqkv[:C] = g["L0_attn_w_qkv"]
    memv = np.ones((MEM, HID + 1), f32)
    memv[:, :HID] = g["L0_attn_mem_kv"][1].reshape(HID, MEM).T
    gate = np.concatenate([g["L0_ffn_gate_w"], g["L0_ffn_gate_b"][None]])
    ln1w = np.concatenate([g["L0_txt_ln1_w"], g["L0_txt_lnf_w"][None]])
    ln1b = np.concatenate([g["L0_txt_ln1_b"], g["L0_txt_lnf_b"][None]])

    def each(a, n):
        return np.ascontiguousarray(np.broadcast_to(a[:, None], (a.shape[0], n, a.shape[1])))

    inv = (f32(1.0) / np.power(f32(10000.0), np.arange(0, C, 2, dtype=f32) / f32(C))).astype(f32)
    ang = (np.arange(TABLE, dtype=f32)[:, None] * inv[None]).astype(f32)
    table = np.concatenate([np.sin(ang), np.cos(ang)], 1).astype(f32).reshape(8, P, C).transpose(1, 0, 2)
    s = np.arange(SEQ)
    dist = (np.abs(s[:, None] // 32 - s[None] // 32) + np.abs(s[:, None] % 32 - s[None] % 32)).astype(f32)
    hs = np.arange(HEADS, dtype=f32)
    right = (-np.exp2(-(0.5 + hs))).astype(f32)[:, None, None] * np.triu(dist)[None]
    left = (-np.exp2(-(1.0 + hs))).astype(f32)[:, None, None] * np.tril(dist)[None]
    bias = (right + left).astype(f32).transpose(1, 0, 2).reshape(SEQ, 2, HALFS)
    hmask = (np.arange(C)[:, None] // HD == np.arange(HEADS)[None]).astype(f32) * f32(HD ** -0.5)
    blk = np.arange(P) // AD
    bd = (blk[:, None] == blk[None]).astype(f32) * f32(AD ** -0.5)
    tri = np.triu(np.ones((CP, CP), f32), 1)
    keep = np.ones((CP, E, CH), f32)
    keep[:, :, 0] = 0
    desc = np.broadcast_to((E - np.arange(E)).astype(f32), (CP, CH, E))
    vocab = (np.arange(8)[None] * P + np.arange(P)[:, None]).astype(f32)
    tokn = (np.arange(CP * CH).reshape(CP, CH) + 1).astype(f32)

    ins = dict(
        x_pad=x_pad, x_txt=rep(g["x_txt"].reshape(-1), 16), pos_ids=rep(g["pos_S"], P),
        tw1=rows_of(g["L0_tok_W1"]), tb1=np.tile(g["L0_tok_b1"], 2)[:, None], tw2=tw2, tb2=tb2,
        tw3=rows_of(g["L0_tok_W3"]), tb3=rep(g["L0_tok_b3"], TP), emb=g["L0_txt_emb_table"],
        iw=rep(g["L0_txt_input_weight"], SEQ), pw=rep(g["L0_txt_position_weight"], SEQ),
        ln1w=each(ln1w, SEQ), ln1b=each(ln1b, SEQ), ln2w=each(g["L0_txt_ln2_w"], SEQ), ln2b=each(g["L0_txt_ln2_b"], SEQ),
        fw1=g["L0_txt_w1"], fb1=g["L0_txt_b1"].reshape(LAYERS, 2, P).transpose(0, 2, 1),
        fw2=g["L0_txt_w2"].reshape(LAYERS, 2, P, C).transpose(0, 2, 1, 3), fb2=each(g["L0_txt_b2"], SEQ),
        wqkv=wqkv, memk=g["L0_attn_mem_kv"][0].reshape(HID, MEM), memv=memv, wout=g["L0_attn_w_out"],
        bout=rep(g["L0_attn_b_out"], CP), gout=rep(g["L0_attn_g_out"], CP), gpre=g["L0_attn_g_pre"][:, None],
        gate=gate, ew1=g["L0_ffn_w1"], eb1=g["L0_ffn_b1"].reshape(E, 2, P).transpose(0, 2, 1),
        ew2=g["L0_ffn_w2"].reshape(E, 2, P, C).transpose(0, 2, 1, 3), eb2=each(g["L0_ffn_b2"], SP_),
        ident_d=np.eye(P, dtype=f32), table_d=table, bias_d=bias, hmask_d=hmask, bd_d=bd, tri_d=tri,
        keep_d=keep.reshape(CP, E * CH), desc_d=desc, vocab_d=vocab, tokn_d=tokn)
    nc = bacc.Bacc("TRN2", target_bir_lowering=False, num_devices=1)
    arrays, args = {}, {}
    for name, a in ins.items():
        a = np.ascontiguousarray(a)
        arrays["in_" + name] = a
        args[name] = nc.dram_tensor("in_" + name, a.shape, mybir.dt.from_np(a.dtype), kind="ExternalInput").ap()
    out = nc.dram_tensor("out_0", (NB, N, C), F32, kind="ExternalOutput").ap()
    early_fusion(nc, out=out, **args)
    r = run_bass_kernel_spmd(nc, [arrays], core_ids=[0])
    return r.results[0]["out_0"]
```

```python
from contextlib import ExitStack

import concourse.bass as bass
from concourse import mybir

F32 = mybir.dt.float32
I32 = mybir.dt.int32
ALU = mybir.AluOpType
ACT = mybir.ActivationFunctionType
AX = mybir.AxisListType.X

P = 128
C = 64
NB = 16
HW = 56
PW = HW + 2
IMG = HW * HW
SEQ = 77
N = IMG + SEQ
TOK = NB * N
XROW = PW * PW + 4
ROWS = 8
TT = ROWS * HW
HALF = TT // 2
GROUPS = HW // ROWS
NCH = 5
TP = TT // 4
LAYERS = 6
HEADS, HD = 8, 8
HALFS = HEADS // 2 * SEQ
FF = 256
TABLE = 1024
LN_EPS = 1e-5
PER_LAYER = NB + 2

CH = 27
CP = N // CH
AH, AD, MEM = 4, 32, 4
HID = AH * AD
KW = 460
E = 8
CAP = -(-(5 * TOK) // (4 * E))
ST = 504
SP_ = 126
TILES_E = -(-CAP // ST)
STRIDE = TILES_E * ST
SLOTS = E * STRIDE
RW = C + 4
FAR = 1 << 20
FMAX = 3.4028234663852886e38

CX = C + E
QW = HID + E
YP = 7

assert CH * CP == N <= 7 * KW and KW <= 4 * CP


def early_fusion(nc, x_pad, x_txt, pos_ids, tw1, tb1, tw2, tb2, tw3, tb3, emb, iw, pw, ln1w, ln1b, ln2w, ln2b,
                 fw1, fb1, fw2, fb2, wqkv, memk, memv, wout, bout, gout, gpre, gate, gateb_d, ew1, eb1, ew2, eb2,
                 centre_d, boutT, goutc, ident_d, table_d, bias_d, hmask_d, bd_d, tri_d, keep_d, desc_d, vocab_d, tokn_d, out):
    h_d = nc.dram_tensor("h_scratch", (TOK, C), F32, kind="Internal").ap()
    slots_d = nc.dram_tensor("slots_scratch", (SLOTS, RW), F32, kind="Internal").ap()
    h_f = h_d.rearrange("t c -> (t c)")
    out_f = out.rearrange("b n c -> (b n c)")
    out_rows = out.rearrange("b n c -> (b n) c")
    slots_f = slots_d.rearrange("t c -> (t c)")

    with ExitStack() as ctx:
        def sb(name, shape, dt=F32):
            return ctx.enter_context(nc.sbuf_tensor(name, shape, dt))

        def sem(name):
            return ctx.enter_context(nc.semaphore(name))

        PS = ctx.enter_context(nc.psum_tensor("PS", [P, 8, 512], F32))

        ident = sb("ident", [P, P])
        spare = sb("spare", [P, 16])
        spare2 = sb("spare2", [1, 48])
        halfneg = sb("halfneg", [P, 2 * CH])
        zeros = sb("zeros", [P, 357])

        XNT = [sb(f"XNT{i}", [P, N]) for i in range(2)]
        WQ = sb("WQ", [P, QW + 2 * HID])
        WU = sb("WU", [P, QW + 2 * HID])
        WH = sb("WH", [P, QW + 2 * HID])
        WL = sb("WL", [P, QW + 2 * HID])
        gpre_s = sb("gpre_s", [P, 1])
        KM = sb("KM", [P, 8])
        ONER = sb("ONER", [P, CP])
        memk_s = sb("memk_s", [P, MEM])
        NKR = [sb(f"NKR{i}", [P, 2 * HID]) for i in range(2)]
        VM = sb("VM", [MEM, HID + 1])
        V = [sb(f"V{i}", [CP, 2, HID + 1]) for i in range(2)]
        BD = sb("BD", [P, P])
        wout_s = sb("wout_s", [P, CX])
        bout_s = sb("bout_s", [CP, CX])
        gout_s = sb("gout_s", [CP, C])
        gate_s = sb("gate_s", [C, E])
        gateb = sb("gateb", [CP, E])
        centre = sb("centre", [C, P])
        boutT_s = sb("boutT_s", [C, CP])
        goutc_s = sb("goutc_s", [C, 1])
        GO = sb("GO", [C, E])
        WOT = sb("WOT", [C, P])
        DESC = sb("DESC", [CP, CH, E])
        KEEP = sb("KEEP", [CP, E * CH])
        CR = sb("CR", [CP, E])
        TRI = sb("TRI", [CP, CP])
        ONES = sb("ONES", [P, CP])
        TKN = sb("TKN", [CP, CH])
        rs = sb("rs", [SEQ, HEADS])
        V9 = [sb(f"V9_{i}", [SEQ, HEADS, HD + 1]) for i in range(4)]

        mix_scope = ExitStack()
        outer, ctx = ctx, mix_scope
        w1c = sb("w1c", [P, NCH, C])
        w2c = sb("w2c", [P, NCH, P])
        w2u = sb("w2u", [P, NCH, P])
        w2h = sb("w2h", [P, NCH, P])
        w2l = sb("w2l", [P, NCH, P])
        w3c = sb("w3c", [P, NCH, C])
        b1c = sb("b1c", [P, 1])
        b2c = sb("b2c", [P, NCH])
        b3c = sb("b3c", [P, 1])
        bias_t = sb("bias_t", [SEQ, 2, HALFS])
        hmask = sb("hmask", [C, HEADS])
        PA = [sb(f"PA{i}", [P, 10 * PW]) for i in range(2)]
        PB = [sb(f"PB{i}", [P, 8 * PW]) for i in range(2)]
        H1 = sb("H1", [P, HALF])
        HU = sb("HU", [P, HALF])
        HS = sb("HS", [P, TT])
        MT = sb("MT", [P, HALF])
        S = sb("S", [P, NCH, TT])
        TS = sb("TS", [P, NCH, TT])
        OT = [sb(f"OT{i}", [TP, 2, 2, C]) for i in range(2)]
        XS = sb("XS", [SEQ, NB, C])
        XNt = sb("XNt", [SEQ, NB, C])
        TC_ = sb("TC_", [SEQ, NB, C])
        TSQ = sb("TSQ", [SEQ, NB, C])
        st1 = sb("st1", [SEQ, NB])
        st2 = sb("st2", [SEQ, NB])
        strs = sb("strs", [SEQ, NB])
        lnw = sb("lnw", [SEQ, 4, C])
        fb2r = sb("fb2r", [SEQ, C])
        tw1s = sb("tw1s", [C, FF])
        tw2s = sb("tw2s", [P, 2, C])
        tb1s = sb("tb1s", [P, 2])
        XB = [sb(f"XB{i}", [SEQ, C]) for i in range(4)]
        XT = sb("XT", [C, SEQ])
        KX = sb("KX", [C, HEADS, SEQ])
        SB_ = sb("SB_", [SEQ, 2, HALFS])
        mx = sb("mx", [SEQ, HEADS])
        PR = sb("PR", [SEQ, 2, HALFS])
        PT = sb("PT", [SEQ, 2, HALFS])
        AO = sb("AO", [SEQ, HEADS, HD])
        X2T = sb("X2T", [C, NB * SEQ])
        GH = sb("GH", [P, 2, NB * SEQ])
        toki = sb("toki", [16, NB * SEQ], I32)
        tokf = sb("tokf", [16, NB * SEQ])
        vocab = sb("vocab", [P, 8])
        posi = sb("posi", [P, SEQ], I32)
        posf = sb("posf", [P, SEQ])
        poh = sb("poh", [P, 8, SEQ])
        tabs = sb("tabs", [P, 8, C])
        embs = sb("embs", [16, C])
        iws = sb("iws", [SEQ, 2])
        posw = sb("posw", [SEQ, C])

        mix_scope.close()
        ctx = outer

        X = [sb(f"X{i}", [CP, CH, C]) for i in range(2)]
        XC = sb("XC", [CP, CH, C])
        SQ = sb("SQ", [CP, CH, C])
        XN = sb("XN", [CP, CH, 2, C])
        XR = [sb(f"XR{i}", [CP, CH, C]) for i in range(2)]
        Y = sb("Y", [CP, CH, CX])
        SQ2 = SQ
        XF = sb("XF", [CP, CH, C])
        ROW = [sb(f"ROW{i}", [CP, CH, RW]) for i in range(2)]
        QT = [sb(f"QT{i}", [P, N]) for i in range(2)]
        fs = sb("fs", [CP, CH])
        ms = sb("ms", [CP, CH])
        vv = sb("vv", [CP, 2 * CH])
        rr = sb("rr", [CP, 2 * CH])
        vv2 = sb("vv2", [CP, CH])
        rr2 = sb("rr2", [CP, CH])
        vv3 = sb("vv3", [CP, CH])
        rr3 = sb("rr3", [CP, CH])
        gs = sb("gs", [CP, 6, CH])
        NK = [sb(f"NK{i}", [P, 1]) for i in range(2)]
        NKP = sb("NKP", [P, 2])
        EM = sb("EM", [P, MEM])
        EMT = [sb(f"EMT{i}", [MEM, P]) for i in range(2)]
        EK = [sb(f"EK{i}", [CP, 2, HID]) for i in range(2)]
        QS = [sb(f"QS{i}", [CP, 2, HID]) for i in range(2)]
        QE = [sb(f"QE{i}", [CP, 2, HID]) for i in range(2)]
        QN = [sb(f"QN{i}", [CP, 2, HID]) for i in range(2)]
        qm = sb("qm", [CP, 2, AH])
        qsum = sb("qsum", [CP, 2, AH])
        rq = sb("rq", [CP, 2, AH])
        rden = sb("rden", [P, 1])
        CN = sb("CN", [P, P])
        CT = sb("CT", [P, P])
        MM = sb("MM", [P, CX])
        XG = [sb(f"XG{i}", [CP, CH, E]) for i in range(2)]
        FX = [sb(f"FX{i}", [CP, CH]) for i in range(2)]
        LG = sb("LG", [CP, CH, E])
        D = sb("D", [CP, CH, E])
        EX = sb("EX", [CP, CH, E])
        CAND = sb("CAND", [CP, CH, E])
        OH = sb("OH", [CP, E, CH])
        SC = sb("SC", [CP, E, CH])
        PX = sb("PX", [CP, E, CH])
        RT = sb("RT", [CP, E])
        SLOT = [sb(f"SLOT{i}", [CP, CH], I32) for i in range(2)]

        R = [sb(f"R{i}", [SP_, 4, RW]) for i in range(4)]
        RX = [sb(f"RX{i}", [SP_, 4, 2, C]) for i in range(2)]
        XE = [sb(f"XE{i}", [P, ST]) for i in range(2)]
        HE = [sb(f"HE{i}", [P, 2, ST]) for i in range(2)]
        YE, GE_, FM, CE, EQ = (QT[0][0:SP_, n * 4 * C:(n + 1) * 4 * C].rearrange("p (j c) -> p j c", c=C)
                               for n in range(5))
        OE = [sb(f"OE{i}", [SP_, 4, C]) for i in range(4)]
        t0 = sb("t0", [SP_, 4])
        t1 = sb("t1", [SP_, 4])
        IDX = [sb(f"IDX{i}", [SP_, 4], I32) for i in range(4)]
        W1E = [sb(f"W1E{i}", [P, FF]) for i in range(2)]
        W1H = [sb(f"W1H{i}", [P, FF]) for i in range(2)]
        W1L = [sb(f"W1L{i}", [P, FF]) for i in range(2)]
        W2E = [sb(f"W2E{i}", [P, 2, C]) for i in range(2)]
        B1E = [sb(f"B1E{i}", [P, 2]) for i in range(2)]
        B2E = [sb(f"B2E{i}", [SP_, C]) for i in range(2)]

        names = """consts zeroed vinit dinit
            pa_in0 pa_in1 conv_done relu_done gate_mm tanh_done prod_done mix_mm mix_out h_up h_hi h_lo w2d mt_done mt_tr st0 st1 h_text
            ln_xc ln_sq ln_var ln_pow ln_out lnd v9_done t_done kx_done xt_done sc_done soft_sub exp_done
            ptr_done pt_done pv_done ao_done aod softd ffw x2_tr x2_cp f1_mm gelu_done f2_mm f2_add
            emb_oh emb_mm embd wts xb_done passed_pe passed_dve passed_pool
            x_in0 x_in1 f_xc f_sq f_var f_pow f_xn f_xin f_xr fd f_tr f_trc f_km f_kmx f_nk f_nkr f_wrow f_em f_emt f_emc f_fx g_mm g_cp wqd q_g f_xs p_lx
            q_mm q_ek q_v q_sub q_exp q_rq q_n q_tr q_trc q_gd q_ctx
            p_cn p_ct p_ctc p_m p_mc p_y p_yb p_sq p_ss p_pow p_yn p_yx p_h2 p_c2 p_c2s p_v3 p_pw3 
            p_lg p_d p_ex p_rt p_tri p_slot p_yg p_s3 p_es p_t2 p1 p2 o_st s_sc0 s_sc1 crd
            e_in0 e_in1 e_in2 e_in3 e_x e_xt e_xc e_h e_hm e_yb e_wu e_wp e_xu e_xp e_y e_o ed e_w0 e_w1 e_s0 e_s1 e_s2 e_s3""".split()
        z = {n: sem(n) for n in names}
        block = ctx.enter_context(nc.Block())

        pa_in = [z["pa_in0"], z["pa_in1"]]
        stored = [z["st0"], z["st1"]]
        x_in = [z["x_in0"], z["x_in1"]]
        scat = [z["s_sc0"], z["s_sc1"]]
        e_w = [z["e_w0"], z["e_w1"]]
        e_in = [z[f"e_in{i}"] for i in range(4)]
        e_sc = [z[f"e_s{i}"] for i in range(4)]

        consts = [(ident[:], ident_d), (w1c[:], tw1), (w2c[:], tw2), (w3c[:], tw3), (b1c[:], tb1), (b2c[:], tb2), (b3c[:], tb3),
                  (bias_t[:], bias_d), (hmask[:], hmask_d), (vocab[:], vocab_d), (toki[:], x_txt), (posi[:], pos_ids),
                  (tabs[:], table_d), (embs[:], emb), (iws[:, 0:1], iw), (iws[:, 1:2], pw), (gpre_s[:], gpre),
                  (WQ[:], wqkv), (memk_s[:], memk), (VM[:], memv), (wout_s[:, 0:C], wout), (bout_s[:, 0:C], bout),
                  (gateb[:], gateb_d), (centre[:], centre_d), (boutT_s[:], boutT), (goutc_s[:], goutc),
                  (gout_s[:], gout), (gate_s[:], gate), (BD[:], bd_d), (TRI[:], tri_d), (KEEP[:], keep_d), (DESC[:], desc_d),
                  (TKN[:], tokn_d), (lnw[:, 2, :], ln1w[0]), (lnw[:, 3, :], ln1b[0])]
        ALL_CONSTS = 16 * len(consts)

        UPPER = -4096

        def parts(ap):
            return ap.bitcast(mybir.dt.float32r)

        class Chain:

            def __init__(self, eng, s, base):
                self.eng, self.s, self.base, self.n = eng, s, base, 0

            def after(self, ins, own=False):
                self.n += 1
                ins.then_inc(self.s, 1)
                self.eng.wait_ge(self.s, self.base + self.n)
                if own:
                    self.eng.sem_inc(z["passed_dve"], 1)

        LN_STEPS, AO_STEPS, SOFT_STEPS = 5, 2, 2

        def tile_place(l, n):
            return (n, l) if n < NB else (4 + 2 * l + n - NB, GROUPS - 1)

        TA, TB, T2, CTX = 4, 5, 6, 7
        NG = -(-CH // 2)

        def chunks(g):
            return range(2 * g, min(2 * g + 2, CH))

        def all_batches(eng, batch, halves=False):
            def kw(h):
                return dict(h=h) if halves else {}

            batch(-1, 1, grp=False, post1=False, post2=False, **kw(-1))
            batch(0, 0, post1=False, post2=False, **kw(0))
            batch(1, 1, post2=False, **kw(0))
            with eng.Fori(0, NB // 2 - 2) as k:
                for par in range(2):
                    batch(2 * k + 2 + par, par, **kw(k + 1))
            batch(NB - 2, 0, **kw(NB // 2 - 1))
            batch(NB - 1, 1, pre=False, **kw(NB // 2 - 1))
            batch(NB, 0, grp=False, pre=False, **kw(NB // 2))
            batch(NB + 1, 1, grp=False, pre=False, post1=False, **kw(NB // 2))

        def all_tiles(eng, slot):
            def expert(e, ep, h):
                for q in range(4):
                    slot(e * TILES_E + q, q, ep, h, new=True)
                with eng.Fori(1, TILES_E // 4) as k:
                    for q in range(4):
                        slot(e * TILES_E + k * 4 + q, q, ep, h)

            expert(0, 0, 0)
            expert(1, 1, 0)
            with eng.Fori(1, E // 2) as h:
                for ep in range(2):
                    expert(2 * h + ep, ep, h)
            for q in range(2):
                slot(E * TILES_E + q, q, 0, E // 2, new=True, live=False)

        def rounds_of(t, q):
            return 4 * (t - q) + 16

        def exists(t, n):
            return not isinstance(t, int) or t >= n

        @block.sync
        def _(sp):
            for dst, src in consts:
                sp.dma_start(dst, src).then_inc(z["consts"], 16)

            def load_tile(par, b, g):
                for half in range(2):
                    rows = slice(C * half, C * half + C)
                    sp.dma_start(PA[par][rows, :], x_pad[b, :, bass.ds(g * (ROWS * PW) + half, 10 * PW)]
                                 ).then_inc(pa_in[par], 16)
                    sp.dma_start(PB[par][rows, :], x_pad[b, :, bass.ds(g * (ROWS * PW) + 2 + half * PW, 8 * PW)]
                                 ).then_inc(pa_in[par], 16)

            def store_tile(i, par, b, g):
                sp.wait_ge(z["mix_out"], i + 1)
                sp.dma_start(h_f[bass.ds(b * (N * C) + g * (TT * C), TT * C)].rearrange("(a p f) -> p a f", a=2, p=TP),
                             OT[par][:, :, :, :].rearrange("p a r c -> p a (r c)")).then_inc(stored[par], 16)

            load_tile(0, 0, 0)
            load_tile(1, 1, 0)
            sp.wait_ge(z["zeroed"], 1)
            for k in range(SLOTS * RW // (P * 1071)):
                sp.dma_start(slots_f[k * P * 1071:(k + 1) * P * 1071].rearrange("(p r f) -> p r f", p=P, r=3),
                             zeros[:, :].unsqueeze(1).to_broadcast([P, 3, 357])).then_inc(z["wts"], 16)
            with sp.Fori(0, LAYERS) as l:
                for n in range(PER_LAYER):
                    i = l * PER_LAYER + n
                    if n == 0:
                        sp.wait_ge(z["f2_add"], l * 4 + 1)
                        sp.wait_ge(z["ln_out"], 2 * l + 1)
                        sp.dma_start(tw1s[:, :], fw1[l]).then_inc(z["ffw"], 16)
                        sp.dma_start(tw2s[:, :, :], fw2[l]).then_inc(z["ffw"], 16)
                        sp.dma_start(tb1s[:, :], fb1[l]).then_inc(z["ffw"], 16)
                        sp.dma_start(fb2r[:, :], fb2[l]).then_inc(z["ffw"], 16)
                        sp.dma_start(lnw[:, 0, :], ln2w[l]).then_inc(z["ffw"], 16)
                        sp.dma_start(lnw[:, 1, :], ln2b[l]).then_inc(z["ffw"], 16)
                        sp.dma_start(lnw[:, 2, :], ln1w[l + 1]).then_inc(z["ffw"], 16)
                        sp.dma_start(lnw[:, 3, :], ln1b[l + 1]).then_inc(z["ffw"], 16)
                    sp.wait_ge(z["prod_done"], NCH * i + NCH)
                    b, g = tile_place(l, n + 2) if n + 2 < PER_LAYER else tile_place(l + 1, n + 2 - PER_LAYER)
                    load_tile(n % 2, b, g)
                    b, g = tile_place(l, n)
                    store_tile(i, n % 2, b, g)
            for n in range(4):
                i = LAYERS * PER_LAYER + n
                if n < 2:
                    sp.wait_ge(z["prod_done"], NCH * i + NCH)
                    load_tile(n % 2, n + 2, GROUPS - 1)
                store_tile(i, n % 2, n, GROUPS - 1)
            sp.wait_ge(z["ln_out"], 2 * LAYERS + 1)
            sp.dma_start(h_d.rearrange("(b n) c -> n b c", b=NB)[IMG:N, :, :], XNt[:, :, :]).then_inc(z["h_text"], 16)

            for par in range(2):
                sp.wait_ge(stored[par], 16 * (56 + 1))
            sp.wait_ge(z["h_text"], 16)

            def load_x(b, par):
                sp.dma_start(X[par][:, :, :].rearrange("p j c -> p (j c)"),
                             h_f[bass.ds(b * (N * C), N * C)].rearrange("(p f) -> p f", p=CP)).then_inc(x_in[par], 16)

            def store_h(b, par):
                sp.wait_ge(z["p_h2"], b + 1)
                sp.dma_start(out_f[bass.ds(b * (N * C), N * C)].rearrange("(p j c) -> p j c", p=CP, j=CH),
                             ROW[par][:, :, 0:C]).then_inc(z["o_st"], 16)

            load_x(0, 0)
            load_x(1, 1)

            with sp.Fori(0, NB // 2 - 1) as k:
                for par in range(2):
                    sp.wait_ge(z["f_xr"], 2 * k + par + 1)
                    load_x(2 * k + par + 2, par)
                    store_h(2 * k + par, par)
            for b in (NB - 2, NB - 1):
                store_h(b, b % 2)

            def load_w(e, par):
                sp.dma_start(W1E[par][:, :], ew1[e]).then_inc(e_w[par], 16)
                sp.dma_start(W2E[par][:, :, :], ew2[e]).then_inc(e_w[par], 16)
                sp.dma_start(B1E[par][:, :], eb1[e]).then_inc(e_w[par], 16)
                sp.dma_start(B2E[par][:, :], eb2[e]).then_inc(e_w[par], 16)

            def load_r(t, q):
                sp.dma_start(R[q][:, :, :].rearrange("p j c -> p (j c)"),
                             slots_f[bass.ds(t * (ST * RW), ST * RW)].rearrange("(p f) -> p f", p=SP_)
                             ).then_inc(e_in[q], 16)

            load_w(0, 0)
            load_w(1, 1)
            for par in range(2):
                sp.wait_ge(scat[par], 16 * CH * (NB // 2) + 16)
            for q in range(4):
                load_r(q, q)
            tiles = E * TILES_E
            with sp.Fori(0, E // 2 - 1) as e2:
                for ep in range(2):
                    e = 2 * e2 + ep
                    with sp.Fori(0, TILES_E // 4) as k:
                        for q in range(4):
                            t = e * TILES_E + k * 4 + q
                            sp.wait_ge(z["e_o"], t + 1)
                            load_r(t + 4, q)
                    load_w(e + 2, ep)
            tail = (E - 2) * TILES_E
            with sp.Fori(0, 2 * TILES_E // 4 - 1) as k:
                for q in range(4):
                    sp.wait_ge(z["e_o"], tail + k * 4 + q + 1)
                    load_r(tail + k * 4 + q + 4, q)
            for q in range(4):
                sp.wait_ge(e_sc[q], 64 * (tiles // 4) + 16)
            sp.wait_ge(z["o_st"], 16 * NB + 16)

        @block.tensor
        def _(pe):
            def wait_first(s, value):
                pe.wait_ge(s, value)
                pe.sem_inc(z["passed_pe"], 1)

            def mm(o, w, r, start=True, stop=True):
                return nc.tensor.matmul(o, w, r, start=start, stop=stop)

            def views(par, half, c):
                pa = PA[par][:, :].rearrange("p (r w) -> p r w", w=PW)
                pb = PB[par][:, :].rearrange("p (r w) -> p r w", w=PW)
                r0 = 4 * half
                if c < 3:
                    return pa[:, c + r0:c + r0 + 4, 0:HW]
                if c == 3:
                    return pb[:, r0:r0 + 4, 0:HW]
                return pa[0:C, 2 + r0:6 + r0, 2:2 + HW]

            def conv(i, par, rounds):
                pe.wait_ge(pa_in[par], 64 * rounds)
                for c in range(NCH):
                    k = C if c == NCH - 1 else P
                    for half in range(2):
                        last = mm(PS[C * half:C * half + C, 0, 0:HALF], w1c[0:k, c, :], views(par, half, c),
                                  start=(c == 0), stop=(c == NCH - 1))
                last.then_inc(z["conv_done"], 1)

            def hidden(i):
                pe.wait_ge(z["h_hi"], i + 1)
                pe.wait_ge(z["h_lo"], i + 1)

            def gates(i, c0=0, c1=NCH):
                for c in range(c0, c1):
                    if c >= 3:
                        pe.wait_ge(z["tanh_done"], NCH * i + c - 2)
                    m = C if c == NCH - 1 else P
                    for n, w in enumerate((w2h, w2l)):
                        last = mm(PS[0:m, 1 + c % 3, 0:TT], parts(w[:, c, 0:m]), parts(HS[:, :]), start=(n == 0),
                                  stop=(n == 1))
                    last.then_inc(z["gate_mm"], 1)

            def mix(i):
                for c in range(NCH):
                    k = C if c == NCH - 1 else P
                    wait_first(z["prod_done"], NCH * i + c + 1)
                    for half in range(2):
                        last = mm(PS[C * half:C * half + C, 5, 0:HALF], w3c[0:k, c, :],
                                  TS[0:k, c, HALF * half:HALF * half + HALF], start=(c == 0), stop=(c == NCH - 1))
                last.then_inc(z["mix_mm"], 1)

            def turn_out(i):
                wait_first(z["mt_done"], i + 1)
                for r in range(2):
                    last = nc.tensor.transpose(PS[0:TP, 4, P * r:P * r + P], MT[:, r::2], ident[:, :])
                last.then_inc(z["mt_tr"], 1)

            def text_turn(j, q):
                wait_first(z["v9_done"], j + 1)
                nc.tensor.transpose(PS[0:C, 0, 256:256 + SEQ], XB[q][:, :], ident[0:SEQ, 0:SEQ]
                                    ).then_inc(z["t_done"], 1)

            def text_scores(j):
                pe.wait_ge(z["kx_done"], j + 1)
                pe.wait_ge(z["ao_done"], j + 1)
                for s in range(2):
                    last = mm(PS[0:SEQ, 6 + s, 0:HALFS], XT[:, :], KX[:, 4 * s:4 * s + 4, :])
                last.then_inc(z["sc_done"], 1)

            def text_probs_turn(j):
                pe.wait_ge(z["exp_done"], j + 1)
                for h in range(HEADS):
                    s, o = h // 4, h % 4 * SEQ
                    last = nc.tensor.transpose(PS[0:SEQ, 6 + s, o:o + SEQ], PR[:, s, o:o + SEQ], ident[0:SEQ, 0:SEQ])
                last.then_inc(z["ptr_done"], 1)

            def text_values(j, q):
                pe.wait_ge(z["pt_done"], j + 1)
                for h in range(HEADS):
                    s, o = h // 4, h % 4 * SEQ
                    last = mm(PS[0:SEQ, 6, 384 + 9 * h:393 + 9 * h], PT[:, s, o:o + SEQ], V9[q][:, h, :])
                last.then_inc(z["pv_done"], 1)

            pe.wait_ge(z["consts"], ALL_CONSTS)
            pe.wait_ge(z["emb_oh"], 1)
            for c in range(8):
                last = mm(PS[0:SEQ, 0, 0:C], poh[:, c, :], tabs[:, c, :], start=(c == 0), stop=(c == 7))
            for b in range(NB):
                last = mm(PS[0:SEQ, 1 + b // 8, C * (b % 8):C * (b % 8) + C], tokf[:, SEQ * b:SEQ * b + SEQ], embs[:, :])
            last.then_inc(z["emb_mm"], 1)
            pe.wait_ge(z["embd"], 4)

            pe.wait_ge(z["w2d"], 3)
            conv(0, 0, 1)
            with pe.Fori(0, LAYERS) as l:
                with pe.Fori(0, NB // 4) as k:
                    for q in range(4):
                        i = l * PER_LAYER + k * 4 + q
                        j = l * NB + k * 4 + q
                        hidden(i)
                        text_turn(j, q)
                        gates(i, 0, 3)
                        if q:
                            text_values(j - 1, q - 1)
                            turn_out(i - 1)
                        gates(i, 3, NCH)
                        text_scores(j)
                        conv(i + 1, (q + 1) % 2, l * 9 + k * 2 + (q + 1) // 2 + 1)
                        mix(i)
                        text_probs_turn(j)
                        if q == 3:
                            text_values(j, q)
                            turn_out(i)
                for u in range(2):
                    i = l * PER_LAYER + NB + u
                    hidden(i)
                    gates(i)
                    conv(i + 1, 1 - u, l * 9 + 9 + u)
                    mix(i)
                    turn_out(i)
                pe.wait_ge(z["ffw"], 128 * l + 128)
                wait_first(z["ln_out"], 2 * l + 2)
                for n in range(4):
                    if n >= 2:
                        wait_first(z["x2_cp"], l * 4 + n - 1)
                    for m in range(4):
                        last = nc.tensor.transpose(PS[0:C, 6 + n % 2, SEQ * m:SEQ * m + SEQ], XNt[:, 4 * n + m, :],
                                                   ident[0:SEQ, 0:SEQ])
                    last.then_inc(z["x2_tr"], 1)
                for n in range(4):
                    pe.wait_ge(z["x2_cp"], l * 4 + max(n, 0) + 1)
                    for f in range(2):
                        i8 = 2 * n + f
                        if n == 0:
                            pe.wait_ge(z["x2_cp"], l * 4 + 4)
                        else:
                            pe.wait_ge(z["gelu_done"], l * 8 + i8 - 1)
                        mm(PS[:, 6 + f, 0:HALFS], tw1s[:, P * f:P * f + P], X2T[:, HALFS * n:HALFS * n + HALFS]
                           ).then_inc(z["f1_mm"], 1)
                for n in range(4):
                    pe.wait_ge(z["gelu_done"], l * 8 + 2 * n + 2)
                    if n:
                        pe.wait_ge(z["f2_add"], l * 4 + n + 1)
                    else:
                        pe.wait_ge(z["mix_out"], l * PER_LAYER + PER_LAYER)
                    for m in range(4):
                        for f in range(2):
                            o = SEQ * (4 * n + m)
                            last = mm(PS[0:SEQ, 5, 256 + C * m:256 + C * m + C], GH[:, f, o:o + SEQ], tw2s[:, f, :],
                                      start=(f == 0), stop=(f == 1))
                    last.then_inc(z["f2_mm"], 1)
            for n in range(4):
                i = LAYERS * PER_LAYER + n
                hidden(i)
                gates(i)
                if n < 3:
                    conv(i + 1, (n + 1) % 2, LAYERS * 9 + (n + 1) // 2 + 1)
                mix(i)
                turn_out(i)

            pe.wait_ge(z["mix_out"], LAYERS * PER_LAYER + 4)

            mm(PS[:, TA, 0:E], centre[:, :], gate_s[:, :])
            nc.tensor.transpose(PS[0:C, TB, 0:P], wout_s[:, 0:C], ident[:, :]).then_inc(z["g_mm"], 1)
            pe.wait_ge(z["g_cp"], 1)
            mm(PS[:, TA, 0:E], WOT[:, :], GO[:, :])
            mm(PS[0:CP, TB, 0:E], boutT_s[:, :], GO[:, :]).then_inc(z["g_mm"], 1)
            pe.wait_ge(z["g_cp"], 2)

            def turn_x(g):
                for j in range(4 * g, min(4 * g + 4, CH)):
                    last = nc.tensor.transpose(PS[:, TA, CP * (j - 4 * g):CP * (j - 4 * g) + CP],
                                               XN[:, j, :, :].rearrange("p a c -> p (a c)"), ident[0:CP, 0:CP])
                last.then_inc(z["f_tr"], 1)

            def project(b, par, g):
                G = NG * b + g
                if g >= 2:
                    pe.wait_ge(z["q_v"], G - 1)
                    pe.wait_ge(z["q_sub"], G - 1)
                n = len(chunks(g))
                mm(PS[0:CP, 2 + g % 2, 0:2 * HID * n].rearrange("p (n c) -> p n c", n=n),
                   parts(ONER[:, :]), parts(NKR[par][:, :]).unsqueeze(1).to_broadcast([P, n, 2 * HID]), stop=False)
                for j in chunks(g):
                    x, s = parts(XNT[par][:, CP * j:CP * j + CP]), j % 2
                    for n, w in enumerate((WH, WL)):
                        mm(PS[0:CP, g % 2, QW * s:QW * s + QW], x, parts(w[:, 0:QW]), start=(n == 0), stop=(n == 1))
                        last = mm(PS[0:CP, 2 + g % 2, 2 * HID * s:2 * HID * s + 2 * HID], x,
                                  parts(w[:, QW:QW + 2 * HID]), start=False, stop=(n == 1 and j == chunks(g)[-1]))
                last.then_inc(z["q_mm"], 1)

            def context(b, g):
                G = NG * b + g
                pe.wait_ge(z["q_ek"], G + 1)
                pe.wait_ge(z["q_v"], G + 1)
                for j in chunks(g):
                    last = mm(PS[:, CTX, 0:HID + 1], EK[g % 2][:, j % 2, :], V[g % 2][:, j % 2, :],
                              start=False, stop=(j == CH - 1))
                last.then_inc(z["q_ctx"], 1)

            def turn_q(b, g):
                G = NG * b + g
                if not (isinstance(G, int) and G == 0):
                    pe.wait_ge(z["q_trc"], G)
                wait_first(z["q_n"], G + 1)
                for j in chunks(g):
                    o = CP * (j % 2)
                    last = nc.tensor.transpose(PS[:, T2, o:o + CP], QN[g % 2][:, j % 2, :], ident[0:CP, 0:CP])
                last.then_inc(z["q_tr"], 1)

            def batch(b, par, grp=True, pre=True, post1=True, post2=True):
                if grp:
                    project(b, par, 0)
                for g in range(NG):
                    if grp and g + 1 < NG:
                        project(b, par, g + 1)
                    if post1 and g == 0:
                        wait_first(z["p_cn"], b)
                        nc.tensor.transpose(PS[:, TA, 0:P], CN[:, :], ident[:, :]).then_inc(z["p_ct"], 1)
                    if grp and g == 0:
                        mm(PS[:, CTX, 0:HID + 1], EMT[par][:, :], VM[:, :], start=True, stop=False)
                    if post1 and 1 <= g < 5:
                        if g == 1:
                            pe.wait_ge(z["p_mc"], b)
                        else:
                            pe.wait_ge(z["p_yb"], 4 * b + g - 5)
                        for j in range(YP * g - YP, min(YP * g, CH)):
                            last = mm(PS[0:CP, TA, CX * (j % YP):CX * (j % YP) + CX],
                                      QT[1 - par][:, CP * j:CP * j + CP], MM[:, :])
                        last.then_inc(z["p_y"], 1)
                    if pre and 6 <= g < 13:
                        if g == 6:
                            if post1:
                                pe.wait_ge(z["p_yb"], 4 * b)
                            wait_first(z["f_xn"], b + 2)
                        else:
                            wait_first(z["f_trc"], 7 * b + g + 1)
                        turn_x(g - 6)
                    if grp:
                        context(b, g)
                    if grp and g >= 2:
                        turn_q(b, g - 2)
                    if post1 and g == 0:
                        pe.wait_ge(z["p_ctc"], b)
                        mm(PS[:, TA, 0:CX], CT[:, :], wout_s[:, :]).then_inc(z["p_m"], 1)
                    if post2 and g == 2:
                        pe.wait_ge(z["p_rt"], b - 1)
                        mm(PS[0:CP, TB, 0:E], TRI[:, :], RT[:, :], start=True, stop=False)
                        mm(PS[0:CP, TB, 0:E], ONES[0:CP, :], CR[:, :], start=False, stop=True).then_inc(z["p_tri"], 1)
                    if pre and g >= 7:
                        n = g - 7
                        if n:
                            pe.wait_ge(z["f_kmx"], 7 * b + 7 + n)
                        elif post2:
                            pe.wait_ge(z["p_slot"], b - 1)
                        pe.wait_ge(z["f_trc"], 7 * b + 8 + n)
                        o = min(KW * n, N - KW)
                        x = parts(XNT[1 - par][:, o:o + KW])
                        mm(PS[:, TB, 0:KW], parts(WH[:, QW:QW + HID]), x, stop=False)
                        mm(PS[:, TB, 0:KW], parts(WL[:, QW:QW + HID]), x, start=False).then_inc(z["f_km"], 1)
                if pre:
                    pe.wait_ge(z["f_nk"], b + 2)
                    mm(PS[0:2, TA, 0:P], NKP[:, :], ident[:, :]).then_inc(z["f_nkr"], 1)
                if grp:
                    turn_q(b, NG - 2)
                if pre:
                    wait_first(z["f_em"], b + 2)
                    nc.tensor.transpose(PS[0:MEM, TB, 0:P], EM[:, :], ident[:, :]).then_inc(z["f_emt"], 1)
                if grp:
                    turn_q(b, NG - 1)
                if pre:
                    pe.wait_ge(z["f_wrow"], b + 2)
                    pe.wait_ge(z["f_emc"], b + 2)

            all_batches(pe, batch)

            def slot(t, q, ep, h, new=False, live=True):
                if exists(t, 2):
                    w = 1 - ep if new and q < 2 else ep
                    pe.wait_ge(z["e_h"], t - 1)
                    if exists(t, 4):
                        pe.wait_ge(z["e_yb"], t - 3)
                    for k4 in range(4):
                        for f in range(2):
                            last = mm(PS[0:SP_, 6 + q % 2, C * k4:C * k4 + C],
                                      HE[q % 2][:, f, SP_ * k4:SP_ * k4 + SP_], W2E[w][:, f, :],
                                      start=(f == 0), stop=(f == 1))
                    last.then_inc(z["e_y"], 1)
                if exists(t, 1) and (live or q < 1):
                    w = 1 - ep if new and q < 1 else ep
                    if new and q == 1:
                        pe.wait_ge(e_w[ep], 64 * h + 64)
                        pe.wait_ge(z["e_wp"], 2 * h + ep + 1)
                    pe.wait_ge(z["e_xc"], t)
                    for f in range(2):
                        for n, w1 in enumerate((W1H, W1L)):
                            last = mm(PS[:, 2 + 2 * (1 - q % 2) + f, 0:ST], parts(w1[w][:, P * f:P * f + P]),
                                      parts(XE[1 - q % 2][:, :]), start=(n == 0), stop=(n == 1))
                    last.then_inc(z["e_hm"], 1)
                if live:
                    wait_first(z["e_xp"], t + 1)
                    for k4 in range(4):
                        last = nc.tensor.transpose(PS[:, q % 2, SP_ * k4:SP_ * k4 + SP_],
                                                   RX[q % 2][:, k4, :, :].rearrange("p a c -> p (a c)"),
                                                   ident[0:SP_, 0:SP_])
                    last.then_inc(z["e_xt"], 1)

            all_tiles(pe, slot)

        @block.scalar
        def _(act):
            def fn(o, i, f, **kw):
                return nc.scalar.activation(o, i, f, **kw)

            def relu(i):
                act.wait_ge(z["conv_done"], i + 1)
                fn(H1[:, :], PS[:, 0, 0:HALF], ACT.Relu, bias=b1c[:, 0:1]).then_inc(z["relu_done"], 1)

            def tanhs(i):
                for c in range(NCH):
                    act.wait_ge(z["gate_mm"], NCH * i + c + 1)
                    m = C if c == NCH - 1 else P
                    fn(S[0:m, c, :], PS[0:m, 1 + c % 3, 0:TT], ACT.Tanh, bias=b2c[0:m, c:c + 1], scale=0.5
                       ).then_inc(z["tanh_done"], 1)

            def upper(i):
                act.wait_ge(z["h_up"], i + 1)
                for half in range(2):
                    last = fn(parts(HS[0:C, HALF * half:HALF * half + HALF]), HU[C * half:C * half + C, :], ACT.Copy)
                last.then_inc(z["h_hi"], 1)

            def add_bias(i):
                act.wait_ge(z["mix_mm"], i + 1)
                fn(MT[:, :], PS[:, 5, 0:HALF], ACT.Identity, bias=b3c[:, 0:1]).then_inc(z["mt_done"], 1)

            def square_ln(n):
                act.wait_ge(z["ln_xc"], n + 1)
                fn(TSQ[:, :, :], TC_[:, :, :], ACT.Square).then_inc(z["ln_sq"], 1)

            act.wait_ge(z["consts"], ALL_CONSTS)
            act.wait_ge(z["dinit"], 1)
            relu(0)
            upper(0)
            square_ln(0)
            with act.Fori(0, LAYERS) as l:
                with act.Fori(0, NB // 4) as k:
                    for q in range(4):
                        i = l * PER_LAYER + k * 4 + q
                        j = l * NB + k * 4 + q
                        act.wait_ge(z["t_done"], j + 1)
                        fn(XT[:, :], PS[0:C, 0, 256:256 + SEQ], ACT.Copy).then_inc(z["xt_done"], 1)
                        tanhs(i)
                        relu(i + 1)
                        act.wait_ge(z["soft_sub"], j + 1)
                        fn(PR[:, :, :], SB_[:, :, :], ACT.Exp).then_inc(z["exp_done"], 1)
                        upper(i + 1)
                        act.wait_ge(z["ptr_done"], j + 1)
                        fn(PT[:, :, :], PS[0:SEQ, 6:8, 0:HALFS], ACT.Copy).then_inc(z["pt_done"], 1)
                        add_bias(i)
                for u in range(2):
                    i = l * PER_LAYER + NB + u
                    tanhs(i)
                    relu(i + 1)
                    if u == 0:
                        square_ln(2 * l + 1)
                    upper(i + 1)
                    add_bias(i)
                for n in range(4):
                    act.wait_ge(z["x2_tr"], l * 4 + n + 1)
                    fn(X2T[:, HALFS * n:HALFS * n + HALFS], PS[0:C, 6 + n % 2, 0:HALFS], ACT.Copy
                       ).then_inc(z["x2_cp"], 1)
                for n in range(4):
                    for f in range(2):
                        act.wait_ge(z["f1_mm"], l * 8 + 2 * n + f + 1)
                        fn(GH[:, f, HALFS * n:HALFS * n + HALFS], PS[:, 6 + f, 0:HALFS], ACT.Gelu,
                           bias=tb1s[:, f:f + 1]).then_inc(z["gelu_done"], 1)
                square_ln(2 * l + 2)
            for n in range(4):
                i = LAYERS * PER_LAYER + n
                tanhs(i)
                if n < 3:
                    relu(i + 1)
                    upper(i + 1)
                add_bias(i)

            def copy_x(b, par, g):
                act.wait_ge(z["f_tr"], 7 * b + g + 1)
                w = CP * min(4, CH - 4 * g)
                fn(parts(XNT[par][:, 4 * CP * g:4 * CP * g + w]), PS[:, TA, 0:w], ACT.Copy).then_inc(z["f_trc"], 1)

            def copy_q(b, par, g):
                act.wait_ge(z["q_tr"], NG * b + g + 1)
                w = CP * len(chunks(g))
                fn(QT[par][:, 2 * CP * g:2 * CP * g + w], PS[:, T2, 0:w], ACT.Copy).then_inc(z["q_trc"], 1)

            def batch(b, par, grp=True, pre=True, post1=True, post2=True):
                for g in range(NG):
                    if grp:
                        G = NG * b + g
                        n = len(chunks(g))
                        kv = PS[0:CP, 2 + g % 2, 0:2 * HID * n].rearrange("p (n c) -> p n c", n=n)
                        act.wait_ge(z["q_mm"], G + 1)
                        if g >= 2:
                            act.wait_ge(z["q_ctx"], G - 1)
                        fn(EK[g % 2][:, 0:n, :], kv[:, :, 0:HID], ACT.Exp).then_inc(z["q_ek"], 1)
                        fn(V[g % 2][:, 0:n, 0:HID], kv[:, :, HID:2 * HID], ACT.Copy).then_inc(z["q_v"], 1)
                        act.wait_ge(z["q_sub"], G + 1)
                        fn(QE[g % 2][:, 0:n, :], QS[g % 2][:, 0:n, :], ACT.Exp).then_inc(z["q_exp"], 1)
                    if pre and 6 <= g < 13:
                        copy_x(b + 1, 1 - par, g - 6)
                    if grp and g >= 2:
                        copy_q(b, par, g - 2)
                    if pre and g == 1:
                        act.wait_ge(z["f_xc"], b + 2)
                        fn(SQ[:, :, :], XC[:, :, :], ACT.Square).then_inc(z["f_sq"], 1)
                    if post1 and g == 5:
                        act.wait_ge(z["p_yb"], 4 * b)
                        fn(SQ2[:, :, :], Y[:, :, 0:C], ACT.Square).then_inc(z["p_sq"], 1)
                    if post2 and g == 1:
                        act.wait_ge(z["p_d"], b - 1)
                        fn(EX[:, :, :], D[:, :, :], ACT.Exp).then_inc(z["p_ex"], 1)
                    if post1 and g == 11:
                        act.wait_ge(z["p_c2"], b)
                        fn(SQ2[:, :, :], XF[:, :, :], ACT.Square).then_inc(z["p_c2s"], 1)
                if grp:
                    copy_q(b, par, NG - 2)
                if pre:
                    act.wait_ge(z["f_nk"], b + 2)
                    fn(EM[:, :], memk_s[:, :], ACT.Exp, bias=NK[1 - par][:, :]).then_inc(z["f_em"], 1)
                    act.wait_ge(z["f_emt"], b + 2)
                    fn(EMT[1 - par][:, :], PS[0:MEM, TB, 0:P], ACT.Copy).then_inc(z["f_emc"], 1)
                if grp:
                    copy_q(b, par, NG - 1)

            all_batches(act, batch)

            def slot(t, q, ep, h, new=False, live=True):
                if live:
                    act.wait_ge(e_in[q], rounds_of(t, q))
                    for k4 in range(4):
                        last = fn(RX[q % 2][:, k4, 1, :], R[q][:, k4, 0:C], ACT.Identity, bias=R[q][:, k4, C:C + 1],
                                  scale=R[q][:, k4, C + 1:C + 2])
                    last.then_inc(z["e_x"], 1)
                if exists(t, 1) and (live or q < 1):
                    w = 1 - ep if new and q < 1 else ep
                    if new and q == 1:
                        act.wait_ge(e_w[ep], 64 * h + 64)
                    act.wait_ge(z["e_hm"], t)
                    for f in range(2):
                        last = fn(HE[1 - q % 2][:, f, :], PS[:, 2 + 2 * (1 - q % 2) + f, 0:ST], ACT.Relu,
                                  bias=B1E[w][:, f:f + 1])
                    last.then_inc(z["e_h"], 1)
                if live:
                    act.wait_ge(z["e_xt"], t + 1)
                    fn(parts(XE[q % 2][:, :]), PS[:, q % 2, 0:ST], ACT.Copy).then_inc(z["e_xc"], 1)

            all_tiles(act, slot)

        @block.gpsimd
        def _(pool):
            gp = nc.gpsimd
            for n, s in enumerate(scat + e_sc):
                pool.dma_start(spare2[0:1, 8 * n:8 * n + 8], vocab_d[0:1, :]).then_inc(s, 16)
            pool.wait_ge(z["zeroed"], 1)

            def ln_power(n):
                pool.wait_ge(z["ln_var"], n + 1)
                gp.tensor_tensor(strs[:, :], st2[:, :], halfneg[0:SEQ, 0:NB], ALU.pow).then_inc(z["ln_pow"], 1)

            ln_power(0)
            with pool.Fori(0, LAYERS) as l:
                with pool.Fori(0, NB // 4) as k:
                    pool.wait_ge(z["ln_out"], 2 * l + 1)
                    for q in range(4):
                        j = l * NB + k * 4 + q
                        pool.wait_ge(z["pv_done"], j + 1)
                        gp.tensor_copy(XB[q][:, :], XNt[:, bass.ds(k * 4 + q, 1), :].rearrange("p o c -> p (o c)"))
                        gp.tensor_copy(V9[q][:, :, 0:HD],
                                       XNt[:, bass.ds(k * 4 + q, 1), :].rearrange("p o (h d) -> p (o h) d", h=HEADS)
                                       ).then_inc(z["v9_done"], 1)
                ln_power(2 * l + 1)
                ln_power(2 * l + 2)

            def scatter(b, par, js):
                for j in js:
                    gp.indirect_dma_start(out=slots_d[:, :],
                                          out_offset=bass.IndirectOffsetOnAxis(ap=SLOT[par][:, j:j + 1], axis=0),
                                          in_=ROW[par][:, j, :], in_offset=None, bounds_check=SLOTS - 1,
                                          oob_is_err=False).then_inc(scat[par], 16)

            def batch(b, par, grp=True, pre=True, post1=True, post2=True):
                if pre:
                    pool.wait_ge(z["f_var"], b + 2)
                    gp.tensor_tensor(rr[:, :], vv[:, :], halfneg[0:CP, :], ALU.pow).then_inc(z["f_pow"], 1)
                if post2:
                    pool.wait_ge(z["p_slot"], b - 1)
                    pool.sem_inc(z["passed_pool"], 1)
                    scatter(b - 2, par, range(0, EARLY))
                if post1:
                    pool.wait_ge(z["p_ss"], b)
                    gp.tensor_tensor(rr2[:, :], vv2[:, :], halfneg[0:CP, 0:CH], ALU.pow).then_inc(z["p_pow"], 1)
                if post2:
                    scatter(b - 2, par, range(EARLY, MOST))
                if post1:
                    pool.wait_ge(z["p_v3"], b)
                    gp.tensor_tensor(rr3[:, :], vv3[:, :], halfneg[0:CP, 0:CH], ALU.pow).then_inc(z["p_pw3"], 1)
                if pre:
                    pool.wait_ge(z["f_pow"], b + 2)
                    if post1:
                        pool.wait_ge(z["p_h2"], b)
                    gp.tensor_tensor(XR[1 - par][:, :, :], XC[:, :, :],
                                     rr[:, 0:CH].unsqueeze(2).to_broadcast([CP, CH, C]), ALU.mult
                                     ).then_inc(z["f_xin"], 1)
                    pool.wait_ge(z["f_xin"], b + 2)
                    gp.tensor_tensor(XR[1 - par][:, :, :], XR[1 - par][:, :, :], X[1 - par][:, :, :], ALU.add
                                     ).then_inc(z["f_xr"], 1)
                if post2:
                    scatter(b - 2, par, range(MOST, CH))

            EARLY, MOST = 5, 23
            pool.wait_ge(z["wts"], 16 * (SLOTS * RW // (P * 1071)))
            all_batches(pool, batch)

            pool.wait_ge(z["o_st"], 16 * NB + 16)
            with pool.Fori(0, E * TILES_E // 4) as k:
                for q in range(4):
                    pool.wait_ge(z["e_o"], k * 4 + q + 1)
                    pool.sem_inc(z["passed_pool"], 1)
                    for k4 in range(4):
                        gp.indirect_dma_start(out=out_rows,
                                              out_offset=bass.IndirectOffsetOnAxis(ap=IDX[q][:, k4:k4 + 1], axis=0),
                                              in_=OE[q][:, k4, :], in_offset=None, bounds_check=TOK - 1,
                                              oob_is_err=False).then_inc(e_sc[q], 16)

        @block.vector
        def _(dve):
            ve = nc.vector

            def bc(ap, shape):
                return ap.to_broadcast(shape)

            LNX = [SEQ, NB, C]

            def layernorm(n, w):
                ch = Chain(dve, z["lnd"], n * LN_STEPS)
                ch.after(ve.reduce_sum(st1[:, :], XS[:, :, :], AX))
                ch.after(ve.tensor_scalar(st1[:, :], st1[:, :], -1.0 / C, None, ALU.mult))
                ve.tensor_tensor(TC_[:, :, :], XS[:, :, :], bc(st1[:, :].unsqueeze(2), LNX), ALU.add
                                 ).then_inc(z["ln_xc"], 1)
                dve.wait_ge(z["ln_sq"], n + 1)
                ch.after(ve.reduce_sum(st2[:, :], TSQ[:, :, :], AX))
                ve.tensor_scalar(st2[:, :], st2[:, :], 1.0 / C, LN_EPS, ALU.mult, ALU.add).then_inc(z["ln_var"], 1)
                dve.wait_ge(z["ln_pow"], n + 1)
                ch.after(ve.tensor_tensor(TC_[:, :, :], TC_[:, :, :], bc(strs[:, :].unsqueeze(2), LNX), ALU.mult))
                ch.after(ve.tensor_tensor(TC_[:, :, :], TC_[:, :, :], bc(lnw[:, w:w + 1, :], LNX), ALU.mult))
                assert ch.n == LN_STEPS
                ve.tensor_tensor(XNt[:, :, :], TC_[:, :, :], bc(lnw[:, w + 1:w + 2, :], LNX), ALU.add
                                 ).then_inc(z["ln_out"], 1)

            def views(par, c):
                pa = PA[par][:, :].rearrange("p (r w) -> p r w", w=PW)
                pb = PB[par][:, :].rearrange("p (r w) -> p r w", w=PW)
                if c < 3:
                    return pa[:, c:c + ROWS, 0:HW]
                if c == 3:
                    return pb[:, 0:ROWS, 0:HW]
                return pa[0:C, 2:2 + ROWS, 2:2 + HW]

            def products(i, par, rounds, c0=0, c1=NCH):
                dve.wait_ge(pa_in[par], 64 * rounds)
                for c in range(c0, c1):
                    m = C if c == NCH - 1 else P
                    dve.wait_ge(z["tanh_done"], NCH * i + c + 1)
                    ve.scalar_tensor_tensor(TS[0:m, c, :].rearrange("p (r w) -> p r w", w=HW),
                                            S[0:m, c, :].rearrange("p (r w) -> p r w", w=HW), 1.0, views(par, c),
                                            op0=ALU.add, op1=ALU.mult).then_inc(z["prod_done"], 1)

            def mix_out(i, par, rounds):
                dve.wait_ge(z["mt_tr"], i + 1)
                dve.wait_ge(stored[par], 16 * rounds)
                ve.tensor_copy(OT[par][:, :, :, :].rearrange("p a r c -> p r a c"),
                               PS[0:TP, 4, 0:2 * P].rearrange("p (r a c) -> p r a c", r=2, a=2)
                               ).then_inc(z["mix_out"], 1)

            def hidden_parts(i):
                dve.wait_ge(z["relu_done"], i + 1)
                ve.tensor_scalar(HU[:, :].bitcast(I32), H1[:, :].bitcast(I32), UPPER, None, ALU.bitwise_and
                                 ).then_inc(z["h_up"], 1)
                dve.wait_ge(z["h_up"], i + 1)
                for half in range(2):
                    rows = slice(C * half, C * half + C)
                    last = ve.tensor_tensor(parts(HS[C:P, HALF * half:HALF * half + HALF]), H1[rows, :], HU[rows, :],
                                            ALU.subtract)
                last.then_inc(z["h_lo"], 1)

            def attend_out(j, b):
                ch = Chain(dve, z["aod"], j * AO_STEPS)
                dve.wait_ge(z["pv_done"], 4 + j + 1)
                o9 = PS[0:SEQ, 6, 384:384 + 9 * HEADS].rearrange("p (h d) -> p h d", h=HEADS)
                ch.after(ve.reciprocal(rs[:, :], o9[:, :, HD]))
                ch.after(ve.tensor_tensor(AO[:, :, :], o9[:, :, 0:HD], bc(rs[:, :].unsqueeze(2), [SEQ, HEADS, HD]),
                                          ALU.mult))
                xs = XS[:, bass.ds(b, 1), :].rearrange("p o c -> p (o c)")
                ve.tensor_tensor(xs, xs, AO[:, :, :].rearrange("p h d -> p (h d)"), ALU.add).then_inc(z["ao_done"], 1)

            def softmax(j):
                ch = Chain(dve, z["softd"], j * SOFT_STEPS)
                dve.wait_ge(z["sc_done"], j + 1)
                ch.after(ve.tensor_tensor(SB_[:, :, :], PS[0:SEQ, 6:8, 0:HALFS], bias_t[:, :, :], ALU.add))
                s3 = SB_[:, :, :].rearrange("p a (h t) -> p (a h) t", h=4)
                ch.after(ve.reduce_max(mx[:, :], s3, AX))
                ve.tensor_tensor(s3, s3, bc(mx[:, :].unsqueeze(2), [SEQ, HEADS, SEQ]), ALU.subtract
                                 ).then_inc(z["soft_sub"], 1)

            ve.memset(halfneg[:, :], -0.5)
            for q in range(4):
                ve.memset(V9[q][:, :, HD:HD + 1], 1.0)
            ve.memset(ONES[:, :], 1.0)
            ve.memset(CR[:, :], 0.0)
            for par in range(2):
                ve.memset(V[par][:, :, HID:HID + 1], 1.0)
            credits = [(stored[0], 16), (stored[1], 16), (z["f2_add"], 1), (z["pv_done"], 4),
                       (z["ao_done"], 1), (z["o_st"], 16)]
            for n, (s, v) in enumerate(credits):
                ve.memset(spare[:, n:n + 1], 0.0).then_inc(s, v)
            ve.memset(zeros[:, :], 0.0).then_inc(z["zeroed"], 1)
            dve.wait_ge(z["consts"], ALL_CONSTS)
            wd = Chain(dve, z["w2d"], 0)
            wd.after(ve.tensor_scalar(w2u[:, :, :].bitcast(I32), w2c[:, :, :].bitcast(I32), UPPER, None,
                                      ALU.bitwise_and))
            ve.tensor_tensor(parts(w2l[:, :, :]), w2c[:, :, :], w2u[:, :, :], ALU.subtract).then_inc(z["w2d"], 1)
            ve.tensor_copy(parts(w2h[:, :, :]), w2u[:, :, :]).then_inc(z["w2d"], 1)
            ini = Chain(dve, z["embd"], 0)
            ve.memset(KM[:, :], 0.0)
            ve.tensor_scalar(w3c[:, :, :], w3c[:, :, :], 0.5, None, ALU.mult)
            ve.tensor_scalar(gout_s[:, :], gout_s[:, :], float(C) ** 0.5, None, ALU.mult)
            ini.after(ve.tensor_scalar(gpre_s[:, :], gpre_s[:, :], float(C) ** 0.5, None, ALU.mult))
            ve.tensor_scalar(WQ[:, :], WQ[:, :], gpre_s[:, 0:1], None, ALU.mult)
            dve.wait_ge(z["zeroed"], 1)
            ve.tensor_copy(parts(ONER[:, :]), ONES[:, :])
            for par in range(2):
                ve.tensor_copy(parts(NKR[par][:, :]), zeros[:, 0:2 * HID])
            ve.tensor_scalar(b2c[:, :], b2c[:, :], 0.5, None, ALU.mult).then_inc(z["dinit"], 1)
            ve.tensor_copy(tokf[:, :], toki[:, :])
            ini.after(ve.tensor_copy(posf[:, :], posi[:, :]))
            for c in range(8):
                ve.tensor_scalar(poh[:, c, :], posf[:, :], vocab[:, c:c + 1], None, ALU.is_equal)
            ve.tensor_scalar(tokf[:, :], tokf[:, :], vocab[0:16, 0:1], None, ALU.is_equal).then_inc(z["emb_oh"], 1)
            dve.wait_ge(z["emb_mm"], 1)
            ini.after(ve.tensor_scalar(posw[:, :], PS[0:SEQ, 0, 0:C], iws[:, 1:2], None, ALU.mult))
            for s in range(2):
                o = ve.scalar_tensor_tensor(XS[:, 8 * s:8 * s + 8, :],
                                            PS[0:SEQ, 1 + s, :].rearrange("p (b c) -> p b c", c=C), iws[:, 0:1],
                                            bc(posw[:, :].unsqueeze(1), [SEQ, 8, C]), op0=ALU.mult, op1=ALU.add)
            ini.after(o)
            hidden_parts(0)
            layernorm(0, 2)
            with dve.Fori(0, LAYERS) as l:
                with dve.Fori(0, NB // 4) as k:
                    for q in range(4):
                        i = l * PER_LAYER + k * 4 + q
                        j = l * NB + k * 4 + q
                        rounds = l * 9 + k * 2 + q // 2 + 1
                        dve.wait_ge(z["xt_done"], j + 1)
                        ve.tensor_tensor(KX[:, :, :], bc(XT[:, :].unsqueeze(1), [C, HEADS, SEQ]),
                                         bc(hmask[:, :].unsqueeze(2), [C, HEADS, SEQ]), ALU.mult
                                         ).then_inc(z["kx_done"], 1)
                        products(i, q % 2, rounds, 0, 2)
                        if q:
                            attend_out(j - 1, k * 4 + q - 1)
                            mix_out(i - 1, (q - 1) % 2, l * 9 + k * 2 + (q - 1) // 2 + 1)
                        products(i, q % 2, rounds, 2, NCH)
                        softmax(j)
                        hidden_parts(i + 1)
                        if q == 3:
                            attend_out(j, k * 4 + q)
                            mix_out(i, q % 2, rounds)
                dve.wait_ge(z["ao_done"], l * NB + NB + 1)
                dve.wait_ge(z["ffw"], 128 * l + 128)
                layernorm(2 * l + 1, 0)
                for u in range(2):
                    i = l * PER_LAYER + NB + u
                    products(i, u, l * 9 + 9)
                    hidden_parts(i + 1)
                    mix_out(i, u, l * 9 + 9)
                for n in range(4):
                    dve.wait_ge(z["f2_mm"], l * 4 + n + 1)
                    xs = XS[:, 4 * n:4 * n + 4, :]
                    ve.tensor_tensor(xs, xs, PS[0:SEQ, 5, 256:512].rearrange("p (m c) -> p m c", m=4), ALU.add
                                     ).then_inc(z["f2_add"], 1)
                dve.wait_ge(z["f2_add"], l * 4 + 4 + 1)
                ve.tensor_tensor(XS[:, :, :], XS[:, :, :], bc(fb2r[:, :].unsqueeze(1), LNX), ALU.add
                                 ).then_inc(z["xb_done"], 1)
                dve.wait_ge(z["xb_done"], l + 1)
                layernorm(2 * l + 2, 2)
            for n in range(4):
                i = LAYERS * PER_LAYER + n
                products(i, n % 2, LAYERS * 9 + n // 2 + 1)
                if n < 3:
                    hidden_parts(i + 1)
                mix_out(i, n % 2, LAYERS * 9 + n // 2 + 1)

            BX = [CP, CH, C]
            BE = [CP, CH, E]
            PRE, QG, POST1, POST2 = 10, 3 * NG, 4, 10
            dve.wait_ge(z["g_mm"], 1)
            ve.tensor_copy(WOT[:, :], PS[0:C, TB, 0:P])
            wq = Chain(dve, z["wqd"], 0)
            wq.after(ve.tensor_copy(WQ[:, HID:QW], PS[:, TA, 0:E]))
            wq.after(ve.tensor_scalar(WU[:, :].bitcast(I32), WQ[:, :].bitcast(I32), UPPER, None, ALU.bitwise_and))
            ve.tensor_tensor(parts(WL[:, :]), WQ[:, :], WU[:, :], ALU.subtract)
            ve.tensor_copy(parts(WH[:, :]), WU[:, :])
            ve.tensor_scalar(GO[:, :], PS[0:C, TA, 0:E], goutc_s[:, 0:1], float(C) ** 0.5, ALU.mult, ALU.mult
                             ).then_inc(z["g_cp"], 1)
            dve.wait_ge(z["g_mm"], 2)
            ve.tensor_copy(wout_s[:, C:CX], PS[:, TA, 0:E])
            ve.tensor_copy(bout_s[:, C:CX], PS[0:CP, TB, 0:E]).then_inc(z["g_cp"], 1)

            mk = Chain(dve, z["crd"], 0)
            mk.after(ve.reduce_max(KM[:, 7:8], memk_s[:, :], AX))

            def heads(t, n):
                return t[:, 0:n, :].rearrange("p n (h d) -> p n h d", h=AH)

            def queries(b, par, g):
                base = QG * b + 3 * g
                if g < NG:
                    n = len(chunks(g))
                    qg = PS[0:CP, g % 2, 0:QW * n].rearrange("p (n c) -> p n c", n=n)
                    q4 = qg[:, :, 0:HID].rearrange("p n (h d) -> p n h d", h=AH)
                    dve.wait_ge(z["q_mm"], NG * b + g + 1)
                    ve.tensor_tensor(XG[par][:, 2 * g:2 * g + n, :], qg[:, :, HID:QW],
                                     bc(FX[par][:, 2 * g:2 * g + n].unsqueeze(2), [CP, n, E]), ALU.mult
                                     ).then_inc(z["q_g"], 1)
                    ve.reduce_max(qm[:, 0:n, :], q4, AX).then_inc(z["q_gd"], 1)
                if g:
                    m = len(chunks(g - 1))
                    o = (g - 1) % 2
                    dve.wait_ge(z["q_exp"], NG * b + g)
                    ve.reduce_sum(qsum[:, 0:m, :], heads(QE[o], m), AX).then_inc(z["q_gd"], 1)
                if g < NG:
                    dve.wait_ge(z["q_gd"], base - 1 if g else base + 1)
                    ve.tensor_tensor(heads(QS[g % 2], n), q4, bc(qm[:, 0:n, :].unsqueeze(3), [CP, n, AH, AD]),
                                     ALU.subtract).then_inc(z["q_sub"], 1)
                if g:
                    last = g == NG
                    dve.wait_ge(z["q_gd"], base - last)
                    ve.reciprocal(rq[:, 0:m, :], qsum[:, 0:m, :]).then_inc(z["q_gd"], 1)
                    dve.wait_ge(z["q_gd"], base - last + 1)
                    if not (isinstance(b, int) and b == 0 and g < 3):
                        dve.wait_ge(z["q_tr"], NG * b + g - 2)
                    ve.tensor_tensor(heads(QN[o], m), heads(QE[o], m), bc(rq[:, 0:m, :].unsqueeze(3), [CP, m, AH, AD]),
                                     ALU.mult).then_inc(z["q_n"], 1)

            def batch(b, par, grp=True, pre=True, post1=True, post2=True, h=0):
                cp, c1, c2 = Chain(dve, z["fd"], (b + 1) * PRE), Chain(dve, z["p1"], (b - 1) * POST1), \
                    Chain(dve, z["p2"], (b - 2) * POST2)
                row1, row2 = ROW[1 - par], ROW[par]
                h2 = row1[:, :, 0:C]
                for g in range(NG):
                    if grp:
                        queries(b, par, g)
                    if pre and g == 0:
                        dve.wait_ge(x_in[1 - par], 16 * (h + par + 1))
                        cp.after(ve.reduce_sum(fs[:, :], X[1 - par][:, :, :], AX))
                        cp.after(ve.tensor_scalar(fs[:, :], fs[:, :], -1.0 / C, None, ALU.mult))
                    if pre and g == 1:
                        if not (isinstance(b, int) and b < 0):
                            dve.wait_ge(z["f_xin"], b + 1)
                        ve.tensor_tensor(XC[:, :, :], X[1 - par][:, :, :], bc(fs[:, :].unsqueeze(2), BX), ALU.add
                                         ).then_inc(z["f_xc"], 1)
                    if pre and g == 2:
                        dve.wait_ge(z["f_sq"], b + 2)
                        cp.after(ve.reduce_sum(vv[:, CH:2 * CH], SQ[:, :, :], AX))
                        cp.after(ve.tensor_scalar(vv[:, 0:CH], vv[:, CH:2 * CH], 1.0 / C, LN_EPS, ALU.mult, ALU.add))
                        ve.scalar_tensor_tensor(vv[:, CH:2 * CH], vv[:, 0:CH], 1e-24, vv[:, CH:2 * CH],
                                                op0=ALU.mult, op1=ALU.max).then_inc(z["f_var"], 1)
                    if pre and g == 5:
                        dve.wait_ge(z["f_pow"], b + 2)
                        if not (isinstance(b, int) and b < 0):
                            dve.wait_ge(z["f_tr"], 7 * b + 7)
                        ve.reciprocal(FX[1 - par][:, :], rr[:, CH:2 * CH]).then_inc(z["f_fx"], 1)
                        cp.after(ve.tensor_tensor(XN[:, :, 1, :], XC[:, :, :], bc(rr[:, CH:2 * CH].unsqueeze(2), BX),
                                                  ALU.mult))
                        cp.after(ve.tensor_scalar(XN[:, :, 0, :].bitcast(I32), XN[:, :, 1, :].bitcast(I32), UPPER,
                                                  None, ALU.bitwise_and))
                        ve.tensor_tensor(XN[:, :, 1, :], XN[:, :, 1, :], XN[:, :, 0, :], ALU.subtract
                                         ).then_inc(z["f_xn"], 1)
                        dve.wait_ge(z["f_fx"], b + 2)
                        cp.after(ve.scalar_tensor_tensor(FX[1 - par][:, :], rr[:, 0:CH], 1.0, FX[1 - par][:, :],
                                                         op0=ALU.add, op1=ALU.mult))
                    if post1 and g == 0:
                        dve.wait_ge(z["q_ctx"], NG * b)
                        c1.after(ve.reciprocal(rden[:, :], PS[:, CTX, HID:HID + 1]))
                        ve.scalar_tensor_tensor(CN[:, :], PS[:, CTX, 0:HID], rden[:, 0:1], BD[:, :], op0=ALU.mult,
                                                op1=ALU.mult).then_inc(z["p_cn"], 1)
                    if post2 and g == 0:
                        dve.wait_ge(z["p_pw3"], b - 1)
                        ve.tensor_tensor(row2[:, :, C], ms[:, :], rr3[:, :], ALU.mult)
                        ve.tensor_copy(row2[:, :, C + 1], rr3[:, :])
                        ve.tensor_copy(row2[:, :, C + 3], TKN[:, :])
                        c2.after(ve.tensor_tensor(LG[:, :, :], LG[:, :, :], bc(rr3[:, :].unsqueeze(2), BE), ALU.mult))
                        ve.tensor_scalar(TKN[:, :], TKN[:, :], float(N), None, ALU.add)
                        ve.tensor_tensor(LG[:, :, :], LG[:, :, :], bc(gateb[:, :].unsqueeze(1), BE), ALU.add
                                         ).then_inc(z["p_lg"], 1)
                    if post1 and g == 0:
                        dve.wait_ge(z["p_ct"], b)
                        ve.tensor_copy(CT[:, :], PS[:, TA, 0:P]).then_inc(z["p_ctc"], 1)
                    if post1 and g == 1:
                        dve.wait_ge(z["p_m"], b)
                        ve.tensor_copy(MM[:, :], PS[:, TA, 0:CX]).then_inc(z["p_mc"], 1)
                    if post1 and 2 <= g < 6:
                        n = min(YP, CH - YP * (g - 2))
                        dve.wait_ge(z["p_y"], 4 * b + g - 5)
                        ve.tensor_tensor(Y[:, YP * (g - 2):YP * (g - 2) + n, :],
                                         PS[0:CP, TA, 0:CX * n].rearrange("p (j c) -> p j c", c=CX),
                                         bc(bout_s[:, :].unsqueeze(1), [CP, n, CX]), ALU.add).then_inc(z["p_yb"], 1)
                    if post1 and g == 6:
                        dve.wait_ge(z["p_sq"], b)
                        c1.after(ve.reduce_sum(vv2[:, :], SQ2[:, :, :], AX))
                        ve.tensor_scalar(vv2[:, :], vv2[:, :], 1e-24, None, ALU.max).then_inc(z["p_ss"], 1)
                    if post1 and g == 7:
                        ve.tensor_tensor(Y[:, :, 0:C], Y[:, :, 0:C], bc(gout_s[:, :].unsqueeze(1), BX), ALU.mult
                                         ).then_inc(z["p_yg"], 1)
                    if post1 and g == 8:
                        dve.wait_ge(z["p_pow"], b)
                        dve.wait_ge(z["p_yg"], b)
                        ve.tensor_tensor(Y[:, :, :], Y[:, :, :], bc(rr2[:, :].unsqueeze(2), [CP, CH, CX]), ALU.mult
                                         ).then_inc(z["p_yn"], 1)
                    if post1 and g == 9:
                        dve.wait_ge(scat[1 - par], (h + par - 1) * (16 * CH) + 16)
                        dve.wait_ge(z["o_st"], b * 16)
                        dve.wait_ge(z["f_xr"], b)
                        dve.wait_ge(z["p_yn"], b)
                        ve.tensor_tensor(h2, Y[:, :, 0:C], XR[1 - par][:, :, :], ALU.add).then_inc(z["p_h2"], 1)
                        dve.wait_ge(z["q_g"], NG * b)
                        ve.tensor_tensor(LG[:, :, :], XG[1 - par][:, :, :], Y[:, :, C:CX], ALU.add
                                         ).then_inc(z["p_lx"], 1)
                    if post1 and g == 10:
                        dve.wait_ge(z["p_h2"], b)
                        c1.after(ve.reduce_sum(ms[:, :], h2, AX))
                        dve.wait_ge(z["p_lx"], b)
                        c1.after(ve.tensor_scalar(ms[:, :], ms[:, :], -1.0 / C, None, ALU.mult))
                    if post1 and g == 11:
                        ve.tensor_tensor(XF[:, :, :], h2, bc(ms[:, :].unsqueeze(2), BX), ALU.add).then_inc(z["p_c2"], 1)
                    if post1 and g == 12:
                        dve.wait_ge(z["p_c2s"], b)
                        dve.wait_ge(z["p_c2"], b)
                        ve.reduce_sum(vv3[:, :], SQ2[:, :, :], AX).then_inc(z["p_s3"], 1)
                        dve.wait_ge(z["p_s3"], b)
                        ve.tensor_scalar(vv3[:, :], vv3[:, :], 1.0 / C, LN_EPS, ALU.mult, ALU.add
                                         ).then_inc(z["p_v3"], 1)
                    if post2 and g == 1:
                        dve.wait_ge(z["p_lg"], b - 1)
                        lg = LG[:, :, :]
                        c2.after(ve.reduce_max(gs[:, 3, :], lg, AX))
                        ve.tensor_tensor(D[:, :, :], lg, bc(gs[:, 3, :].unsqueeze(2), [CP, CH, E]), ALU.subtract
                                         ).then_inc(z["p_d"], 1)
                        dve.wait_ge(z["p_d"], b - 1)
                        c2.after(ve.scalar_tensor_tensor(CAND[:, :, :], D[:, :, :], 0.0, DESC[:, :, :], op0=ALU.is_ge,
                                                         op1=ALU.mult))
                        c2.after(ve.reduce_max(gs[:, 4, :], CAND[:, :, :], AX))
                        c2.after(ve.tensor_tensor(OH[:, :, :].rearrange("p e j -> p j e"), DESC[:, :, :],
                                                  bc(gs[:, 4, :].unsqueeze(2), [CP, CH, E]), ALU.is_equal))
                        c2.after(ve.tensor_tensor_scan(SC[:, :, :].rearrange("p e j -> p (e j)"), KEEP[:, :],
                                                       OH[:, :, :].rearrange("p e j -> p (e j)"), 0.0, ALU.mult,
                                                       ALU.add))
                        ve.tensor_copy(RT[:, :], SC[:, :, CH - 1]).then_inc(z["p_rt"], 1)
                    if post2 and g == 3:
                        dve.wait_ge(z["p_ex"], b - 1)
                        ve.reduce_sum(gs[:, 5, :], EX[:, :, :], AX).then_inc(z["p_es"], 1)
                        dve.wait_ge(z["p_tri"], b - 1)
                        ve.tensor_tensor(CR[:, :], CR[:, :], RT[:, :], ALU.add)
                        c2.after(ve.tensor_tensor(PX[:, :, :], SC[:, :, :],
                                                  bc(PS[0:CP, TB, 0:E].unsqueeze(2), [CP, E, CH]), ALU.add))
                        c2.after(ve.tensor_tensor(PX[:, :, :], PX[:, :, :], OH[:, :, :], ALU.mult))
                        dve.wait_ge(z["p_es"], b - 1)
                        ve.reciprocal(row2[:, :, C + 2], gs[:, 5, :])
                        c2.after(ve.reduce_sum(gs[:, 0, :], PX[:, :, :].rearrange("p e j -> p j e"), AX))
                        ve.tensor_scalar(gs[:, 1, :], gs[:, 0, :], float(CAP), float(FAR), ALU.is_gt, ALU.mult)
                        ve.tensor_scalar(gs[:, 2, :], gs[:, 4, :], -float(STRIDE), float(E * STRIDE - 1), ALU.mult,
                                         ALU.add).then_inc(z["p_t2"], 1)
                        dve.wait_ge(z["p_t2"], b - 1)
                        c2.after(ve.tensor_tensor(gs[:, 2, :], gs[:, 2, :], gs[:, 0, :], ALU.add))
                        ve.tensor_tensor(SLOT[par][:, :], gs[:, 2, :], gs[:, 1, :], ALU.add).then_inc(z["p_slot"], 1)
                        assert c2.n == POST2, c2.n
                    if pre and g >= 7:
                        n = g - 7
                        dve.wait_ge(z["f_km"], 7 * b + 8 + n)
                        ve.reduce_max(KM[:, n:n + 1], PS[:, TB, 0:KW], AX).then_inc(z["f_kmx"], 1)
                if pre:
                    dve.wait_ge(z["f_kmx"], 7 * b + 14)
                    cp.after(ve.reduce_max(NK[1 - par][:, :], KM[:, :], AX))
                    cp.after(ve.tensor_scalar(NK[1 - par][:, :], NK[1 - par][:, :], -1.0, None, ALU.mult))
                    cp.after(ve.tensor_scalar(NKP[:, 0:1].bitcast(I32), NK[1 - par][:, :].bitcast(I32), UPPER, None,
                                              ALU.bitwise_and))
                    ve.tensor_tensor(NKP[:, 1:2], NK[1 - par][:, :], NKP[:, 0:1], ALU.subtract).then_inc(z["f_nk"], 1)
                    assert cp.n == PRE, cp.n
                if post1:
                    assert c1.n == POST1, c1.n
                if grp:
                    queries(b, par, NG)
                if pre:
                    dve.wait_ge(z["f_nkr"], b + 2)
                    ve.tensor_copy(parts(NKR[1 - par][0:2, 0:P]), PS[0:2, TA, 0:P]).then_inc(z["f_wrow"], 1)

            all_batches(dve, batch, halves=True)

            XS4 = [SP_, 4, C]
            EXP = 7

            def slot(t, q, ep, h, new=False, live=True):
                if live and new and q == 0:
                    e = 2 * h + ep
                    dve.wait_ge(e_w[ep], 64 * h + 64)
                    ve.tensor_scalar(WU[:, 0:FF].bitcast(I32), W1E[ep][:, :].bitcast(I32), UPPER, None,
                                     ALU.bitwise_and).then_inc(z["e_wu"], 1)
                    dve.wait_ge(z["e_wu"], e + 1)
                    ve.tensor_tensor(parts(W1L[ep][:, :]), W1E[ep][:, :], WU[:, 0:FF], ALU.subtract)
                    ve.tensor_copy(parts(W1H[ep][:, :]), WU[:, 0:FF]).then_inc(z["e_wp"], 1)
                if live:
                    x = RX[q % 2]
                    dve.wait_ge(z["e_x"], t + 1)
                    ve.tensor_scalar(x[:, :, 0, :].bitcast(I32), x[:, :, 1, :].bitcast(I32), UPPER, None,
                                     ALU.bitwise_and).then_inc(z["e_xu"], 1)
                    dve.wait_ge(z["e_xu"], t + 1)
                    ve.tensor_tensor(x[:, :, 1, :], x[:, :, 1, :], x[:, :, 0, :], ALU.subtract
                                     ).then_inc(z["e_xp"], 1)
                if not exists(t, 2):
                    return
                w = 1 - ep if new and q < 2 else ep
                r = (q + 2) % 4
                ch = Chain(dve, z["ed"], (t - 2) * EXP)
                if new and q == 2:
                    dve.wait_ge(e_w[ep], 64 * h + 64)
                dve.wait_ge(e_in[r], rounds_of(t - 2, r))
                ve.tensor_scalar(t0[:, :], R[r][:, :, C + 3], 0.0, float(FAR), ALU.is_equal, ALU.mult)
                ch.after(ve.tensor_scalar(t1[:, :], R[r][:, :, C + 3], -1.0, None, ALU.add))
                dve.wait_ge(e_sc[r], 16 * (t - 2 - r) + 16)
                ve.tensor_tensor(IDX[r][:, :], t0[:, :], t1[:, :], ALU.add)
                dve.wait_ge(z["e_y"], t - 1)
                ve.tensor_tensor(YE[:, :, :], PS[0:SP_, 6 + q % 2, 0:4 * C].rearrange("p (j c) -> p j c", c=C),
                                 bc(B2E[w][:, :].unsqueeze(1), XS4), ALU.add).then_inc(z["e_yb"], 1)
                dve.wait_ge(z["e_yb"], t - 1)
                ch.after(ve.tensor_tensor(YE[:, :, :], YE[:, :, :], bc(R[r][:, :, C + 2:C + 3], XS4), ALU.mult))
                ch.after(ve.tensor_scalar(GE_[:, :, :], YE[:, :, :], -FMAX, None, ALU.is_ge))
                ve.tensor_tensor(EQ[:, :, :], YE[:, :, :], YE[:, :, :], ALU.is_equal)
                ch.after(ve.tensor_scalar(CE[:, :, :], YE[:, :, :], 1e4, -1e4, ALU.min, ALU.max))
                ch.after(ve.scalar_tensor_tensor(FM[:, :, :], YE[:, :, :], FMAX, GE_[:, :, :],
                                                 op0=ALU.is_le, op1=ALU.mult))
                ch.after(ve.tensor_tensor(CE[:, :, :], CE[:, :, :], EQ[:, :, :], ALU.mult), own=True)
                ch.after(ve.copy_predicated(CE[:, :, :], FM[:, :, :].bitcast(I32), YE[:, :, :]))
                ve.tensor_tensor(OE[r][:, :, :], CE[:, :, :], R[r][:, :, 0:C], ALU.add).then_inc(z["e_o"], 1)
                assert ch.n == EXP, ch.n

            all_tiles(dve, slot)


def kernel(**inputs):
    import numpy as np
    import concourse.bacc as bacc
    from concourse.bass_utils import run_bass_kernel_spmd

    g = {k: np.asarray(v) for k, v in inputs.items()}
    f32 = np.float32

    def rep(a, n):
        return np.ascontiguousarray(np.broadcast_to(a[None], (n,) + a.shape))

    x_pad = np.zeros((NB, C, XROW), f32)
    x_pad[:, :, :PW * PW].reshape(NB, C, PW, PW)[:, :, 1:-1, 1:-1] = g["x"]
    pairs = [(0, 1), (3, 4), (6, 7), (2, 5), (8,)]

    def rows_of(w):
        w = w.reshape(C, 9, -1)
        o = np.zeros((P, NCH, w.shape[2]), f32)
        for c, taps in enumerate(pairs):
            for s, t in enumerate(taps):
                o[C * s:C * s + C, c] = w[:, t]
        return o

    w2 = g["L0_tok_W2"].reshape(C, C, 9)
    b2 = g["L0_tok_b2"].reshape(C, 9)
    tw2, tb2 = np.zeros((P, NCH, P), f32), np.zeros((P, NCH), f32)
    for c, taps in enumerate(pairs):
        for s, t in enumerate(taps):
            tw2[0:C, c, C * s:C * s + C] = tw2[C:P, c, C * s:C * s + C] = w2[:, :, t]
            tb2[C * s:C * s + C, c] = b2[:, t]
    wqkv = np.zeros((2, C, QW + 2 * HID), f32)
    wqkv[:, :, :HID] = g["L0_attn_w_qkv"][:, :HID]
    wqkv[:, :, QW:] = g["L0_attn_w_qkv"][:, HID:]
    memv = np.ones((MEM, HID + 1), f32)
    memv[:, :HID] = g["L0_attn_mem_kv"][1].reshape(HID, MEM).T
    ln1w = np.concatenate([g["L0_txt_ln1_w"], g["L0_txt_lnf_w"][None]])
    ln1b = np.concatenate([g["L0_txt_ln1_b"], g["L0_txt_lnf_b"][None]])

    def each(a, n):
        return np.ascontiguousarray(np.broadcast_to(a[:, None], (a.shape[0], n, a.shape[1])))

    inv = (f32(1.0) / np.power(f32(10000.0), np.arange(0, C, 2, dtype=f32) / f32(C))).astype(f32)
    ang = (np.arange(TABLE, dtype=f32)[:, None] * inv[None]).astype(f32)
    table = np.concatenate([np.sin(ang), np.cos(ang)], 1).astype(f32).reshape(8, P, C).transpose(1, 0, 2)
    s = np.arange(SEQ)
    dist = (np.abs(s[:, None] // 32 - s[None] // 32) + np.abs(s[:, None] % 32 - s[None] % 32)).astype(f32)
    hs = np.arange(HEADS, dtype=f32)
    right = (-np.exp2(-(0.5 + hs))).astype(f32)[:, None, None] * np.triu(dist)[None]
    left = (-np.exp2(-(1.0 + hs))).astype(f32)[:, None, None] * np.tril(dist)[None]
    bias = (right + left).astype(f32).transpose(1, 0, 2).reshape(SEQ, 2, HALFS)
    hmask = (np.arange(C)[:, None] // HD == np.arange(HEADS)[None]).astype(f32) * f32(HD ** -0.5)
    blk = np.arange(P) // AD
    bd = (blk[:, None] == blk[None]).astype(f32) * f32(AD ** -0.5)
    tri = np.triu(np.ones((CP, CP), f32), 1)
    keep = np.ones((CP, E, CH), f32)
    keep[:, :, 0] = 0
    desc = np.broadcast_to((E - np.arange(E)).astype(f32), (CP, CH, E))
    vocab = (np.arange(8)[None] * P + np.arange(P)[:, None]).astype(f32)
    tokn = (np.arange(CP * CH).reshape(CP, CH) + 1).astype(f32)

    ins = dict(
        x_pad=x_pad, x_txt=rep(g["x_txt"].reshape(-1), 16), pos_ids=rep(g["pos_S"], P),
        tw1=rows_of(g["L0_tok_W1"]), tb1=np.tile(g["L0_tok_b1"], 2)[:, None], tw2=tw2, tb2=tb2,
        tw3=rows_of(g["L0_tok_W3"]), tb3=np.tile(g["L0_tok_b3"], 2)[:, None], emb=g["L0_txt_emb_table"],
        iw=rep(g["L0_txt_input_weight"], SEQ), pw=rep(g["L0_txt_position_weight"], SEQ),
        ln1w=each(ln1w, SEQ), ln1b=each(ln1b, SEQ), ln2w=each(g["L0_txt_ln2_w"], SEQ), ln2b=each(g["L0_txt_ln2_b"], SEQ),
        fw1=g["L0_txt_w1"], fb1=g["L0_txt_b1"].reshape(LAYERS, 2, P).transpose(0, 2, 1),
        fw2=g["L0_txt_w2"].reshape(LAYERS, 2, P, C).transpose(0, 2, 1, 3), fb2=each(g["L0_txt_b2"], SEQ),
        wqkv=wqkv.reshape(P, -1), memk=g["L0_attn_mem_kv"][0].reshape(HID, MEM), memv=memv, wout=g["L0_attn_w_out"],
        bout=rep(g["L0_attn_b_out"], CP), gout=rep(g["L0_attn_g_out"], CP), gpre=np.tile(g["L0_attn_g_pre"], 2)[:, None],
        gate=g["L0_ffn_gate_w"], gateb_d=rep(g["L0_ffn_gate_b"], CP), boutT=rep(g["L0_attn_b_out"], CP).T,
        goutc=g["L0_attn_g_out"][:, None], centre_d=np.tile(np.eye(C) - 1.0 / C, 2).astype(f32), ew1=np.concatenate([g["L0_ffn_w1"]] * 2, 1), eb1=g["L0_ffn_b1"].reshape(E, 2, P).transpose(0, 2, 1),
        ew2=g["L0_ffn_w2"].reshape(E, 2, P, C).transpose(0, 2, 1, 3), eb2=each(g["L0_ffn_b2"], SP_),
        ident_d=np.eye(P, dtype=f32), table_d=table, bias_d=bias, hmask_d=hmask, bd_d=bd, tri_d=tri,
        keep_d=keep.reshape(CP, E * CH), desc_d=desc, vocab_d=vocab, tokn_d=tokn)
    nc = bacc.Bacc("TRN2", target_bir_lowering=False, num_devices=1)
    arrays, args = {}, {}
    for name, a in ins.items():
        a = np.ascontiguousarray(a)
        arrays["in_" + name] = a
        args[name] = nc.dram_tensor("in_" + name, a.shape, mybir.dt.from_np(a.dtype), kind="ExternalInput").ap()
    out = nc.dram_tensor("out_0", (NB, N, C), F32, kind="ExternalOutput").ap()
    early_fusion(nc, out=out, **args)
    r = run_bass_kernel_spmd(nc, [arrays], core_ids=[0])
    return r.results[0]["out_0"]
```

```python
from contextlib import ExitStack

import concourse.bass as bass
from concourse import mybir

F32 = mybir.dt.float32
I32 = mybir.dt.int32
ALU = mybir.AluOpType
ACT = mybir.ActivationFunctionType
AX = mybir.AxisListType.X

P = 128
C = 64
NB = 16
HW = 56
PW = HW + 2
IMG = HW * HW
SEQ = 77
N = IMG + SEQ
TOK = NB * N
XROW = PW * PW + 4
ROWS = 8
TT = ROWS * HW
HALF = TT // 2
GROUPS = HW // ROWS
NCH = 5
TP = TT // 4
LAYERS = 6
HEADS, HD = 8, 8
HALFS = HEADS // 2 * SEQ
FF = 256
TABLE = 1024
LN_EPS = 1e-5
PER_LAYER = NB + 2

CH = 27
CP = N // CH
AH, AD, MEM = 4, 32, 4
HID = AH * AD
KW = 460
E = 8
CAP = -(-(5 * TOK) // (4 * E))
ST = 504
SP_ = 126
TILES_E = -(-CAP // ST)
STRIDE = TILES_E * ST
SLOTS = E * STRIDE
RW = C + 4
FAR = 1 << 20
FMAX = 3.4028234663852886e38

CX = C + E
QW = HID + E
YP = 7

assert CH * CP == N <= 7 * KW and KW <= 4 * CP


def early_fusion(nc, x_pad, x_txt, pos_ids, tw1, tb1, tw2, tb2, tw3, tb3, emb, iw, pw, ln1w, ln1b, ln2w, ln2b,
                 fw1, fb1, fw2, fb2, wqkv, memk, memv, wout, bout, gout, gpre, gate, gateb_d, ew1, eb1, ew2, eb2,
                 centre_d, boutT, goutc, ident_d, table_d, bias_d, hmask_d, bd_d, tri_d, keep_d, desc_d, vocab_d, tokn_d, out):
    h_d = nc.dram_tensor("h_scratch", (TOK, C), F32, kind="Internal").ap()
    slots_d = nc.dram_tensor("slots_scratch", (SLOTS, RW), F32, kind="Internal").ap()
    h_f = h_d.rearrange("t c -> (t c)")
    out_f = out.rearrange("b n c -> (b n c)")
    out_rows = out.rearrange("b n c -> (b n) c")
    slots_f = slots_d.rearrange("t c -> (t c)")

    with ExitStack() as ctx:
        def sb(name, shape, dt=F32):
            return ctx.enter_context(nc.sbuf_tensor(name, shape, dt))

        def sem(name):
            return ctx.enter_context(nc.semaphore(name))

        PS = ctx.enter_context(nc.psum_tensor("PS", [P, 8, 512], F32))

        ident = sb("ident", [P, P])
        spare = sb("spare", [P, 16])
        spare2 = sb("spare2", [1, 48])
        halfneg = sb("halfneg", [P, 2 * CH])
        zeros = sb("zeros", [P, 357])

        XNT = [sb(f"XNT{i}", [P, N]) for i in range(2)]
        WQ = sb("WQ", [P, QW + 2 * HID])
        WU = sb("WU", [P, QW + 2 * HID])
        WH = sb("WH", [P, QW + 2 * HID])
        WL = sb("WL", [P, QW + 2 * HID])
        gpre_s = sb("gpre_s", [P, 1])
        KM = sb("KM", [P, 8])
        ONER = sb("ONER", [P, CP])
        memk_s = sb("memk_s", [P, MEM])
        NKR = [sb(f"NKR{i}", [P, 2 * HID]) for i in range(2)]
        VM = sb("VM", [MEM, HID + 1])
        V = [sb(f"V{i}", [CP, 2, HID + 1]) for i in range(2)]
        BD = sb("BD", [P, P])
        wout_s = sb("wout_s", [P, CX])
        bout_s = sb("bout_s", [CP, CX])
        gout_s = sb("gout_s", [CP, C])
        gate_s = sb("gate_s", [C, E])
        gateb = sb("gateb", [CP, E])
        centre = sb("centre", [C, P])
        boutT_s = sb("boutT_s", [C, CP])
        goutc_s = sb("goutc_s", [C, 1])
        GO = sb("GO", [C, E])
        WOT = sb("WOT", [C, P])
        DESC = sb("DESC", [CP, CH, E])
        KEEP = sb("KEEP", [CP, E * CH])
        CR = sb("CR", [CP, E])
        TRI = sb("TRI", [CP, CP])
        ONES = sb("ONES", [P, CP])
        TKN = sb("TKN", [CP, CH])
        rs = sb("rs", [SEQ, HEADS])
        V9 = [sb(f"V9_{i}", [SEQ, HEADS, HD + 1]) for i in range(4)]

        mix_scope = ExitStack()
        outer, ctx = ctx, mix_scope
        w1c = sb("w1c", [P, NCH, C])
        w2c = sb("w2c", [P, NCH, P])
        w2u = sb("w2u", [P, NCH, P])
        w2h = sb("w2h", [P, NCH, P])
        w2l = sb("w2l", [P, NCH, P])
        w3c = sb("w3c", [P, NCH, C])
        b1c = sb("b1c", [P, 1])
        b2c = sb("b2c", [P, NCH])
        b3c = sb("b3c", [P, 1])
        bias_t = sb("bias_t", [SEQ, 2, HALFS])
        hmask = sb("hmask", [C, HEADS])
        PA = [sb(f"PA{i}", [P, 10 * PW]) for i in range(2)]
        PB = [sb(f"PB{i}", [P, 8 * PW]) for i in range(2)]
        H1 = sb("H1", [P, HALF])
        HU = sb("HU", [P, HALF])
        HS = sb("HS", [P, TT])
        MT = sb("MT", [P, HALF])
        S = sb("S", [P, NCH, TT])
        TS = sb("TS", [P, NCH, TT])
        OT = [sb(f"OT{i}", [TP, 2, 2, C]) for i in range(2)]
        XS = sb("XS", [SEQ, NB, C])
        XNt = sb("XNt", [SEQ, NB, C])
        TC_ = sb("TC_", [SEQ, NB, C])
        TSQ = sb("TSQ", [SEQ, NB, C])
        st1 = sb("st1", [SEQ, NB])
        st2 = sb("st2", [SEQ, NB])
        strs = sb("strs", [SEQ, NB])
        lnw = sb("lnw", [SEQ, 4, C])
        fb2r = sb("fb2r", [SEQ, C])
        tw1s = sb("tw1s", [C, FF])
        tw2s = sb("tw2s", [P, 2, C])
        tb1s = sb("tb1s", [P, 2])
        XB = [sb(f"XB{i}", [SEQ, C]) for i in range(4)]
        XT = sb("XT", [C, SEQ])
        KX = sb("KX", [C, HEADS, SEQ])
        SB_ = sb("SB_", [SEQ, 2, HALFS])
        mx = sb("mx", [SEQ, HEADS])
        PR = sb("PR", [SEQ, 2, HALFS])
        PT = sb("PT", [SEQ, 2, HALFS])
        AO = sb("AO", [SEQ, HEADS, HD])
        X2T = sb("X2T", [C, NB * SEQ])
        GH = sb("GH", [P, 2, NB * SEQ])
        toki = sb("toki", [16, NB * SEQ], I32)
        tokf = sb("tokf", [16, NB * SEQ])
        vocab = sb("vocab", [P, 8])
        posi = sb("posi", [P, SEQ], I32)
        posf = sb("posf", [P, SEQ])
        poh = sb("poh", [P, 8, SEQ])
        tabs = sb("tabs", [P, 8, C])
        embs = sb("embs", [16, C])
        iws = sb("iws", [SEQ, 2])
        posw = sb("posw", [SEQ, C])

        mix_scope.close()
        ctx = outer

        X = [sb(f"X{i}", [CP, CH, C]) for i in range(2)]
        XC = sb("XC", [CP, CH, C])
        SQ = sb("SQ", [CP, CH, C])
        XN = sb("XN", [CP, CH, 2, C])
        XR = [sb(f"XR{i}", [CP, CH, C]) for i in range(2)]
        Y = sb("Y", [CP, CH, CX])
        SQ2 = SQ
        XF = sb("XF", [CP, CH, C])
        ROW = [sb(f"ROW{i}", [CP, CH, RW]) for i in range(2)]
        QT = [sb(f"QT{i}", [P, N]) for i in range(2)]
        fs = sb("fs", [CP, CH])
        ms = sb("ms", [CP, CH])
        vv = sb("vv", [CP, 2 * CH])
        rr = sb("rr", [CP, 2 * CH])
        vv2 = sb("vv2", [CP, CH])
        rr2 = sb("rr2", [CP, CH])
        vv3 = sb("vv3", [CP, CH])
        rr3 = sb("rr3", [CP, CH])
        gs = sb("gs", [CP, 6, CH])
        NK = [sb(f"NK{i}", [P, 1]) for i in range(2)]
        NKP = sb("NKP", [P, 2])
        EM = sb("EM", [P, MEM])
        EMT = [sb(f"EMT{i}", [MEM, P]) for i in range(2)]
        EK = [sb(f"EK{i}", [CP, 2, HID]) for i in range(2)]
        QS = [sb(f"QS{i}", [CP, 2, HID]) for i in range(2)]
        QE = [sb(f"QE{i}", [CP, 2, HID]) for i in range(2)]
        QN = [sb(f"QN{i}", [CP, 2, HID]) for i in range(2)]
        qm = sb("qm", [CP, 2, AH])
        qsum = sb("qsum", [CP, 2, AH])
        rq = sb("rq", [CP, 2, AH])
        rden = sb("rden", [P, 1])
        CN = sb("CN", [P, P])
        CT = sb("CT", [P, P])
        MM = sb("MM", [P, CX])
        XG = [sb(f"XG{i}", [CP, CH, E]) for i in range(2)]
        FX = [sb(f"FX{i}", [CP, CH]) for i in range(2)]
        LG = sb("LG", [CP, CH, E])
        D = sb("D", [CP, CH, E])
        EX = sb("EX", [CP, CH, E])
        CAND = sb("CAND", [CP, CH, E])
        OH = sb("OH", [CP, E, CH])
        SC = sb("SC", [CP, E, CH])
        PX = sb("PX", [CP, E, CH])
        RT = sb("RT", [CP, E])
        SLOT = [sb(f"SLOT{i}", [CP, CH], I32) for i in range(2)]

        R = [sb(f"R{i}", [SP_, 4, RW]) for i in range(4)]
        RX = [sb(f"RX{i}", [SP_, 4, 2, C]) for i in range(2)]
        XE = [sb(f"XE{i}", [P, ST]) for i in range(2)]
        HE = [sb(f"HE{i}", [P, 2, ST]) for i in range(2)]
        YE, GE_, FM, CE, EQ = (QT[0][0:SP_, n * 4 * C:(n + 1) * 4 * C].rearrange("p (j c) -> p j c", c=C)
                               for n in range(5))
        OE = [sb(f"OE{i}", [SP_, 4, C]) for i in range(4)]
        t0 = sb("t0", [SP_, 4])
        t1 = sb("t1", [SP_, 4])
        IDX = [sb(f"IDX{i}", [SP_, 4], I32) for i in range(4)]
        W1E = [sb(f"W1E{i}", [P, FF]) for i in range(2)]
        W1H = [sb(f"W1H{i}", [P, FF]) for i in range(2)]
        W1L = [sb(f"W1L{i}", [P, FF]) for i in range(2)]
        W2E = [sb(f"W2E{i}", [P, 2, C]) for i in range(2)]
        B1E = [sb(f"B1E{i}", [P, 2]) for i in range(2)]
        B2E = [sb(f"B2E{i}", [C, 1]) for i in range(2)]
        YTS = sb("YTS", [C, ST])

        names = """consts zeroed dinit
            pa_in0 pa_in1 conv_done relu_done gate_mm tanh_done prod_done mix_mm mix_out h_up h_hi h_lo w2d mt_done mt_tr st0 st1 h_text
            ln_xc ln_sq ln_var ln_pow ln_out lnd v9_done t_done kx_done xt_done sc_done soft_sub exp_done
            ptr_done pt_done pv_done ao_done aod softd ffw x2_tr x2_cp f1_mm gelu_done f2_mm f2_add
            emb_oh emb_mm embd wts xb_done passed_pe passed_dve passed_pool
            x_in0 x_in1 f_xc f_sq f_var f_pow f_pw1 f_xn f_xin f_xr fd f_tr f_trc f_km f_kmx f_nk f_nkr f_wrow f_em f_emt f_emc f_fx f_fy f_xu g_mm g_cp wqd q_g p_lx
            q_mm q_ek q_v q_sub q_exp q_n q_tr q_trc q_gd q_ctx
            p_cn p_ct p_ctc p_m p_mc p_y p_yb p_sq p_ss p_pow p_yn p_h2 p_c2 p_c2s p_v3 p_pw3 
            p_lg p_d p_ex p_rt p_tri p_slot p_yg p_s3 p_es p_t2 p1 p2 o_st s_sc0 s_sc1 crd
            e_in0 e_in1 e_in2 e_in3 e_x e_xt e_xc e_h e_hm e_ym e_yc e_yb e_wu e_wp e_xu e_xp e_y e_o ed e_w0 e_w1 e_s0 e_s1 e_s2 e_s3""".split()
        z = {n: sem(n) for n in names}
        block = ctx.enter_context(nc.Block())

        pa_in = [z["pa_in0"], z["pa_in1"]]
        stored = [z["st0"], z["st1"]]
        x_in = [z["x_in0"], z["x_in1"]]
        scat = [z["s_sc0"], z["s_sc1"]]
        e_w = [z["e_w0"], z["e_w1"]]
        e_in = [z[f"e_in{i}"] for i in range(4)]
        e_sc = [z[f"e_s{i}"] for i in range(4)]

        consts = [(ident[:], ident_d), (w1c[:], tw1), (w2c[:], tw2), (w3c[:], tw3), (b1c[:], tb1), (b2c[:], tb2), (b3c[:], tb3),
                  (bias_t[:], bias_d), (hmask[:], hmask_d), (vocab[:], vocab_d), (toki[:], x_txt), (posi[:], pos_ids),
                  (tabs[:], table_d), (embs[:], emb), (iws[:, 0:1], iw), (iws[:, 1:2], pw), (gpre_s[:], gpre),
                  (WQ[:], wqkv), (memk_s[:], memk), (VM[:], memv), (wout_s[:, 0:C], wout), (bout_s[:, 0:C], bout),
                  (gateb[:], gateb_d), (centre[:], centre_d), (boutT_s[:], boutT), (goutc_s[:], goutc),
                  (gout_s[:], gout), (gate_s[:], gate), (BD[:], bd_d), (TRI[:], tri_d), (KEEP[:], keep_d), (DESC[:], desc_d),
                  (TKN[:], tokn_d), (lnw[:, 2, :], ln1w[0]), (lnw[:, 3, :], ln1b[0])]
        ALL_CONSTS = 16 * len(consts)

        UPPER = -4096

        def parts(ap):
            return ap.bitcast(mybir.dt.float32r)

        class Chain:

            def __init__(self, eng, s, base):
                self.eng, self.s, self.base, self.n = eng, s, base, 0

            def after(self, ins, own=False):
                self.n += 1
                ins.then_inc(self.s, 1)
                self.eng.wait_ge(self.s, self.base + self.n)
                if own:
                    self.eng.sem_inc(z["passed_dve"], 1)

        F2 = [(5, 256), (6, 0)]
        LN_STEPS, AO_STEPS, SOFT_STEPS = 5, 2, 2

        def tile_place(l, n):
            return (n, l) if n < NB else (4 + 2 * l + n - NB, GROUPS - 1)

        TA, TB, T2, CTX = 4, 5, 6, 7
        NG = -(-CH // 2)

        def chunks(g):
            return range(2 * g, min(2 * g + 2, CH))

        def first(G, n):
            return isinstance(G, int) and G < n

        def lagged(b, par, g, n, grp, post1):
            if g >= n:
                return [(b, par, g - n)] if grp else []
            return [(b - 1, 1 - par, NG + g - n)] if post1 else []

        def all_batches(eng, batch, halves=False):
            def kw(h):
                return dict(h=h) if halves else {}

            batch(-1, 1, grp=False, post1=False, post2=False, **kw(-1))
            batch(0, 0, post1=False, post2=False, **kw(0))
            batch(1, 1, post2=False, **kw(0))
            with eng.Fori(0, NB // 2 - 2) as k:
                for par in range(2):
                    batch(2 * k + 2 + par, par, **kw(k + 1))
            batch(NB - 2, 0, **kw(NB // 2 - 1))
            batch(NB - 1, 1, pre=False, **kw(NB // 2 - 1))
            batch(NB, 0, grp=False, pre=False, **kw(NB // 2))
            batch(NB + 1, 1, grp=False, pre=False, post1=False, **kw(NB // 2))

        def all_tiles(eng, slot):
            def expert(e, ep, h):
                for q in range(4):
                    slot(e * TILES_E + q, q, ep, h, new=True)
                with eng.Fori(1, TILES_E // 4) as k:
                    for q in range(4):
                        slot(e * TILES_E + k * 4 + q, q, ep, h)

            expert(0, 0, 0)
            expert(1, 1, 0)
            with eng.Fori(1, E // 2) as h:
                for ep in range(2):
                    expert(2 * h + ep, ep, h)
            for q in range(2):
                slot(E * TILES_E + q, q, 0, E // 2, new=True, live=False)

        def rounds_of(t, q):
            return 4 * (t - q) + 16

        def exists(t, n):
            return not isinstance(t, int) or t >= n

        @block.sync
        def _(sp):
            for dst, src in consts:
                sp.dma_start(dst, src).then_inc(z["consts"], 16)

            def load_tile(par, b, g):
                for half in range(2):
                    rows = slice(C * half, C * half + C)
                    sp.dma_start(PA[par][rows, :], x_pad[b, :, bass.ds(g * (ROWS * PW) + half, 10 * PW)]
                                 ).then_inc(pa_in[par], 16)
                    sp.dma_start(PB[par][rows, :], x_pad[b, :, bass.ds(g * (ROWS * PW) + 2 + half * PW, 8 * PW)]
                                 ).then_inc(pa_in[par], 16)

            def store_tile(i, par, b, g):
                sp.wait_ge(z["mix_out"], i + 1)
                sp.dma_start(h_f[bass.ds(b * (N * C) + g * (TT * C), TT * C)].rearrange("(a p f) -> p a f", a=2, p=TP),
                             OT[par][:, :, :, :].rearrange("p a r c -> p a (r c)")).then_inc(stored[par], 16)

            load_tile(0, 0, 0)
            load_tile(1, 1, 0)
            sp.wait_ge(z["zeroed"], 1)
            for k in range(SLOTS * RW // (P * 1071)):
                sp.dma_start(slots_f[k * P * 1071:(k + 1) * P * 1071].rearrange("(p r f) -> p r f", p=P, r=3),
                             zeros[:, :].unsqueeze(1).to_broadcast([P, 3, 357])).then_inc(z["wts"], 16)
            with sp.Fori(0, LAYERS) as l:
                for n in range(PER_LAYER):
                    i = l * PER_LAYER + n
                    if n == 0:
                        sp.wait_ge(z["f2_add"], l * 4 + 1)
                        sp.wait_ge(z["ln_out"], 2 * l + 1)
                        sp.dma_start(tw1s[:, :], fw1[l]).then_inc(z["ffw"], 16)
                        sp.dma_start(tw2s[:, :, :], fw2[l]).then_inc(z["ffw"], 16)
                        sp.dma_start(tb1s[:, :], fb1[l]).then_inc(z["ffw"], 16)
                        sp.dma_start(fb2r[:, :], fb2[l]).then_inc(z["ffw"], 16)
                        sp.dma_start(lnw[:, 0, :], ln2w[l]).then_inc(z["ffw"], 16)
                        sp.dma_start(lnw[:, 1, :], ln2b[l]).then_inc(z["ffw"], 16)
                        sp.dma_start(lnw[:, 2, :], ln1w[l + 1]).then_inc(z["ffw"], 16)
                        sp.dma_start(lnw[:, 3, :], ln1b[l + 1]).then_inc(z["ffw"], 16)
                    sp.wait_ge(z["prod_done"], NCH * i + NCH)
                    b, g = tile_place(l, n + 2) if n + 2 < PER_LAYER else tile_place(l + 1, n + 2 - PER_LAYER)
                    load_tile(n % 2, b, g)
                    b, g = tile_place(l, n)
                    store_tile(i, n % 2, b, g)
            for n in range(4):
                i = LAYERS * PER_LAYER + n
                if n < 2:
                    sp.wait_ge(z["prod_done"], NCH * i + NCH)
                    load_tile(n % 2, n + 2, GROUPS - 1)
                store_tile(i, n % 2, n, GROUPS - 1)
            sp.wait_ge(z["ln_out"], 2 * LAYERS + 1)
            sp.dma_start(h_d.rearrange("(b n) c -> n b c", b=NB)[IMG:N, :, :], XNt[:, :, :]).then_inc(z["h_text"], 16)

            for par in range(2):
                sp.wait_ge(stored[par], 16 * (56 + 1))
            sp.wait_ge(z["h_text"], 16)

            def load_x(b, par):
                sp.dma_start(X[par][:, :, :].rearrange("p j c -> p (j c)"),
                             h_f[bass.ds(b * (N * C), N * C)].rearrange("(p f) -> p f", p=CP)).then_inc(x_in[par], 16)

            def store_h(b, par):
                sp.wait_ge(z["p_h2"], b + 1)
                sp.dma_start(out_f[bass.ds(b * (N * C), N * C)].rearrange("(p j c) -> p j c", p=CP, j=CH),
                             ROW[par][:, :, 0:C]).then_inc(z["o_st"], 16)

            load_x(0, 0)
            load_x(1, 1)

            with sp.Fori(0, NB // 2 - 1) as k:
                for par in range(2):
                    sp.wait_ge(z["f_xr"], 2 * k + par + 1)
                    load_x(2 * k + par + 2, par)
                    store_h(2 * k + par, par)
            for b in (NB - 2, NB - 1):
                store_h(b, b % 2)

            def load_w(e, par):
                sp.dma_start(W1E[par][:, :], ew1[e]).then_inc(e_w[par], 16)
                sp.dma_start(W2E[par][:, :, :], ew2[e]).then_inc(e_w[par], 16)
                sp.dma_start(B1E[par][:, :], eb1[e]).then_inc(e_w[par], 16)
                sp.dma_start(B2E[par][:, :], eb2[e]).then_inc(e_w[par], 16)

            def load_r(t, q):
                sp.dma_start(R[q][:, :, :].rearrange("p j c -> p (j c)"),
                             slots_f[bass.ds(t * (ST * RW), ST * RW)].rearrange("(p f) -> p f", p=SP_)
                             ).then_inc(e_in[q], 16)

            load_w(0, 0)
            load_w(1, 1)
            for par in range(2):
                sp.wait_ge(scat[par], 16 * CH * (NB // 2) + 16)
            for q in range(4):
                load_r(q, q)
            tiles = E * TILES_E
            with sp.Fori(0, E // 2 - 1) as e2:
                for ep in range(2):
                    e = 2 * e2 + ep
                    with sp.Fori(0, TILES_E // 4) as k:
                        for q in range(4):
                            t = e * TILES_E + k * 4 + q
                            sp.wait_ge(z["e_o"], t + 1)
                            load_r(t + 4, q)
                    load_w(e + 2, ep)
            tail = (E - 2) * TILES_E
            with sp.Fori(0, 2 * TILES_E // 4 - 1) as k:
                for q in range(4):
                    sp.wait_ge(z["e_o"], tail + k * 4 + q + 1)
                    load_r(tail + k * 4 + q + 4, q)
            sp.wait_ge(z["e_o"], E * TILES_E - 3)
            load_r(E * TILES_E - 4, 0)
            for q in range(4):
                sp.wait_ge(e_sc[q], 64 * (tiles // 4) + 16)
            sp.wait_ge(z["o_st"], 16 * NB + 16)

        @block.tensor
        def _(pe):
            def wait_first(s, value):
                pe.wait_ge(s, value)
                pe.sem_inc(z["passed_pe"], 1)

            def mm(o, w, r, start=True, stop=True):
                return nc.tensor.matmul(o, w, r, start=start, stop=stop)

            def views(par, half, c):
                pa = PA[par][:, :].rearrange("p (r w) -> p r w", w=PW)
                pb = PB[par][:, :].rearrange("p (r w) -> p r w", w=PW)
                r0 = 4 * half
                if c < 3:
                    return pa[:, c + r0:c + r0 + 4, 0:HW]
                if c == 3:
                    return pb[:, r0:r0 + 4, 0:HW]
                return pa[0:C, 2 + r0:6 + r0, 2:2 + HW]

            def conv(i, par, rounds):
                pe.wait_ge(pa_in[par], 64 * rounds)
                for c in range(NCH):
                    k = C if c == NCH - 1 else P
                    for half in range(2):
                        last = mm(PS[C * half:C * half + C, 0, 0:HALF], w1c[0:k, c, :], views(par, half, c),
                                  start=(c == 0), stop=(c == NCH - 1))
                last.then_inc(z["conv_done"], 1)

            def hidden(i):
                pe.wait_ge(z["h_hi"], i + 1)
                pe.wait_ge(z["h_lo"], i + 1)

            def gates(i, c0=0, c1=NCH):
                for c in range(c0, c1):
                    if c >= 3:
                        pe.wait_ge(z["tanh_done"], NCH * i + c - 2)
                    m = C if c == NCH - 1 else P
                    for n, w in enumerate((w2h, w2l)):
                        last = mm(PS[0:m, 1 + c % 3, 0:TT], parts(w[:, c, 0:m]), parts(HS[:, :]), start=(n == 0),
                                  stop=(n == 1))
                    last.then_inc(z["gate_mm"], 1)

            def mix(i):
                for c in range(NCH):
                    k = C if c == NCH - 1 else P
                    wait_first(z["prod_done"], NCH * i + c + 1)
                    for half in range(2):
                        last = mm(PS[C * half:C * half + C, 5, 0:HALF], w3c[0:k, c, :],
                                  TS[0:k, c, HALF * half:HALF * half + HALF], start=(c == 0), stop=(c == NCH - 1))
                last.then_inc(z["mix_mm"], 1)

            def turn_out(i):
                wait_first(z["mt_done"], i + 1)
                for r in range(2):
                    last = nc.tensor.transpose(PS[0:TP, 4, P * r:P * r + P], MT[:, r::2], ident[:, :])
                last.then_inc(z["mt_tr"], 1)

            def text_turn(j, q):
                wait_first(z["v9_done"], j + 1)
                nc.tensor.transpose(PS[0:C, 0, 256:256 + SEQ], XB[q][:, :], ident[0:SEQ, 0:SEQ]
                                    ).then_inc(z["t_done"], 1)

            def text_scores(j):
                pe.wait_ge(z["kx_done"], j + 1)
                pe.wait_ge(z["ao_done"], j + 1)
                for s in range(2):
                    last = mm(PS[0:SEQ, 6 + s, 0:HALFS], XT[:, :], KX[:, 4 * s:4 * s + 4, :])
                last.then_inc(z["sc_done"], 1)

            def text_probs_turn(j):
                pe.wait_ge(z["exp_done"], j + 1)
                for h in range(HEADS):
                    s, o = h // 4, h % 4 * SEQ
                    last = nc.tensor.transpose(PS[0:SEQ, 6 + s, o:o + SEQ], PR[:, s, o:o + SEQ], ident[0:SEQ, 0:SEQ])
                last.then_inc(z["ptr_done"], 1)

            def text_values(j, q):
                pe.wait_ge(z["pt_done"], j + 1)
                for h in range(HEADS):
                    s, o = h // 4, h % 4 * SEQ
                    last = mm(PS[0:SEQ, 6, 384 + 9 * h:393 + 9 * h], PT[:, s, o:o + SEQ], V9[q][:, h, :])
                last.then_inc(z["pv_done"], 1)

            pe.wait_ge(z["consts"], ALL_CONSTS)
            pe.wait_ge(z["emb_oh"], 1)
            for c in range(8):
                last = mm(PS[0:SEQ, 0, 0:C], poh[:, c, :], tabs[:, c, :], start=(c == 0), stop=(c == 7))
            for b in range(NB):
                last = mm(PS[0:SEQ, 1 + b // 8, C * (b % 8):C * (b % 8) + C], tokf[:, SEQ * b:SEQ * b + SEQ], embs[:, :])
            last.then_inc(z["emb_mm"], 1)
            pe.wait_ge(z["embd"], 4)

            def image_tile(i, par, rounds, last=False):
                hidden(i)
                gates(i)
                if not last:
                    conv(i + 1, par, rounds)
                mix(i)
                turn_out(i)

            pe.wait_ge(z["w2d"], 3)
            conv(0, 0, 1)
            with pe.Fori(0, LAYERS) as l:
                with pe.Fori(0, NB // 4) as k:
                    for q in range(4):
                        i = l * PER_LAYER + k * 4 + q
                        j = l * NB + k * 4 + q
                        hidden(i)
                        text_turn(j, q)
                        gates(i, 0, 3)
                        if q:
                            text_values(j - 1, q - 1)
                            turn_out(i - 1)
                        gates(i, 3, NCH)
                        text_scores(j)
                        conv(i + 1, (q + 1) % 2, l * 9 + k * 2 + (q + 1) // 2 + 1)
                        mix(i)
                        text_probs_turn(j)
                        if q == 3:
                            text_values(j, q)
                            turn_out(i)
                i = l * PER_LAYER + NB
                hidden(i)
                gates(i)
                conv(i + 1, 1, l * 9 + 9)
                mix(i)
                hidden(i + 1)
                gates(i + 1)
                turn_out(i)
                pe.wait_ge(z["ffw"], 128 * l + 128)
                wait_first(z["ln_out"], 2 * l + 2)
                for n in range(4):
                    if n >= 2:
                        wait_first(z["x2_cp"], l * 4 + n - 1)
                    for m in range(4):
                        last = nc.tensor.transpose(PS[0:C, 6 + n % 2, SEQ * m:SEQ * m + SEQ], XNt[:, 4 * n + m, :],
                                                   ident[0:SEQ, 0:SEQ])
                    last.then_inc(z["x2_tr"], 1)
                for n in range(4):
                    pe.wait_ge(z["x2_cp"], l * 4 + max(n, 0) + 1)
                    for f in range(2):
                        i8 = 2 * n + f
                        if n == 0:
                            pe.wait_ge(z["x2_cp"], l * 4 + 4)
                        else:
                            pe.wait_ge(z["gelu_done"], l * 8 + i8 - 1)
                        mm(PS[:, 6 + f, 0:HALFS], tw1s[:, P * f:P * f + P], X2T[:, HALFS * n:HALFS * n + HALFS]
                           ).then_inc(z["f1_mm"], 1)
                for n in range(4):
                    pe.wait_ge(z["gelu_done"], l * 8 + 2 * n + 2)
                    if n == 1:
                        pe.wait_ge(z["gelu_done"], l * 8 + 8)
                    if n >= 2:
                        pe.wait_ge(z["f2_add"], l * 4 + n)
                    bank, o2 = F2[n % 2]
                    for m in range(4):
                        for f in range(2):
                            o = SEQ * (4 * n + m)
                            last = mm(PS[0:SEQ, bank, o2 + C * m:o2 + C * m + C], GH[:, f, o:o + SEQ], tw2s[:, f, :],
                                      start=(f == 0), stop=(f == 1))
                    last.then_inc(z["f2_mm"], 1)
                pe.wait_ge(z["f2_add"], l * 4 + 5)
                conv(i + 2, 0, l * 9 + 10)
                mix(i + 1)
                turn_out(i + 1)
            for n in range(4):
                image_tile(LAYERS * PER_LAYER + n, (n + 1) % 2, LAYERS * 9 + (n + 1) // 2 + 1, last=(n == 3))

            pe.wait_ge(z["mix_out"], LAYERS * PER_LAYER + 4)

            mm(PS[:, TA, 0:E], centre[:, :], gate_s[:, :])
            nc.tensor.transpose(PS[0:C, TB, 0:P], wout_s[:, 0:C], ident[:, :]).then_inc(z["g_mm"], 1)
            pe.wait_ge(z["g_cp"], 1)
            mm(PS[:, TA, 0:E], WOT[:, :], GO[:, :])
            mm(PS[0:CP, TB, 0:E], boutT_s[:, :], GO[:, :]).then_inc(z["g_mm"], 1)
            pe.wait_ge(z["g_cp"], 2)

            def turn_x(g):
                for j in range(4 * g, min(4 * g + 4, CH)):
                    last = nc.tensor.transpose(PS[:, TA, CP * (j - 4 * g):CP * (j - 4 * g) + CP],
                                               XN[:, j, :, :].rearrange("p a c -> p (a c)"), ident[0:CP, 0:CP])
                last.then_inc(z["f_tr"], 1)

            def project(b, par, g):
                G = NG * b + g
                if not first(G, 2):
                    pe.wait_ge(z["q_v"], G - 1)
                    pe.wait_ge(z["q_sub"], G - 1)
                n = len(chunks(g))
                mm(PS[0:CP, 2 + g % 2, 0:2 * HID * n].rearrange("p (n c) -> p n c", n=n),
                   parts(ONER[:, :]), parts(NKR[par][:, :]).unsqueeze(1).to_broadcast([P, n, 2 * HID]), stop=False)
                for j in chunks(g):
                    x, s = parts(XNT[par][:, CP * j:CP * j + CP]), j % 2
                    for n, w in enumerate((WH, WL)):
                        mm(PS[0:CP, g % 2, QW * s:QW * s + QW], x, parts(w[:, 0:QW]), start=(n == 0), stop=(n == 1))
                        last = mm(PS[0:CP, 2 + g % 2, 2 * HID * s:2 * HID * s + 2 * HID], x,
                                  parts(w[:, QW:QW + 2 * HID]), start=False, stop=(n == 1 and j == chunks(g)[-1]))
                last.then_inc(z["q_mm"], 1)

            def context(b, g):
                G = NG * b + g
                pe.wait_ge(z["q_ek"], G + 1)
                pe.wait_ge(z["q_v"], G + 1)
                for j in chunks(g):
                    last = mm(PS[:, CTX, 0:HID + 1], EK[g % 2][:, j % 2, :], V[g % 2][:, j % 2, :],
                              start=False, stop=(j == CH - 1))
                last.then_inc(z["q_ctx"], 1)

            def turn_q(b, g):
                G = NG * b + g
                if not first(G, 1):
                    pe.wait_ge(z["q_trc"], G)
                wait_first(z["q_n"], G + 1)
                for j in chunks(g):
                    o = CP * (j % 2)
                    last = nc.tensor.transpose(PS[:, T2, o:o + CP], QN[g % 2][:, j % 2, :], ident[0:CP, 0:CP])
                last.then_inc(z["q_tr"], 1)

            def keys(b, par, n):
                if 0 < n < 6:
                    pe.wait_ge(z["f_kmx"], 7 * b + n)
                pe.wait_ge(z["f_trc"], 7 * b + n + 1)
                o = min(KW * n, N - KW)
                x = parts(XNT[par][:, o:o + KW])
                bank = TA if n == 6 else TB
                mm(PS[:, bank, 0:KW], parts(WH[:, QW:QW + HID]), x, stop=False)
                mm(PS[:, bank, 0:KW], parts(WL[:, QW:QW + HID]), x, start=False).then_inc(z["f_km"], 1)

            def batch(b, par, grp=True, pre=True, post1=True, post2=True):
                for g in range(NG):
                    if post1 and g == 0:
                        wait_first(z["p_cn"], b)
                        nc.tensor.transpose(PS[:, TA, 0:P], CN[:, :], ident[:, :]).then_inc(z["p_ct"], 1)
                    if grp and g + 1 < NG:
                        project(b, par, g + 1)
                    if pre and g == 13:
                        pe.wait_ge(z["f_nk"], b + 2)
                        mm(PS[0:2, TA, 0:P], NKP[:, :], ident[:, :]).then_inc(z["f_nkr"], 1)
                    if grp and g == 0:
                        pe.wait_ge(z["f_emc"], b + 1)
                        mm(PS[:, CTX, 0:HID + 1], EMT[par][:, :], VM[:, :], start=True, stop=False)
                    if post1 and 1 <= g < 5:
                        if g == 1:
                            pe.wait_ge(z["p_mc"], b)
                        else:
                            pe.wait_ge(z["p_yb"], 4 * b + g - 5)
                        for j in range(YP * g - YP, min(YP * g, CH)):
                            last = mm(PS[0:CP, TA, CX * (j % YP):CX * (j % YP) + CX],
                                      QT[1 - par][:, CP * j:CP * j + CP], MM[:, :])
                        last.then_inc(z["p_y"], 1)
                    if pre and g == 6:
                        if post1:
                            pe.wait_ge(z["p_yb"], 4 * b)
                        wait_first(z["f_xn"], b + 2)
                        turn_x(0)
                    if pre and 7 <= g < 12:
                        wait_first(z["f_trc"], 7 * b + g + 2)
                        turn_x(g - 5)
                    if pre and g == 12:
                        keys(b + 1, 1 - par, 5)
                        keys(b + 1, 1 - par, 6)
                    if grp:
                        context(b, g)
                    for bq, pq, gq in lagged(b, par, g, 2, grp, post1):
                        turn_q(bq, gq)
                    if pre and g == 6:
                        wait_first(z["f_trc"], 7 * b + 8)
                        turn_x(1)
                    if post1 and g == 0:
                        pe.wait_ge(z["p_ctc"], b)
                        mm(PS[:, TA, 0:CX], CT[:, :], wout_s[:, :]).then_inc(z["p_m"], 1)
                    if post2 and g == 2:
                        pe.wait_ge(z["p_rt"], b - 1)
                        mm(PS[0:CP, TB, 0:E], TRI[:, :], RT[:, :], start=True, stop=False)
                        mm(PS[0:CP, TB, 0:E], ONES[0:CP, :], CR[:, :], start=False, stop=True).then_inc(z["p_tri"], 1)
                    if pre and 7 <= g < 12:
                        if g == 7 and post2:
                            pe.wait_ge(z["p_slot"], b - 1)
                        keys(b + 1, 1 - par, g - 7)
                    if pre and g == 13:
                        pe.wait_ge(z["f_wrow"], b + 2)
                        project(b + 1, 1 - par, 0)
                        wait_first(z["f_em"], b + 2)
                        nc.tensor.transpose(PS[0:MEM, TB, 0:P], EM[:, :], ident[:, :]).then_inc(z["f_emt"], 1)

            all_batches(pe, batch)

            def slot(t, q, ep, h, new=False, live=True):
                if exists(t, 1) and (live or q < 1):
                    w = 1 - ep if new and q < 1 else ep
                    if new and q == 1:
                        pe.wait_ge(e_w[ep], 64 * h + 64)
                        pe.wait_ge(z["e_wp"], 2 * h + ep + 1)
                    pe.wait_ge(z["e_xc"], t)
                    for f in range(2):
                        for n, w1 in enumerate((W1H, W1L)):
                            last = mm(PS[:, 2 + 2 * (1 - q % 2) + f, 0:ST], parts(w1[w][:, P * f:P * f + P]),
                                      parts(XE[1 - q % 2][:, :]), start=(n == 0), stop=(n == 1))
                    last.then_inc(z["e_hm"], 1)
                if exists(t, 2):
                    if exists(t, 3):
                        pe.wait_ge(z["e_yb"], t - 2)
                    wait_first(z["e_yc"], t - 1)
                    for k4 in range(4):
                        last = nc.tensor.transpose(PS[0:SP_, 7, C * k4:C * k4 + C],
                                                   YTS[:, SP_ * k4:SP_ * k4 + SP_], ident[0:C, 0:C])
                    last.then_inc(z["e_y"], 1)
                if live:
                    wait_first(z["e_xp"], t + 1)
                    for k4 in range(4):
                        last = nc.tensor.transpose(PS[:, q % 2, SP_ * k4:SP_ * k4 + SP_],
                                                   RX[q % 2][:, k4, :, :].rearrange("p a c -> p (a c)"),
                                                   ident[0:SP_, 0:SP_])
                    last.then_inc(z["e_xt"], 1)
                if exists(t, 1) and (live or q < 1):
                    for f in range(2):
                        pe.wait_ge(z["e_h"], 2 * t - 1 + f)
                        last = mm(PS[0:C, 6, 0:ST], W2E[w][:, f, :], HE[1 - q % 2][:, f, :], start=(f == 0),
                                  stop=(f == 1))
                    last.then_inc(z["e_ym"], 1)

            all_tiles(pe, slot)

        @block.scalar
        def _(act):
            def fn(o, i, f, **kw):
                return nc.scalar.activation(o, i, f, **kw)

            def relu(i):
                act.wait_ge(z["conv_done"], i + 1)
                fn(H1[:, :], PS[:, 0, 0:HALF], ACT.Relu, bias=b1c[:, 0:1]).then_inc(z["relu_done"], 1)

            def tanhs(i):
                for c in range(NCH):
                    act.wait_ge(z["gate_mm"], NCH * i + c + 1)
                    m = C if c == NCH - 1 else P
                    fn(S[0:m, c, :], PS[0:m, 1 + c % 3, 0:TT], ACT.Tanh, bias=b2c[0:m, c:c + 1], scale=0.5
                       ).then_inc(z["tanh_done"], 1)

            def upper(i):
                act.wait_ge(z["h_up"], i + 1)
                for half in range(2):
                    last = fn(parts(HS[0:C, HALF * half:HALF * half + HALF]), HU[C * half:C * half + C, :], ACT.Copy)
                last.then_inc(z["h_hi"], 1)

            def add_bias(i):
                act.wait_ge(z["mix_mm"], i + 1)
                fn(MT[:, :], PS[:, 5, 0:HALF], ACT.Identity, bias=b3c[:, 0:1]).then_inc(z["mt_done"], 1)

            def square_ln(n):
                act.wait_ge(z["ln_xc"], n + 1)
                fn(TSQ[:, :, :], TC_[:, :, :], ACT.Square).then_inc(z["ln_sq"], 1)

            def next_hidden(i):
                relu(i + 1)
                upper(i + 1)

            act.wait_ge(z["consts"], ALL_CONSTS)
            act.wait_ge(z["dinit"], 1)
            relu(0)
            upper(0)
            square_ln(0)
            with act.Fori(0, LAYERS) as l:
                with act.Fori(0, NB // 4) as k:
                    for q in range(4):
                        i = l * PER_LAYER + k * 4 + q
                        j = l * NB + k * 4 + q
                        act.wait_ge(z["t_done"], j + 1)
                        fn(XT[:, :], PS[0:C, 0, 256:256 + SEQ], ACT.Copy).then_inc(z["xt_done"], 1)
                        tanhs(i)
                        relu(i + 1)
                        act.wait_ge(z["soft_sub"], j + 1)
                        fn(PR[:, :, :], SB_[:, :, :], ACT.Exp).then_inc(z["exp_done"], 1)
                        upper(i + 1)
                        act.wait_ge(z["ptr_done"], j + 1)
                        fn(PT[:, :, :], PS[0:SEQ, 6:8, 0:HALFS], ACT.Copy).then_inc(z["pt_done"], 1)
                        add_bias(i)
                i = l * PER_LAYER + NB
                tanhs(i)
                square_ln(2 * l + 1)
                next_hidden(i)
                add_bias(i)
                tanhs(i + 1)
                for n in range(4):
                    act.wait_ge(z["x2_tr"], l * 4 + n + 1)
                    fn(X2T[:, HALFS * n:HALFS * n + HALFS], PS[0:C, 6 + n % 2, 0:HALFS], ACT.Copy
                       ).then_inc(z["x2_cp"], 1)
                for n in range(4):
                    for f in range(2):
                        act.wait_ge(z["f1_mm"], l * 8 + 2 * n + f + 1)
                        fn(GH[:, f, HALFS * n:HALFS * n + HALFS], PS[:, 6 + f, 0:HALFS], ACT.Gelu,
                           bias=tb1s[:, f:f + 1]).then_inc(z["gelu_done"], 1)
                square_ln(2 * l + 2)
                next_hidden(i + 1)
                add_bias(i + 1)
            for n in range(4):
                tanhs(LAYERS * PER_LAYER + n)
                if n < 3:
                    next_hidden(LAYERS * PER_LAYER + n)
                add_bias(LAYERS * PER_LAYER + n)

            def copy_x(b, par, g):
                act.wait_ge(z["f_tr"], 7 * b + g + 1)
                w = CP * min(4, CH - 4 * g)
                fn(parts(XNT[par][:, 4 * CP * g:4 * CP * g + w]), PS[:, TA, 0:w], ACT.Copy).then_inc(z["f_trc"], 1)

            def copy_q(b, par, g):
                act.wait_ge(z["q_tr"], NG * b + g + 1)
                w = CP * len(chunks(g))
                fn(QT[par][:, 2 * CP * g:2 * CP * g + w], PS[:, T2, 0:w], ACT.Copy).then_inc(z["q_trc"], 1)

            def batch(b, par, grp=True, pre=True, post1=True, post2=True):
                for g in range(NG):
                    if grp:
                        G = NG * b + g
                        n = len(chunks(g))
                        kv = PS[0:CP, 2 + g % 2, 0:2 * HID * n].rearrange("p (n c) -> p n c", n=n)
                        act.wait_ge(z["q_mm"], G + 1)
                        if not first(G, 2):
                            act.wait_ge(z["q_ctx"], G - 1)
                        fn(EK[g % 2][:, 0:n, :], kv[:, :, 0:HID], ACT.Exp).then_inc(z["q_ek"], 1)
                        fn(V[g % 2][:, 0:n, 0:HID], kv[:, :, HID:2 * HID], ACT.Copy).then_inc(z["q_v"], 1)
                        act.wait_ge(z["q_sub"], G + 1)
                        fn(QE[g % 2][:, 0:n, :], QS[g % 2][:, 0:n, :], ACT.Exp).then_inc(z["q_exp"], 1)
                    if pre and g == 6:
                        copy_x(b + 1, 1 - par, 0)
                    if pre and 7 <= g < 12:
                        copy_x(b + 1, 1 - par, g - 5)
                    for bq, pq, gq in lagged(b, par, g, 2, grp, post1):
                        copy_q(bq, pq, gq)
                    if pre and g == 6:
                        copy_x(b + 1, 1 - par, 1)
                    if pre and g == 13:
                        act.wait_ge(z["f_nk"], b + 2)
                        fn(EM[:, :], memk_s[:, :], ACT.Exp, bias=NK[1 - par][:, :]).then_inc(z["f_em"], 1)
                        act.wait_ge(z["f_emt"], b + 2)
                        fn(EMT[1 - par][:, :], PS[0:MEM, TB, 0:P], ACT.Copy).then_inc(z["f_emc"], 1)
                    if pre and g == 1:
                        act.wait_ge(z["f_xc"], b + 2)
                        fn(SQ[:, :, :], XC[:, :, :], ACT.Square).then_inc(z["f_sq"], 1)
                    if post1 and g == 5:
                        act.wait_ge(z["p_yb"], 4 * b)
                        fn(SQ2[:, :, :], Y[:, :, 0:C], ACT.Square).then_inc(z["p_sq"], 1)
                    if post2 and g == 2:
                        act.wait_ge(z["p_d"], b - 1)
                        fn(EX[:, :, :], D[:, :, :], ACT.Exp).then_inc(z["p_ex"], 1)
                    if post1 and g == 11:
                        act.wait_ge(z["p_c2"], b)
                        fn(SQ2[:, 0:CH // 2, :], XF[:, 0:CH // 2, :], ACT.Square).then_inc(z["p_c2s"], 1)
                    if post1 and g == 12:
                        fn(SQ2[:, CH // 2:CH, :], XF[:, CH // 2:CH, :], ACT.Square).then_inc(z["p_c2s"], 1)

            all_batches(act, batch)

            def normalise(t, q):
                act.wait_ge(e_in[q], rounds_of(t, q))
                for k4 in range(4):
                    last = fn(RX[q % 2][:, k4, 1, :], R[q][:, k4, 0:C], ACT.Identity, bias=R[q][:, k4, C:C + 1],
                              scale=R[q][:, k4, C + 1:C + 2])
                last.then_inc(z["e_x"], 1)

            def slot(t, q, ep, h, new=False, live=True):
                if exists(t, 2):
                    act.wait_ge(z["e_ym"], t - 1)
                    if exists(t, 3):
                        act.wait_ge(z["e_y"], t - 2)
                    w = 1 - ep if new and q < 2 else ep
                    fn(YTS[:, :], PS[0:C, 6, 0:ST], ACT.Identity, bias=B2E[w][:, 0:1]).then_inc(z["e_yc"], 1)
                if exists(t, 1) and (live or q < 1):
                    w = 1 - ep if new and q < 1 else ep
                    if new and q == 1:
                        act.wait_ge(e_w[ep], 64 * h + 64)
                    act.wait_ge(z["e_hm"], t)
                    for f in range(2):
                        fn(HE[1 - q % 2][:, f, :], PS[:, 2 + 2 * (1 - q % 2) + f, 0:ST], ACT.Relu,
                           bias=B1E[w][:, f:f + 1]).then_inc(z["e_h"], 1)
                if live:
                    act.wait_ge(z["e_xt"], t + 1)
                    fn(parts(XE[q % 2][:, :]), PS[:, q % 2, 0:ST], ACT.Copy).then_inc(z["e_xc"], 1)
                    normalise(t + 1, (q + 1) % 4)

            normalise(0, 0)
            all_tiles(act, slot)

        @block.gpsimd
        def _(pool):
            gp = nc.gpsimd
            for n, s in enumerate(scat + e_sc):
                pool.dma_start(spare2[0:1, 8 * n:8 * n + 8], vocab_d[0:1, :]).then_inc(s, 16)
            pool.wait_ge(z["zeroed"], 1)

            def ln_power(n):
                pool.wait_ge(z["ln_var"], n + 1)
                gp.tensor_tensor(strs[:, :], st2[:, :], halfneg[0:SEQ, 0:NB], ALU.pow).then_inc(z["ln_pow"], 1)

            ln_power(0)
            with pool.Fori(0, LAYERS) as l:
                with pool.Fori(0, NB // 4) as k:
                    pool.wait_ge(z["ln_out"], 2 * l + 1)
                    for q in range(4):
                        j = l * NB + k * 4 + q
                        pool.wait_ge(z["pv_done"], j + 1)
                        gp.tensor_copy(XB[q][:, :], XNt[:, bass.ds(k * 4 + q, 1), :].rearrange("p o c -> p (o c)"))
                        gp.tensor_copy(V9[q][:, :, 0:HD],
                                       XNt[:, bass.ds(k * 4 + q, 1), :].rearrange("p o (h d) -> p (o h) d", h=HEADS)
                                       ).then_inc(z["v9_done"], 1)
                ln_power(2 * l + 1)
                ln_power(2 * l + 2)

            def scatter(b, par, js):
                for j in js:
                    gp.indirect_dma_start(out=slots_d[:, :],
                                          out_offset=bass.IndirectOffsetOnAxis(ap=SLOT[par][:, j:j + 1], axis=0),
                                          in_=ROW[par][:, j, :], in_offset=None, bounds_check=SLOTS - 1,
                                          oob_is_err=False).then_inc(scat[par], 16)

            def batch(b, par, grp=True, pre=True, post1=True, post2=True):
                if pre:
                    pool.wait_ge(z["f_var"], b + 2)
                    for first_col, done in ((CH, z["f_pow"]), (0, z["f_pw1"])):
                        cols = slice(first_col, first_col + CH)
                        gp.tensor_tensor(rr[:, cols], vv[:, cols], halfneg[0:CP, 0:CH], ALU.pow).then_inc(done, 1)
                if post2:
                    pool.wait_ge(z["p_slot"], b - 1)
                    pool.sem_inc(z["passed_pool"], 1)
                    scatter(b - 2, par, range(0, EARLY))
                if post1:
                    pool.wait_ge(z["p_ss"], b)
                    gp.tensor_tensor(rr2[:, :], vv2[:, :], halfneg[0:CP, 0:CH], ALU.pow).then_inc(z["p_pow"], 1)
                if post2:
                    scatter(b - 2, par, range(EARLY, MOST))
                if pre:
                    pool.wait_ge(z["f_pw1"], b + 2)
                    if post1:
                        pool.wait_ge(z["p_h2"], b)
                    gp.tensor_tensor(XR[1 - par][:, :, :], XC[:, :, :],
                                     rr[:, 0:CH].unsqueeze(2).to_broadcast([CP, CH, C]), ALU.mult
                                     ).then_inc(z["f_xin"], 1)
                    pool.wait_ge(z["f_xin"], b + 2)
                    gp.tensor_tensor(XR[1 - par][:, :, :], XR[1 - par][:, :, :], X[1 - par][:, :, :], ALU.add
                                     ).then_inc(z["f_xr"], 1)
                if post1:
                    pool.wait_ge(z["p_v3"], b)
                    gp.tensor_tensor(rr3[:, :], vv3[:, :], halfneg[0:CP, 0:CH], ALU.pow).then_inc(z["p_pw3"], 1)
                if post2:
                    scatter(b - 2, par, range(MOST, CH))

            EARLY, MOST = 5, 21
            pool.wait_ge(z["wts"], 16 * (SLOTS * RW // (P * 1071)))
            all_batches(pool, batch)

            pool.wait_ge(z["o_st"], 16 * NB + 16)
            with pool.Fori(0, E * TILES_E // 4) as k:
                for q in range(4):
                    pool.wait_ge(z["e_o"], k * 4 + q + 1)
                    pool.sem_inc(z["passed_pool"], 1)
                    for k4 in range(4):
                        gp.indirect_dma_start(out=out_rows,
                                              out_offset=bass.IndirectOffsetOnAxis(ap=IDX[q][:, k4:k4 + 1], axis=0),
                                              in_=OE[q][:, k4, :], in_offset=None, bounds_check=TOK - 1,
                                              oob_is_err=False).then_inc(e_sc[q], 16)

        @block.vector
        def _(dve):
            ve = nc.vector

            def bc(ap, shape):
                return ap.to_broadcast(shape)

            LNX = [SEQ, NB, C]

            def layernorm(n, w, beside=(None, None)):
                ch = Chain(dve, z["lnd"], n * LN_STEPS)
                ch.after(ve.reduce_sum(st1[:, :], XS[:, :, :], AX))
                ch.after(ve.tensor_scalar(st1[:, :], st1[:, :], -1.0 / C, None, ALU.mult))
                ve.tensor_tensor(TC_[:, :, :], XS[:, :, :], bc(st1[:, :].unsqueeze(2), LNX), ALU.add
                                 ).then_inc(z["ln_xc"], 1)
                if beside[0]:
                    beside[0]()
                dve.wait_ge(z["ln_sq"], n + 1)
                ch.after(ve.reduce_sum(st2[:, :], TSQ[:, :, :], AX))
                ve.tensor_scalar(st2[:, :], st2[:, :], 1.0 / C, LN_EPS, ALU.mult, ALU.add).then_inc(z["ln_var"], 1)
                if beside[1]:
                    beside[1]()
                dve.wait_ge(z["ln_pow"], n + 1)
                ch.after(ve.tensor_tensor(TC_[:, :, :], TC_[:, :, :], bc(strs[:, :].unsqueeze(2), LNX), ALU.mult))
                ch.after(ve.tensor_tensor(TC_[:, :, :], TC_[:, :, :], bc(lnw[:, w:w + 1, :], LNX), ALU.mult))
                assert ch.n == LN_STEPS
                ve.tensor_tensor(XNt[:, :, :], TC_[:, :, :], bc(lnw[:, w + 1:w + 2, :], LNX), ALU.add
                                 ).then_inc(z["ln_out"], 1)

            def views(par, c):
                pa = PA[par][:, :].rearrange("p (r w) -> p r w", w=PW)
                pb = PB[par][:, :].rearrange("p (r w) -> p r w", w=PW)
                if c < 3:
                    return pa[:, c:c + ROWS, 0:HW]
                if c == 3:
                    return pb[:, 0:ROWS, 0:HW]
                return pa[0:C, 2:2 + ROWS, 2:2 + HW]

            def products(i, par, rounds, c0=0, c1=NCH):
                dve.wait_ge(pa_in[par], 64 * rounds)
                for c in range(c0, c1):
                    m = C if c == NCH - 1 else P
                    dve.wait_ge(z["tanh_done"], NCH * i + c + 1)
                    ve.scalar_tensor_tensor(TS[0:m, c, :].rearrange("p (r w) -> p r w", w=HW),
                                            S[0:m, c, :].rearrange("p (r w) -> p r w", w=HW), 1.0, views(par, c),
                                            op0=ALU.add, op1=ALU.mult).then_inc(z["prod_done"], 1)

            def mix_out(i, par, rounds):
                dve.wait_ge(z["mt_tr"], i + 1)
                dve.wait_ge(stored[par], 16 * rounds)
                ve.tensor_copy(OT[par][:, :, :, :].rearrange("p a r c -> p r a c"),
                               PS[0:TP, 4, 0:2 * P].rearrange("p (r a c) -> p r a c", r=2, a=2)
                               ).then_inc(z["mix_out"], 1)

            def hidden_parts(i):
                dve.wait_ge(z["relu_done"], i + 1)
                ve.tensor_scalar(HU[:, :].bitcast(I32), H1[:, :].bitcast(I32), UPPER, None, ALU.bitwise_and
                                 ).then_inc(z["h_up"], 1)
                dve.wait_ge(z["h_up"], i + 1)
                for half in range(2):
                    rows = slice(C * half, C * half + C)
                    last = ve.tensor_tensor(parts(HS[C:P, HALF * half:HALF * half + HALF]), H1[rows, :], HU[rows, :],
                                            ALU.subtract)
                last.then_inc(z["h_lo"], 1)

            def attend_out(j, b):
                ch = Chain(dve, z["aod"], j * AO_STEPS)
                dve.wait_ge(z["pv_done"], 4 + j + 1)
                o9 = PS[0:SEQ, 6, 384:384 + 9 * HEADS].rearrange("p (h d) -> p h d", h=HEADS)
                ch.after(ve.reciprocal(rs[:, :], o9[:, :, HD]))
                ch.after(ve.tensor_tensor(AO[:, :, :], o9[:, :, 0:HD], bc(rs[:, :].unsqueeze(2), [SEQ, HEADS, HD]),
                                          ALU.mult))
                xs = XS[:, bass.ds(b, 1), :].rearrange("p o c -> p (o c)")
                ve.tensor_tensor(xs, xs, AO[:, :, :].rearrange("p h d -> p (h d)"), ALU.add).then_inc(z["ao_done"], 1)

            def softmax(j):
                ch = Chain(dve, z["softd"], j * SOFT_STEPS)
                dve.wait_ge(z["sc_done"], j + 1)
                ch.after(ve.tensor_tensor(SB_[:, :, :], PS[0:SEQ, 6:8, 0:HALFS], bias_t[:, :, :], ALU.add))
                s3 = SB_[:, :, :].rearrange("p a (h t) -> p (a h) t", h=4)
                ch.after(ve.reduce_max(mx[:, :], s3, AX))
                ve.tensor_tensor(s3, s3, bc(mx[:, :].unsqueeze(2), [SEQ, HEADS, SEQ]), ALU.subtract
                                 ).then_inc(z["soft_sub"], 1)

            ve.memset(halfneg[:, :], -0.5)
            for q in range(4):
                ve.memset(V9[q][:, :, HD:HD + 1], 1.0)
            ve.memset(ONES[:, :], 1.0)
            ve.memset(CR[:, :], 0.0)
            for par in range(2):
                ve.memset(V[par][:, :, HID:HID + 1], 1.0)
            credits = [(stored[0], 16), (stored[1], 16), (z["f2_add"], 1), (z["pv_done"], 4),
                       (z["ao_done"], 1), (z["o_st"], 16)]
            for n, (s, v) in enumerate(credits):
                ve.memset(spare[:, n:n + 1], 0.0).then_inc(s, v)
            ve.memset(zeros[:, :], 0.0).then_inc(z["zeroed"], 1)
            dve.wait_ge(z["consts"], ALL_CONSTS)
            wd = Chain(dve, z["w2d"], 0)
            wd.after(ve.tensor_scalar(w2u[:, :, :].bitcast(I32), w2c[:, :, :].bitcast(I32), UPPER, None,
                                      ALU.bitwise_and))
            ve.tensor_tensor(parts(w2l[:, :, :]), w2c[:, :, :], w2u[:, :, :], ALU.subtract).then_inc(z["w2d"], 1)
            ve.tensor_copy(parts(w2h[:, :, :]), w2u[:, :, :]).then_inc(z["w2d"], 1)
            ini = Chain(dve, z["embd"], 0)
            ve.memset(KM[:, :], 0.0)
            ve.tensor_scalar(w3c[:, :, :], w3c[:, :, :], 0.5, None, ALU.mult)
            ve.tensor_scalar(gout_s[:, :], gout_s[:, :], float(C) ** 0.5, None, ALU.mult)
            ini.after(ve.tensor_scalar(gpre_s[:, :], gpre_s[:, :], float(C) ** 0.5, None, ALU.mult))
            ve.tensor_scalar(WQ[:, :], WQ[:, :], gpre_s[:, 0:1], None, ALU.mult)
            dve.wait_ge(z["zeroed"], 1)
            ve.tensor_copy(parts(ONER[:, :]), ONES[:, :])
            for par in range(2):
                ve.tensor_copy(parts(NKR[par][:, :]), zeros[:, 0:2 * HID])
            ve.tensor_scalar(b2c[:, :], b2c[:, :], 0.5, None, ALU.mult).then_inc(z["dinit"], 1)
            ve.tensor_copy(tokf[:, :], toki[:, :])
            ini.after(ve.tensor_copy(posf[:, :], posi[:, :]))
            for c in range(8):
                ve.tensor_scalar(poh[:, c, :], posf[:, :], vocab[:, c:c + 1], None, ALU.is_equal)
            ve.tensor_scalar(tokf[:, :], tokf[:, :], vocab[0:16, 0:1], None, ALU.is_equal).then_inc(z["emb_oh"], 1)
            dve.wait_ge(z["emb_mm"], 1)
            ini.after(ve.tensor_scalar(posw[:, :], PS[0:SEQ, 0, 0:C], iws[:, 1:2], None, ALU.mult))
            for s in range(2):
                o = ve.scalar_tensor_tensor(XS[:, 8 * s:8 * s + 8, :],
                                            PS[0:SEQ, 1 + s, :].rearrange("p (b c) -> p b c", c=C), iws[:, 0:1],
                                            bc(posw[:, :].unsqueeze(1), [SEQ, 8, C]), op0=ALU.mult, op1=ALU.add)
            ini.after(o)
            hidden_parts(0)
            layernorm(0, 2)
            with dve.Fori(0, LAYERS) as l:
                with dve.Fori(0, NB // 4) as k:
                    for q in range(4):
                        i = l * PER_LAYER + k * 4 + q
                        j = l * NB + k * 4 + q
                        rounds = l * 9 + k * 2 + q // 2 + 1
                        dve.wait_ge(z["xt_done"], j + 1)
                        ve.tensor_tensor(KX[:, :, :], bc(XT[:, :].unsqueeze(1), [C, HEADS, SEQ]),
                                         bc(hmask[:, :].unsqueeze(2), [C, HEADS, SEQ]), ALU.mult
                                         ).then_inc(z["kx_done"], 1)
                        products(i, q % 2, rounds, 0, 2)
                        if q:
                            attend_out(j - 1, k * 4 + q - 1)
                            mix_out(i - 1, (q - 1) % 2, l * 9 + k * 2 + (q - 1) // 2 + 1)
                        products(i, q % 2, rounds, 2, NCH)
                        softmax(j)
                        hidden_parts(i + 1)
                        if q == 3:
                            attend_out(j, k * 4 + q)
                            mix_out(i, q % 2, rounds)
                dve.wait_ge(z["ao_done"], l * NB + NB + 1)
                dve.wait_ge(z["ffw"], 128 * l + 128)
                i = l * PER_LAYER + NB

                def end_of_tile():
                    products(i, 0, l * 9 + 9, 2, NCH)
                    hidden_parts(i + 1)

                layernorm(2 * l + 1, 0, (lambda: products(i, 0, l * 9 + 9, 0, 2), end_of_tile))
                mix_out(i, 0, l * 9 + 9)
                products(i + 1, 1, l * 9 + 9)
                ve.tensor_tensor(XS[:, :, :], XS[:, :, :], bc(fb2r[:, :].unsqueeze(1), LNX), ALU.add
                                 ).then_inc(z["xb_done"], 1)
                dve.wait_ge(z["xb_done"], l + 1)
                for n in range(4):
                    dve.wait_ge(z["f2_mm"], l * 4 + n + 1)
                    xs = XS[:, 4 * n:4 * n + 4, :]
                    bank, o2 = F2[n % 2]
                    ve.tensor_tensor(xs, xs, PS[0:SEQ, bank, o2:o2 + 256].rearrange("p (m c) -> p m c", m=4), ALU.add
                                     ).then_inc(z["f2_add"], 1)
                dve.wait_ge(z["f2_add"], l * 4 + 4 + 1)
                layernorm(2 * l + 2, 2, (None, lambda: hidden_parts(i + 2)))
                mix_out(i + 1, 1, l * 9 + 9)
            for n in range(4):
                i = LAYERS * PER_LAYER + n
                products(i, n % 2, LAYERS * 9 + n // 2 + 1)
                if n < 3:
                    hidden_parts(i + 1)
                mix_out(i, n % 2, LAYERS * 9 + n // 2 + 1)

            BX = [CP, CH, C]
            BE = [CP, CH, E]
            PRE, POST1, POST2 = 8, 4, 10
            dve.wait_ge(z["g_mm"], 1)
            ve.tensor_copy(WOT[:, :], PS[0:C, TB, 0:P])
            wq = Chain(dve, z["wqd"], 0)
            wq.after(ve.tensor_copy(WQ[:, HID:QW], PS[:, TA, 0:E]))
            wq.after(ve.tensor_scalar(WU[:, :].bitcast(I32), WQ[:, :].bitcast(I32), UPPER, None, ALU.bitwise_and))
            ve.tensor_tensor(parts(WL[:, :]), WQ[:, :], WU[:, :], ALU.subtract)
            ve.tensor_copy(parts(WH[:, :]), WU[:, :])
            ve.tensor_scalar(GO[:, :], PS[0:C, TA, 0:E], goutc_s[:, 0:1], float(C) ** 0.5, ALU.mult, ALU.mult
                             ).then_inc(z["g_cp"], 1)
            dve.wait_ge(z["g_mm"], 2)
            ve.tensor_copy(wout_s[:, C:CX], PS[:, TA, 0:E])
            ve.tensor_copy(bout_s[:, C:CX], PS[0:CP, TB, 0:E]).then_inc(z["g_cp"], 1)

            mk = Chain(dve, z["crd"], 0)
            mk.after(ve.reduce_max(KM[:, 7:8], memk_s[:, :], AX))

            def heads(t, n):
                return t[:, 0:n, :].rearrange("p n (h d) -> p n h d", h=AH)

            def queries(b, par, g, grp, post1):
                G = NG * b + g
                count = 3 * G - (1 if grp else 2)
                before = lagged(b, par, g, 1, grp, post1)
                if grp:
                    n = len(chunks(g))
                    qg = PS[0:CP, g % 2, 0:QW * n].rearrange("p (n c) -> p n c", n=n)
                    q4 = qg[:, :, 0:HID].rearrange("p n (h d) -> p n h d", h=AH)
                    dve.wait_ge(z["q_mm"], G + 1)
                    if g == 0:
                        dve.wait_ge(z["f_fy"], b + 1)
                    ve.tensor_tensor(XG[par][:, 2 * g:2 * g + n, :], qg[:, :, HID:QW],
                                     bc(FX[par][:, 2 * g:2 * g + n].unsqueeze(2), [CP, n, E]), ALU.mult
                                     ).then_inc(z["q_g"], 1)
                    ve.reduce_max(qm[:, 0:n, :], q4, AX).then_inc(z["q_gd"], 1)
                for _, _, go in before:
                    m, o = len(chunks(go)), go % 2
                    dve.wait_ge(z["q_exp"], G)
                    ve.reduce_sum(qsum[:, 0:m, :], heads(QE[o], m), AX).then_inc(z["q_gd"], 1)
                if grp:
                    dve.wait_ge(z["q_gd"], count if before else 1)
                    ve.tensor_tensor(heads(QS[g % 2], n), q4, bc(qm[:, 0:n, :].unsqueeze(3), [CP, n, AH, AD]),
                                     ALU.subtract).then_inc(z["q_sub"], 1)
                for _, _, go in before:
                    dve.wait_ge(z["q_gd"], count + 1)
                    ve.reciprocal(rq[:, 0:m, :], qsum[:, 0:m, :]).then_inc(z["q_gd"], 1)
                    dve.wait_ge(z["q_gd"], count + 2)
                    if not first(G, 3):
                        dve.wait_ge(z["q_tr"], G - 2)
                    ve.tensor_tensor(heads(QN[o], m), heads(QE[o], m), bc(rq[:, 0:m, :].unsqueeze(3), [CP, m, AH, AD]),
                                     ALU.mult).then_inc(z["q_n"], 1)

            def batch(b, par, grp=True, pre=True, post1=True, post2=True, h=0):
                cp, c1, c2 = Chain(dve, z["fd"], (b + 1) * PRE), Chain(dve, z["p1"], (b - 1) * POST1), \
                    Chain(dve, z["p2"], (b - 2) * POST2)
                row1, row2 = ROW[1 - par], ROW[par]
                h2 = row1[:, :, 0:C]
                for g in range(NG):
                    if post1 and g == 0:
                        dve.wait_ge(z["q_ctx"], NG * b)
                        c1.after(ve.reciprocal(rden[:, :], PS[:, CTX, HID:HID + 1]))
                        ve.scalar_tensor_tensor(CN[:, :], PS[:, CTX, 0:HID], rden[:, 0:1], BD[:, :], op0=ALU.mult,
                                                op1=ALU.mult).then_inc(z["p_cn"], 1)
                    if grp or post1 and g == 0:
                        queries(b, par, g, grp, post1)
                    if post1 and g == 0:
                        dve.wait_ge(z["p_ct"], b)
                        ve.tensor_copy(CT[:, :], PS[:, TA, 0:P]).then_inc(z["p_ctc"], 1)
                    if pre and g == 0:
                        dve.wait_ge(x_in[1 - par], 16 * (h + par + 1))
                        cp.after(ve.reduce_sum(fs[:, :], X[1 - par][:, :, :], AX))
                        cp.after(ve.tensor_scalar(fs[:, :], fs[:, :], -1.0 / C, None, ALU.mult))
                    if pre and g == 1:
                        if not (isinstance(b, int) and b < 0):
                            dve.wait_ge(z["f_xin"], b + 1)
                        ve.tensor_tensor(XC[:, :, :], X[1 - par][:, :, :], bc(fs[:, :].unsqueeze(2), BX), ALU.add
                                         ).then_inc(z["f_xc"], 1)
                    if post2 and g == 2:
                        dve.wait_ge(z["p_lg"], b - 1)
                        lg = LG[:, :, :]
                        c2.after(ve.reduce_max(gs[:, 3, :], lg, AX))
                        ve.tensor_tensor(D[:, :, :], lg, bc(gs[:, 3, :].unsqueeze(2), [CP, CH, E]), ALU.subtract
                                         ).then_inc(z["p_d"], 1)
                        dve.wait_ge(z["p_d"], b - 1)
                        c2.after(ve.scalar_tensor_tensor(CAND[:, :, :], D[:, :, :], 0.0, DESC[:, :, :], op0=ALU.is_ge,
                                                         op1=ALU.mult))
                        c2.after(ve.reduce_max(gs[:, 4, :], CAND[:, :, :], AX))
                        c2.after(ve.tensor_tensor(OH[:, :, :].rearrange("p e j -> p j e"), DESC[:, :, :],
                                                  bc(gs[:, 4, :].unsqueeze(2), [CP, CH, E]), ALU.is_equal))
                        c2.after(ve.tensor_tensor_scan(SC[:, :, :].rearrange("p e j -> p (e j)"), KEEP[:, :],
                                                       OH[:, :, :].rearrange("p e j -> p (e j)"), 0.0, ALU.mult,
                                                       ALU.add))
                        ve.tensor_copy(RT[:, :], SC[:, :, CH - 1]).then_inc(z["p_rt"], 1)
                    if pre and g == 2:
                        dve.wait_ge(z["f_sq"], b + 2)
                        cp.after(ve.reduce_sum(vv[:, CH:2 * CH], SQ[:, :, :], AX))
                        cp.after(ve.tensor_scalar(vv[:, 0:CH], vv[:, CH:2 * CH], 1.0 / C, LN_EPS, ALU.mult, ALU.add))
                        ve.scalar_tensor_tensor(vv[:, CH:2 * CH], vv[:, 0:CH], 1e-24, vv[:, CH:2 * CH],
                                                op0=ALU.mult, op1=ALU.max).then_inc(z["f_var"], 1)
                    if pre and g == 4:
                        dve.wait_ge(z["f_pow"], b + 2)
                        if not (isinstance(b, int) and b < 0):
                            dve.wait_ge(z["f_tr"], 7 * b + 7)
                        ve.reciprocal(FX[1 - par][:, :], rr[:, CH:2 * CH]).then_inc(z["f_fx"], 1)
                        cp.after(ve.tensor_tensor(XN[:, :, 1, :], XC[:, :, :], bc(rr[:, CH:2 * CH].unsqueeze(2), BX),
                                                  ALU.mult))
                        ve.tensor_scalar(XN[:, :, 0, :].bitcast(I32), XN[:, :, 1, :].bitcast(I32), UPPER, None,
                                         ALU.bitwise_and).then_inc(z["f_xu"], 1)
                        dve.wait_ge(z["f_pw1"], b + 2)
                        dve.wait_ge(z["f_fx"], b + 2)
                        ve.scalar_tensor_tensor(FX[1 - par][:, :], rr[:, 0:CH], 1.0, FX[1 - par][:, :],
                                                op0=ALU.add, op1=ALU.mult).then_inc(z["f_fy"], 1)
                    if pre and g == 5:
                        dve.wait_ge(z["f_xu"], b + 2)
                        ve.tensor_tensor(XN[:, :, 1, :], XN[:, :, 1, :], XN[:, :, 0, :], ALU.subtract
                                         ).then_inc(z["f_xn"], 1)
                    if post2 and g == 1:
                        dve.wait_ge(z["p_pw3"], b - 1)
                        ve.tensor_tensor(row2[:, :, C], ms[:, :], rr3[:, :], ALU.mult)
                        ve.tensor_copy(row2[:, :, C + 1], rr3[:, :])
                        ve.tensor_copy(row2[:, :, C + 3], TKN[:, :])
                        c2.after(ve.tensor_tensor(LG[:, :, :], LG[:, :, :], bc(rr3[:, :].unsqueeze(2), BE), ALU.mult))
                        ve.tensor_scalar(TKN[:, :], TKN[:, :], float(N), None, ALU.add)
                        ve.tensor_tensor(LG[:, :, :], LG[:, :, :], bc(gateb[:, :].unsqueeze(1), BE), ALU.add
                                         ).then_inc(z["p_lg"], 1)
                    if post1 and g == 6:
                        dve.wait_ge(z["p_sq"], b)
                        c1.after(ve.reduce_sum(vv2[:, :], SQ2[:, :, :], AX))
                        ve.tensor_scalar(vv2[:, :], vv2[:, :], 1e-24, None, ALU.max).then_inc(z["p_ss"], 1)
                    if post1 and g == 7:
                        ve.tensor_tensor(Y[:, :, 0:C], Y[:, :, 0:C], bc(gout_s[:, :].unsqueeze(1), BX), ALU.mult
                                         ).then_inc(z["p_yg"], 1)
                    if post1 and g == 8:
                        dve.wait_ge(z["p_pow"], b)
                        dve.wait_ge(z["p_yg"], b)
                        ve.tensor_tensor(Y[:, :, :], Y[:, :, :], bc(rr2[:, :].unsqueeze(2), [CP, CH, CX]), ALU.mult
                                         ).then_inc(z["p_yn"], 1)
                    if post1 and g == 9:
                        dve.wait_ge(scat[1 - par], (h + par - 1) * (16 * CH) + 16)
                        dve.wait_ge(z["o_st"], b * 16)
                        dve.wait_ge(z["f_xr"], b)
                        dve.wait_ge(z["p_yn"], b)
                        ve.tensor_tensor(h2, Y[:, :, 0:C], XR[1 - par][:, :, :], ALU.add).then_inc(z["p_h2"], 1)
                        dve.wait_ge(z["q_g"], NG * b)
                        ve.tensor_tensor(LG[:, :, :], XG[1 - par][:, :, :], Y[:, :, C:CX], ALU.add
                                         ).then_inc(z["p_lx"], 1)
                    if post1 and g == 10:
                        dve.wait_ge(z["p_h2"], b)
                        c1.after(ve.reduce_sum(ms[:, :], h2, AX))
                        dve.wait_ge(z["p_lx"], b)
                        c1.after(ve.tensor_scalar(ms[:, :], ms[:, :], -1.0 / C, None, ALU.mult))
                    if post1 and g == 11:
                        ve.tensor_tensor(XF[:, :, :], h2, bc(ms[:, :].unsqueeze(2), BX), ALU.add).then_inc(z["p_c2"], 1)
                    if post2 and g == 3:
                        dve.wait_ge(z["p_ex"], b - 1)
                        ve.reduce_sum(gs[:, 5, :], EX[:, :, :], AX).then_inc(z["p_es"], 1)
                        dve.wait_ge(z["p_tri"], b - 1)
                        ve.tensor_tensor(CR[:, :], CR[:, :], RT[:, :], ALU.add)
                        c2.after(ve.tensor_tensor(PX[:, :, :], SC[:, :, :],
                                                  bc(PS[0:CP, TB, 0:E].unsqueeze(2), [CP, E, CH]), ALU.add))
                        c2.after(ve.tensor_tensor(PX[:, :, :], PX[:, :, :], OH[:, :, :], ALU.mult))
                        dve.wait_ge(z["p_es"], b - 1)
                        ve.reciprocal(row2[:, :, C + 2], gs[:, 5, :])
                        c2.after(ve.reduce_sum(gs[:, 0, :], PX[:, :, :].rearrange("p e j -> p j e"), AX))
                        ve.tensor_scalar(gs[:, 1, :], gs[:, 0, :], float(CAP), float(FAR), ALU.is_gt, ALU.mult)
                        ve.tensor_scalar(gs[:, 2, :], gs[:, 4, :], -float(STRIDE), float(E * STRIDE - 1), ALU.mult,
                                         ALU.add).then_inc(z["p_t2"], 1)
                        dve.wait_ge(z["p_t2"], b - 1)
                        c2.after(ve.tensor_tensor(gs[:, 2, :], gs[:, 2, :], gs[:, 0, :], ALU.add))
                        ve.tensor_tensor(SLOT[par][:, :], gs[:, 2, :], gs[:, 1, :], ALU.add).then_inc(z["p_slot"], 1)
                        assert c2.n == POST2, c2.n
                    if pre and 7 <= g < 13:
                        for n in ((g - 7,) if g < 12 else (5, 6)):
                            dve.wait_ge(z["f_km"], 7 * b + 8 + n)
                            ve.reduce_max(KM[:, n:n + 1], PS[:, TA if n == 6 else TB, 0:KW], AX).then_inc(z["f_kmx"], 1)
                    if pre and g == 12:
                        dve.wait_ge(z["f_kmx"], 7 * b + 14)
                        cp.after(ve.reduce_max(NK[1 - par][:, :], KM[:, :], AX))
                        cp.after(ve.tensor_scalar(NK[1 - par][:, :], NK[1 - par][:, :], -1.0, None, ALU.mult))
                        cp.after(ve.tensor_scalar(NKP[:, 0:1].bitcast(I32), NK[1 - par][:, :].bitcast(I32), UPPER, None,
                                                  ALU.bitwise_and))
                        ve.tensor_tensor(NKP[:, 1:2], NK[1 - par][:, :], NKP[:, 0:1], ALU.subtract
                                         ).then_inc(z["f_nk"], 1)
                        assert cp.n == PRE, cp.n
                    if pre and g == 13:
                        dve.wait_ge(z["f_nkr"], b + 2)
                        ve.tensor_copy(parts(NKR[1 - par][0:2, 0:P]), PS[0:2, TA, 0:P]).then_inc(z["f_wrow"], 1)
                    if post1 and g == 13:
                        dve.wait_ge(z["p_c2s"], 2 * b)
                        dve.wait_ge(z["p_c2"], b)
                        ve.reduce_sum(vv3[:, :], SQ2[:, :, :], AX).then_inc(z["p_s3"], 1)
                        dve.wait_ge(z["p_s3"], b)
                        ve.tensor_scalar(vv3[:, :], vv3[:, :], 1.0 / C, LN_EPS, ALU.mult, ALU.add
                                         ).then_inc(z["p_v3"], 1)
                    if post1 and g == 0:
                        dve.wait_ge(z["p_m"], b)
                        ve.tensor_copy(MM[:, :], PS[:, TA, 0:CX]).then_inc(z["p_mc"], 1)
                    if post1 and 1 <= g < 5:
                        n = min(YP, CH - YP * (g - 1))
                        dve.wait_ge(z["p_y"], 4 * b + g - 4)
                        ve.tensor_tensor(Y[:, YP * (g - 1):YP * (g - 1) + n, :],
                                         PS[0:CP, TA, 0:CX * n].rearrange("p (j c) -> p j c", c=CX),
                                         bc(bout_s[:, :].unsqueeze(1), [CP, n, CX]), ALU.add).then_inc(z["p_yb"], 1)
                if post1:
                    assert c1.n == POST1, c1.n

            all_batches(dve, batch, halves=True)

            XS4 = [SP_, 4, C]
            EXP = 6

            def slot(t, q, ep, h, new=False, live=True):
                if live and new and q == 0:
                    e = 2 * h + ep
                    dve.wait_ge(e_w[ep], 64 * h + 64)
                    ve.tensor_scalar(WU[:, 0:FF].bitcast(I32), W1E[ep][:, :].bitcast(I32), UPPER, None,
                                     ALU.bitwise_and).then_inc(z["e_wu"], 1)
                    dve.wait_ge(z["e_wu"], e + 1)
                    ve.tensor_tensor(parts(W1L[ep][:, :]), W1E[ep][:, :], WU[:, 0:FF], ALU.subtract)
                    ve.tensor_copy(parts(W1H[ep][:, :]), WU[:, 0:FF]).then_inc(z["e_wp"], 1)
                if live:
                    x = RX[q % 2]
                    dve.wait_ge(z["e_x"], t + 1)
                    ve.tensor_scalar(x[:, :, 0, :].bitcast(I32), x[:, :, 1, :].bitcast(I32), UPPER, None,
                                     ALU.bitwise_and).then_inc(z["e_xu"], 1)
                    dve.wait_ge(z["e_xu"], t + 1)
                    ve.tensor_tensor(x[:, :, 1, :], x[:, :, 1, :], x[:, :, 0, :], ALU.subtract
                                     ).then_inc(z["e_xp"], 1)
                if not exists(t, 2):
                    return
                r = (q + 2) % 4
                ch = Chain(dve, z["ed"], (t - 2) * EXP)
                dve.wait_ge(e_in[r], rounds_of(t - 2, r))
                ve.tensor_scalar(t0[:, :], R[r][:, :, C + 3], 0.0, float(FAR), ALU.is_equal, ALU.mult)
                ch.after(ve.tensor_scalar(t1[:, :], R[r][:, :, C + 3], -1.0, None, ALU.add))
                dve.wait_ge(e_sc[r], 16 * (t - 2 - r) + 16)
                ve.tensor_tensor(IDX[r][:, :], t0[:, :], t1[:, :], ALU.add)
                dve.wait_ge(z["e_y"], t - 1)
                ve.tensor_tensor(YE[:, :, :], PS[0:SP_, 7, 0:4 * C].rearrange("p (j c) -> p j c", c=C),
                                 bc(R[r][:, :, C + 2:C + 3], XS4), ALU.mult).then_inc(z["e_yb"], 1)
                dve.wait_ge(z["e_yb"], t - 1)
                ch.after(ve.tensor_scalar(GE_[:, :, :], YE[:, :, :], -FMAX, None, ALU.is_ge))
                ve.tensor_tensor(EQ[:, :, :], YE[:, :, :], YE[:, :, :], ALU.is_equal)
                ch.after(ve.tensor_scalar(CE[:, :, :], YE[:, :, :], 1e4, -1e4, ALU.min, ALU.max))
                ch.after(ve.scalar_tensor_tensor(FM[:, :, :], YE[:, :, :], FMAX, GE_[:, :, :],
                                                 op0=ALU.is_le, op1=ALU.mult))
                ch.after(ve.tensor_tensor(CE[:, :, :], CE[:, :, :], EQ[:, :, :], ALU.mult), own=True)
                ch.after(ve.copy_predicated(CE[:, :, :], FM[:, :, :].bitcast(I32), YE[:, :, :]))
                ve.tensor_tensor(OE[r][:, :, :], CE[:, :, :], R[r][:, :, 0:C], ALU.add).then_inc(z["e_o"], 1)
                assert ch.n == EXP, ch.n

            all_tiles(dve, slot)


def kernel(**inputs):
    import numpy as np
    import concourse.bacc as bacc
    from concourse.bass_utils import run_bass_kernel_spmd

    g = {k: np.asarray(v) for k, v in inputs.items()}
    f32 = np.float32

    def rep(a, n):
        return np.ascontiguousarray(np.broadcast_to(a[None], (n,) + a.shape))

    x_pad = np.zeros((NB, C, XROW), f32)
    x_pad[:, :, :PW * PW].reshape(NB, C, PW, PW)[:, :, 1:-1, 1:-1] = g["x"]
    pairs = [(0, 1), (3, 4), (6, 7), (2, 5), (8,)]

    def rows_of(w):
        w = w.reshape(C, 9, -1)
        o = np.zeros((P, NCH, w.shape[2]), f32)
        for c, taps in enumerate(pairs):
            for s, t in enumerate(taps):
                o[C * s:C * s + C, c] = w[:, t]
        return o

    w2 = g["L0_tok_W2"].reshape(C, C, 9)
    b2 = g["L0_tok_b2"].reshape(C, 9)
    tw2, tb2 = np.zeros((P, NCH, P), f32), np.zeros((P, NCH), f32)
    for c, taps in enumerate(pairs):
        for s, t in enumerate(taps):
            tw2[0:C, c, C * s:C * s + C] = tw2[C:P, c, C * s:C * s + C] = w2[:, :, t]
            tb2[C * s:C * s + C, c] = b2[:, t]
    wqkv = np.zeros((2, C, QW + 2 * HID), f32)
    wqkv[:, :, :HID] = g["L0_attn_w_qkv"][:, :HID]
    wqkv[:, :, QW:] = g["L0_attn_w_qkv"][:, HID:]
    memv = np.ones((MEM, HID + 1), f32)
    memv[:, :HID] = g["L0_attn_mem_kv"][1].reshape(HID, MEM).T
    ln1w = np.concatenate([g["L0_txt_ln1_w"], g["L0_txt_lnf_w"][None]])
    ln1b = np.concatenate([g["L0_txt_ln1_b"], g["L0_txt_lnf_b"][None]])

    def each(a, n):
        return np.ascontiguousarray(np.broadcast_to(a[:, None], (a.shape[0], n, a.shape[1])))

    inv = (f32(1.0) / np.power(f32(10000.0), np.arange(0, C, 2, dtype=f32) / f32(C))).astype(f32)
    ang = (np.arange(TABLE, dtype=f32)[:, None] * inv[None]).astype(f32)
    table = np.concatenate([np.sin(ang), np.cos(ang)], 1).astype(f32).reshape(8, P, C).transpose(1, 0, 2)
    s = np.arange(SEQ)
    dist = (np.abs(s[:, None] // 32 - s[None] // 32) + np.abs(s[:, None] % 32 - s[None] % 32)).astype(f32)
    hs = np.arange(HEADS, dtype=f32)
    right = (-np.exp2(-(0.5 + hs))).astype(f32)[:, None, None] * np.triu(dist)[None]
    left = (-np.exp2(-(1.0 + hs))).astype(f32)[:, None, None] * np.tril(dist)[None]
    bias = (right + left).astype(f32).transpose(1, 0, 2).reshape(SEQ, 2, HALFS)
    hmask = (np.arange(C)[:, None] // HD == np.arange(HEADS)[None]).astype(f32) * f32(HD ** -0.5)
    blk = np.arange(P) // AD
    bd = (blk[:, None] == blk[None]).astype(f32) * f32(AD ** -0.5)
    tri = np.triu(np.ones((CP, CP), f32), 1)
    keep = np.ones((CP, E, CH), f32)
    keep[:, :, 0] = 0
    desc = np.broadcast_to((E - np.arange(E)).astype(f32), (CP, CH, E))
    vocab = (np.arange(8)[None] * P + np.arange(P)[:, None]).astype(f32)
    tokn = (np.arange(CP * CH).reshape(CP, CH) + 1).astype(f32)

    ins = dict(
        x_pad=x_pad, x_txt=rep(g["x_txt"].reshape(-1), 16), pos_ids=rep(g["pos_S"], P),
        tw1=rows_of(g["L0_tok_W1"]), tb1=np.tile(g["L0_tok_b1"], 2)[:, None], tw2=tw2, tb2=tb2,
        tw3=rows_of(g["L0_tok_W3"]), tb3=np.tile(g["L0_tok_b3"], 2)[:, None], emb=g["L0_txt_emb_table"],
        iw=rep(g["L0_txt_input_weight"], SEQ), pw=rep(g["L0_txt_position_weight"], SEQ),
        ln1w=each(ln1w, SEQ), ln1b=each(ln1b, SEQ), ln2w=each(g["L0_txt_ln2_w"], SEQ), ln2b=each(g["L0_txt_ln2_b"], SEQ),
        fw1=g["L0_txt_w1"], fb1=g["L0_txt_b1"].reshape(LAYERS, 2, P).transpose(0, 2, 1),
        fw2=g["L0_txt_w2"].reshape(LAYERS, 2, P, C).transpose(0, 2, 1, 3), fb2=each(g["L0_txt_b2"], SEQ),
        wqkv=wqkv.reshape(P, -1), memk=g["L0_attn_mem_kv"][0].reshape(HID, MEM), memv=memv, wout=g["L0_attn_w_out"],
        bout=rep(g["L0_attn_b_out"], CP), gout=rep(g["L0_attn_g_out"], CP), gpre=np.tile(g["L0_attn_g_pre"], 2)[:, None],
        gate=g["L0_ffn_gate_w"], gateb_d=rep(g["L0_ffn_gate_b"], CP), boutT=rep(g["L0_attn_b_out"], CP).T,
        goutc=g["L0_attn_g_out"][:, None], centre_d=np.tile(np.eye(C) - 1.0 / C, 2).astype(f32), ew1=np.concatenate([g["L0_ffn_w1"]] * 2, 1), eb1=g["L0_ffn_b1"].reshape(E, 2, P).transpose(0, 2, 1),
        ew2=g["L0_ffn_w2"].reshape(E, 2, P, C).transpose(0, 2, 1, 3), eb2=g["L0_ffn_b2"][:, :, None],
        ident_d=np.eye(P, dtype=f32), table_d=table, bias_d=bias, hmask_d=hmask, bd_d=bd, tri_d=tri,
        keep_d=keep.reshape(CP, E * CH), desc_d=desc, vocab_d=vocab, tokn_d=tokn)
    nc = bacc.Bacc("TRN2", target_bir_lowering=False, num_devices=1)
    arrays, args = {}, {}
    for name, a in ins.items():
        a = np.ascontiguousarray(a)
        arrays["in_" + name] = a
        args[name] = nc.dram_tensor("in_" + name, a.shape, mybir.dt.from_np(a.dtype), kind="ExternalInput").ap()
    out = nc.dram_tensor("out_0", (NB, N, C), F32, kind="ExternalOutput").ap()
    early_fusion(nc, out=out, **args)
    r = run_bass_kernel_spmd(nc, [arrays], core_ids=[0])
    return r.results[0]["out_0"]
```
